# Optimizing a Trainium2 kernel written in Bass

```python
import numpy as np
import jax
import jax.numpy as jnp

def _softmax(x, axis=-1):
    return jax.nn.softmax(x, axis=axis)

def _gelu(x):
    return jax.nn.gelu(x, approximate=True)

def _silu(x):
    return jax.nn.silu(x)

def _sigmoid(x):
    return jax.nn.sigmoid(x)

def _layernorm(x, axis=-1, eps=1e-05):
    m = jnp.mean(x, axis=axis, keepdims=True)
    v = jnp.var(x, axis=axis, keepdims=True)
    return (x - m) / jnp.sqrt(v + eps)

def _scatter_add(tgt, idx, src, axis=0):
    return tgt.at[idx].add(src)

def _segment_sum(src, seg, n):
    return jax.ops.segment_sum(src, seg, n)
kernel_name = 'mk_xattn_ffn_d1_seqx_r4_da2e3f'

def setup_inputs(seed: int=0):
    np.random.seed(seed)
    _w = jnp.asarray

    def _rec_inputs():
        import jax
        import jax.numpy as jnp
        _rk = jax.random.key(seed)
        x = 7.22e-05 + 1 * jax.random.normal(jax.random.fold_in(_rk, 1), (4, 512, 256), jnp.float32)
        _lenS = 512 - jax.random.randint(jax.random.fold_in(_rk, 7), (4,), 0, max(1, 512 // 4) + 1, jnp.int32)
        _lenS2 = 512 - jax.random.randint(jax.random.fold_in(_rk, 8), (4,), 0, max(1, 512 // 4) + 1, jnp.int32)
        _ctx_1024P = jax.random.normal(jax.random.fold_in(_rk, 11), (4, 16, 256), jnp.float32)
        _ctx_1024c = jax.random.dirichlet(jax.random.fold_in(_rk, 511), 0.3 * jnp.ones((16,), jnp.float32), (4, 512))
        _ctx_1024t = jnp.einsum('bsk,bkd->bsd', _ctx_1024c, _ctx_1024P)
        _ctx_1024t = _ctx_1024t * jax.lax.rsqrt(jnp.mean(jnp.square(_ctx_1024t)) + 1e-12) * 0.953939
        ctx_1024 = 4.13588e-05 + 0.999923 * (_ctx_1024t + 0.3 * jax.random.normal(jax.random.fold_in(_rk, 611), (4, 512, 256), jnp.float32))
        return (x, ctx_1024)
    x, ctx_1024 = _rec_inputs()

    def _L0_xattn_setup():
        import jax, jax.numpy as jnp
        import numpy as np
        B, N, E, H = (2, 1024, 256, 16)
        D = E // H
        SEG_LENS = (256, 512)
        DIL_RATES = (1, 2)

        def _dilated_attention(q, k, v, seg_lens, dil_rates):
            b, n, h, d = q.shape
            G = len(seg_lens)
            g = h // G
            scale = float(d) ** (-0.5)
            outs = []
            for i, (s, r) in enumerate(zip(seg_lens, dil_rates)):
                off = i % r
                hs = slice(i * g, (i + 1) * g)

                def _seg(x):
                    return x[:, :, hs, :].reshape(b, n // s, s, g, d)[:, :, off::r]
                qi, ki, vi = (_seg(q), _seg(k), _seg(v))
                scores = jnp.einsum('bnqhd,bnkhd->bnhqk', qi, ki) * scale
                attn = jax.nn.softmax(scores, axis=-1)
                x = jnp.einsum('bnhqk,bnkhd->bnqhd', attn, vi)
                og = jnp.zeros((b, n // s, s, g, d), q.dtype).at[:, :, off::r].set(x)
                outs.append(og.reshape(b, n, g, d))
            return jnp.concatenate(outs, axis=2)
        key = jax.random.key(seed)
        ks = jax.random.split(key, 8)
        w = lambda k, i, o: jax.random.normal(k, (i, o), jnp.float32) * (2.0 / (i + o)) ** 0.5
        return {'query': jax.random.normal(ks[0], (B, N, E), jnp.float32), 'key': jax.random.normal(ks[1], (B, N, E), jnp.float32), 'value': jax.random.normal(ks[2], (B, N, E), jnp.float32), 'Wq': w(ks[3], E, E), 'bq': jnp.zeros((E,), jnp.float32), 'Wk': w(ks[4], E, E), 'bk': jnp.zeros((E,), jnp.float32), 'Wv': w(ks[5], E, E), 'bv': jnp.zeros((E,), jnp.float32), 'Wg': w(ks[6], E, E), 'bg': jnp.zeros((E,), jnp.float32), 'Wo': w(ks[7], E, E), 'bo': jnp.zeros((E,), jnp.float32)}
    _L0_xattn_all = _L0_xattn_setup()
    _L0_xattn_in = {k: v for k, v in _L0_xattn_all.items() if k in ('Wq', 'bq', 'Wk', 'bk', 'Wv', 'bv', 'Wg', 'bg', 'Wo', 'bo')}
    del _L0_xattn_all

    def _L0_ffn_setup():
        import jax, jax.numpy as jnp
        import numpy as np
        TOP_K = 2

        def _swiglu_mlp(x, wgu, wd, inter):
            gu = x @ wgu
            a = jax.nn.silu(gu[:, :inter]) * gu[:, inter:]
            return a @ wd
        key = jax.random.key(seed)
        ks = jax.random.split(key, 6)
        H, I, E = (256, 704, 8)
        B, S = (2, 256)
        w = 0.02
        return {'x': jax.random.normal(ks[0], (B, S, H), jnp.float32), 'gate_w': jax.random.normal(ks[1], (H, E), jnp.float32) * w, 'base_wgu': jax.random.normal(ks[2], (H, 2 * I), jnp.float32) * w, 'base_wd': jax.random.normal(ks[3], (I, H), jnp.float32) * w, 'exp_wgu': jax.random.normal(ks[4], (E, H, 2 * I), jnp.float32) * w, 'exp_wd': jax.random.normal(ks[5], (E, I, H), jnp.float32) * w}
    _L0_ffn_all = _L0_ffn_setup()
    _L0_ffn_in = {k: v for k, v in _L0_ffn_all.items() if k in ('gate_w', 'base_wgu', 'base_wd', 'exp_wgu', 'exp_wd')}
    del _L0_ffn_all
    return {'x': x, 'ctx_1024': ctx_1024, 'L0_xattn_Wq': _L0_xattn_in['Wq'], 'L0_xattn_bq': _L0_xattn_in['bq'], 'L0_xattn_Wk': _L0_xattn_in['Wk'], 'L0_xattn_bk': _L0_xattn_in['bk'], 'L0_xattn_Wv': _L0_xattn_in['Wv'], 'L0_xattn_bv': _L0_xattn_in['bv'], 'L0_xattn_Wg': _L0_xattn_in['Wg'], 'L0_xattn_bg': _L0_xattn_in['bg'], 'L0_xattn_Wo': _L0_xattn_in['Wo'], 'L0_xattn_bo': _L0_xattn_in['bo'], 'L0_ffn_gate_w': _L0_ffn_in['gate_w'], 'L0_ffn_base_wgu': _L0_ffn_in['base_wgu'], 'L0_ffn_base_wd': _L0_ffn_in['base_wd'], 'L0_ffn_exp_wgu': _L0_ffn_in['exp_wgu'], 'L0_ffn_exp_wd': _L0_ffn_in['exp_wd']}

def reference(x, ctx_1024, L0_xattn_Wq, L0_xattn_bq, L0_xattn_Wk, L0_xattn_bk, L0_xattn_Wv, L0_xattn_bv, L0_xattn_Wg, L0_xattn_bg, L0_xattn_Wo, L0_xattn_bo, L0_ffn_gate_w, L0_ffn_base_wgu, L0_ffn_base_wd, L0_ffn_exp_wgu, L0_ffn_exp_wd):
    import jax
    import jax.numpy as jnp

    def _L0_xattn_ref(query, key, value, Wq, bq, Wk, bk, Wv, bv, Wg, bg, Wo, bo):
        import jax, jax.numpy as jnp
        import numpy as np
        B, N, E, H = (2, 1024, 256, 16)
        D = E // H
        SEG_LENS = (256, 512)
        DIL_RATES = (1, 2)

        def _dilated_attention(q, k, v, seg_lens, dil_rates):
            b, n, h, d = q.shape
            G = len(seg_lens)
            g = h // G
            scale = float(d) ** (-0.5)
            outs = []
            for i, (s, r) in enumerate(zip(seg_lens, dil_rates)):
                off = i % r
                hs = slice(i * g, (i + 1) * g)

                def _seg(x):
                    return x[:, :, hs, :].reshape(b, n // s, s, g, d)[:, :, off::r]
                qi, ki, vi = (_seg(q), _seg(k), _seg(v))
                scores = jnp.einsum('bnqhd,bnkhd->bnhqk', qi, ki) * scale
                attn = jax.nn.softmax(scores, axis=-1)
                x = jnp.einsum('bnhqk,bnkhd->bnqhd', attn, vi)
                og = jnp.zeros((b, n // s, s, g, d), q.dtype).at[:, :, off::r].set(x)
                outs.append(og.reshape(b, n, g, d))
            return jnp.concatenate(outs, axis=2)
        b, n, _ = query.shape
        q = query @ Wq + bq
        k = key @ Wk + bk
        v = value @ Wv + bv
        q = q.reshape(b, n, H, D)
        k = k.reshape(b, n, H, D)
        v = v.reshape(b, n, H, D)
        attn_out = _dilated_attention(q, k, v, SEG_LENS, DIL_RATES)
        attn_out = attn_out.reshape(b, n, E)
        gate = jax.nn.sigmoid(query @ Wg + bg)
        attn_out = gate * attn_out
        return attn_out @ Wo + bo

    def _L0_ffn_ref(x, gate_w, base_wgu, base_wd, exp_wgu, exp_wd):
        import jax, jax.numpy as jnp
        import numpy as np
        TOP_K = 2

        def _swiglu_mlp(x, wgu, wd, inter):
            gu = x @ wgu
            a = jax.nn.silu(gu[:, :inter]) * gu[:, inter:]
            return a @ wd
        orig_shape = x.shape
        H = orig_shape[-1]
        I = base_wd.shape[0]
        E = gate_w.shape[1]
        xt = x.reshape(-1, H)
        T = xt.shape[0]
        base_y = _swiglu_mlp(xt, base_wgu, base_wd, I)
        logits = xt @ gate_w
        probs = jax.nn.softmax(logits.astype(jnp.float32), axis=-1)
        topw, topi = jax.lax.top_k(probs, TOP_K)
        topw = topw / jnp.sum(topw, axis=-1, keepdims=True)
        topw = topw.astype(x.dtype)
        cw = jnp.zeros((T, E), x.dtype).at[jnp.arange(T)[:, None], topi].add(topw)
        out = base_y
        for e in range(E):
            ye = _swiglu_mlp(xt, exp_wgu[e], exp_wd[e], I)
            out = out + cw[:, e:e + 1] * ye
        return out.reshape(orig_shape)
    x = x + _L0_xattn_ref(_layernorm(x, axis=-1), ctx_1024, ctx_1024, L0_xattn_Wq, L0_xattn_bq, L0_xattn_Wk, L0_xattn_bk, L0_xattn_Wv, L0_xattn_bv, L0_xattn_Wg, L0_xattn_bg, L0_xattn_Wo, L0_xattn_bo)
    x = x + _L0_ffn_ref(_layernorm(x, axis=-1), L0_ffn_gate_w, L0_ffn_base_wgu, L0_ffn_base_wd, L0_ffn_exp_wgu, L0_ffn_exp_wd)
    return x

_drawn_inputs = setup_inputs


def setup_inputs(seed=0):
    import zlib

    import numpy as np

    out = dict(_drawn_inputs(seed))
    spreads = {'L0_xattn_bq': (0.0, 0.721),
     'L0_xattn_bk': (0.0, 0.8),
     'L0_xattn_bv': (0.0, 0.1),
     'L0_xattn_bg': (0.0, 0.8),
     'L0_xattn_bo': (0.0, 0.1)}
    factors = {'L0_ffn_gate_w': 3.384, 'L0_ffn_exp_wgu': 2.928, 'L0_ffn_exp_wd': 2.931}
    for name, (base, spread) in spreads.items():
        noise = np.random.default_rng([zlib.crc32(name.encode()), seed]).standard_normal(out[name].shape)
        drawn = base * np.exp(spread * noise) if base else spread * noise
        out[name] = jnp.asarray(drawn.astype(out[name].dtype))
    for name, factor in factors.items():
        out[name] = (out[name] * factor).astype(out[name].dtype)
    return out
```

```python
from contextlib import ExitStack

import concourse.bass as bass
from concourse import mybir

F32 = mybir.dt.float32
F32R = mybir.dt.float32r
I32 = mybir.dt.int32
ALU = mybir.AluOpType
ACT = mybir.ActivationFunctionType
X = mybir.AxisListType.X
ds = bass.ds

P = 128
BATCH, NTOK, D = 4, 512, 256
T = BATCH * NTOK
KD = D // P
HEADS, HDIM = 16, 16
GH = HEADS // 2
SEG = 256
NSEG = T // SEG
UNITS = NSEG + BATCH
PAIRS = GH // 2
LN_EPS = 1e-5
F = 704
FB = 6
FSZ = [P] * (F // P) + [F % P]
E = 8
TOPK = 2
JOBS = T * TOPK // SEG + E - 1
COLS = 2 * (JOBS + 1)
ROWS = T + SEG
BIG = 3.0e38


def build(nc, x, ctx_in, Wq, bq, Wk, bk, Wv, bv, Wg, bg, Wo, bo, gate_w, base_wgu, base_wd,
          exp_wgu, exp_wd, out):
    xn_tab = nc.dram_tensor("xn_tab", (ROWS, D), F32, kind="Internal").ap()
    x_seg = x.rearrange("b (s p a) d -> (b s) p (a d)", p=P, a=2)
    ctx_seg = ctx_in.rearrange("b (s p a) d -> (b s) p (a d)", p=P, a=2)
    out_seg = out[0:T, :].rearrange("(s p a) d -> s p (a d)", p=P, a=2)
    xn_seg = xn_tab[0:T, :].rearrange("(s p a) d -> s p (a d)", p=P, a=2)

    es = ExitStack()
    with es:
        def sb(name, shape, dt=F32, where=None):
            return (where or es).enter_context(nc.sbuf_tensor(name, shape, dt))

        def ps(name, shape=(P, 512), where=None):
            return (where or es).enter_context(nc.psum_tensor(name, list(shape), F32))

        def sem(name):
            return es.enter_context(nc.semaphore(name))

        x_all = sb("x_all", [P, NSEG, 2 * D])
        ident = sb("ident", [P, P])
        headmask = sb("headmask", [P, GH])
        ones = sb("ones", [P, P])
        tri = sb("tri", [P, P])
        halves = sb("halves", [P, 2])
        wq_s = sb("wq_s", [P, KD, D])
        wk_s = sb("wk_s", [P, KD, D])
        wv_s = sb("wv_s", [P, KD, D])
        wg_s = sb("wg_s", [P, KD, D])
        wo_s = sb("wo_s", [P, KD, D])
        gw_s = sb("gw_s", [P, KD, E])
        bias_s = sb("bias_s", [P, 3, 2])
        bias_m = sb("bias_m", [P, 2, 2])
        bv_b = sb("bv_b", [P, D])
        bo_b = sb("bo_b", [P, D])
        gT = sb("gT", [P, UNITS * SEG])
        attn = sb("attn", [P, UNITS * SEG])
        xn = [sb(f"xn{h}", [P, 2, D]) for h in range(2)]
        stats = [sb(f"stats{h}", [P, 2, 6]) for h in range(2)]
        mv = [sb(f"mv{h}", [P, 2, 2]) for h in range(2)]
        veps = [sb(f"veps{h}", [P, 2]) for h in range(2)]
        rstd = [sb(f"rstd{h}", [P, 2]) for h in range(2)]
        raw_gu0 = sb("raw_gu0", [P, KD, 2 * F])
        raw_d0 = sb("raw_d0", [P, FB, D])
        logits = sb("logits", [P, 2 * NSEG, E])

        early = ExitStack()
        ctx_s = [sb(f"ctx_s{h}", [P, 2 * D], where=early) for h in range(2)]
        xT = [sb(f"xT{h}", [P, KD, SEG], where=early) for h in range(2)]
        cT = [sb(f"cT{h}", [P, KD, SEG], where=early) for h in range(2)]
        qT = sb("qT", [P, UNITS * SEG], where=early)
        kT = sb("kT", [P, UNITS * SEG], where=early)
        v_all = sb("v_all", [P, UNITS * 2, P], where=early)
        km = [sb(f"km{r}", [P, 2, SEG], where=early) for r in range(PAIRS)]
        qs = [sb(f"qs{h}", [P, SEG], where=early) for h in range(2)]
        vpad = [sb(f"vpad{h}", [P, 2, GH, P], where=early) for h in range(2)]
        prob = [sb(f"prob{r}", [P, 2, 2, SEG], where=early) for r in range(2)]
        pT = [[sb(f"pT{r}{h}", [P, 2, SEG], where=early) for h in range(2)] for r in range(2)]
        nmax = [sb(f"nmax{r}", [P, 2, 2], where=early) for r in range(2)]
        rsum = [sb(f"rsum{h}", [P, 2, GH], where=early) for h in range(2)]
        rinv = [sb(f"rinv{h}", [P, 2, GH], where=early) for h in range(2)]
        rexp = [sb(f"rexp{h}", [P, 2, GH, HDIM], where=early) for h in range(2)]
        rts = [sb(f"rts{h}", [P, SEG], where=early) for h in range(2)]
        early.close()

        ag = [sb(f"ag{h}", [P, 3 * P]) for h in range(2)]
        x2T = [sb(f"x2T{h}", [P, KD, SEG]) for h in range(2)]
        shared = ExitStack()
        x2h = sb("x2h", [P, NSEG, KD, SEG], F32R, where=shared)
        x2l = sb("x2l", [P, NSEG, KD, SEG], F32R, where=shared)
        shared.close()
        raw_gu1 = sb("raw_gu1", [P, KD, 2 * F])
        raw_d1 = sb("raw_d1", [P, FB, D])
        raw_gu, raw_d = [raw_gu0, raw_gu1], [raw_d0, raw_d1]
        xg = [sb(f"xg{h}", [P, 2, D]) for h in range(2)]
        xjh = [sb(f"xjh{h}", [P, KD, SEG], F32R) for h in range(2)]
        xjl = [sb(f"xjl{h}", [P, KD, SEG], F32R) for h in range(2)]
        rest = 2 * NSEG * KD * SEG - (KD * 2 * F + FB * D) - 3 * 2 * KD * SEG
        sb("rest", [P, rest])
        wh_gu = sb("wh_gu", [P, KD, 2 * F], F32R)
        wl_gu = sb("wl_gu", [P, KD, 2 * F], F32R)
        wh_d = sb("wh_d", [P, FB, D], F32R)
        wl_d = sb("wl_d", [P, FB, D], F32R)
        sg = [sb(f"sg{r}", [P, SEG]) for r in range(2)]
        act = [sb(f"act{r}", [P, SEG]) for r in range(2)]
        act_h = sb("act_h", [P, FB, SEG], F32R)
        act_l = sb("act_l", [P, FB, SEG], F32R)
        y_s = [sb(f"y_s{h}", [P, 2, D]) for h in range(2)]
        NT = 2 * NSEG
        desc = sb("desc", [P, E])
        k256 = sb("k256", [P, T // SEG])
        jcol = sb("jcol", [1, JOBS + 1])
        rowid = sb("rowid", [P, TOPK, NT])
        spare = sb("spare", [P, JOBS + 1, 2])
        iota = sb("iota", [P, P])
        m1 = sb("m1", [P, TOPK, NT])
        eq = sb("eq", [P, NT, E])
        fi = sb("fi", [P, NT])
        sel = sb("sel", [P, TOPK, NT, E])
        l2 = sb("l2", [P, NT, E])
        wexp = sb("wexp", [P, 3, NT])
        wts = sb("wts", [P, TOPK, NT])
        member = sb("member", [P, NT, E])
        scan = [sb(f"scan{r}", [P, NT, E]) for r in range(2)]
        ntile = sb("ntile", [P, E, T // SEG])
        tiles = sb("tiles", [P, E])
        tend = [sb(f"tend{r}", [P, E]) for r in range(2)]
        pos = sb("pos", [P, NT, E])
        poss = sb("poss", [P, TOPK, NT])
        posi = sb("posi", [P, 3, TOPK, NT], I32)
        posf = sb("posf", [P, 2, TOPK, NT])
        jobe = sb("jobe", [1, JOBS + 1, E])
        jobf = sb("jobf", [1, JOBS + 1])
        jobi = sb("jobi", [1, JOBS + 1], I32)
        hot = [sb(f"hot{r}", [P, P]) for r in range(2)]
        val = [sb(f"val{r}", [P, 2, COLS]) for r in range(2)]
        tokf = sb("tokf", [P, 3, COLS])
        toki = sb("toki", [P, COLS], I32)
        slot_g = sb("slot_g", [P, 2], I32)
        slot_s = sb("slot_s", [P, 2], I32)
        zero = sb("zero", [P, 2, D])

        bank = [ps(f"bank{n}") for n in range(8)]

        ld_w = sem("ld_w")
        ld_x = [sem(f"ld_x{h}") for h in range(2)]
        ld_c = [sem(f"ld_c{h}") for h in range(2)]
        passed = sem("passed")
        consts = sem("consts")
        dv = sem("dv")
        gp = sem("gp")
        var_rdy = sem("var_rdy")
        rstd_rdy = sem("rstd_rdy")
        xn_rdy = sem("xn_rdy")
        xt_ps = sem("xt_ps")
        ct_ps = sem("ct_ps")
        xt_ev = sem("xt_ev")
        ct_ev = sem("ct_ev")
        q_ps, k_ps, g_ps1, v_ps = sem("q_ps"), sem("k_ps"), sem("g_ps1"), sem("v_ps")
        q_ev, k_ev, ge_ev, v_ev = sem("q_ev"), sem("k_ev"), sem("ge_ev"), sem("v_ev")
        gate_rdy = sem("gate_rdy")
        bm_rdy = sem("bm_rdy")
        qs_rdy, vp_rdy, km_rdy = sem("qs_rdy"), sem("vp_rdy"), sem("km_rdy")
        s_ps = sem("s_ps")
        m_rdy = sem("m_rdy")
        p_rdy = sem("p_rdy")
        t_ps = sem("t_ps")
        pt_ev = [sem(f"pt_ev{h}") for h in range(2)]
        pv_ps = sem("pv_ps")
        o_ev = sem("o_ev")
        rt_ps = sem("rt_ps")
        rexp_rdy, rts_rdy = sem("rexp_rdy"), sem("rts_rdy")
        xbo = sem("xbo")
        ag_rdy = sem("ag_rdy")
        xo_ps = sem("xo_ps")
        x1_rdy = sem("x1_rdy")
        var2, rstd2, xn2_rdy = sem("var2"), sem("rstd2"), sem("xn2_rdy")
        xn2_st = [sem(f"xn2_st{h}") for h in range(2)]
        t2_ps = sem("t2_ps")
        t2_ev = sem("t2_ev")
        lg_ps = sem("lg_ps")
        lg_ev = sem("lg_ev")
        x2h_rdy, x2l_rdy = sem("x2h_rdy"), sem("x2l_rdy")
        ld_raw = [sem(f"ld_raw{h}") for h in range(2)]
        wh_rdy, wl_rdy = sem("wh_rdy"), sem("wl_rdy")
        wd_rdy, wdl_rdy = sem("wd_rdy"), sem("wdl_rdy")
        g_ps, u_ps = sem("g_ps"), sem("u_ps")
        sg_rdy = sem("sg_rdy")
        a_rdy = sem("a_rdy")
        ah_rdy = sem("ah_rdy")
        al_rdy = sem("al_rdy")
        dn_ps = sem("dn_ps")
        y_rdy = sem("y_rdy")
        out_st = [sem(f"out_st{h}") for h in range(2)]
        zero_st = sem("zero_st")
        m_in, dif_rdy, ex_rdy = sem("m_in"), sem("dif_rdy"), sem("ex_rdy")
        pre_ps, pre_ev = sem("pre_ps"), sem("pre_ev")
        hot_rdy, hot_ps = sem("hot_rdy"), sem("hot_ps")
        jobs_rdy, slots_rdy = sem("jobs_rdy"), sem("slots_rdy")
        sg_cp, ss_cp = sem("sg_cp"), sem("ss_cp")
        gath = [[sem(f"gath{h}{a}") for a in range(2)] for h in range(2)]
        tj_ps, xjh_rdy, xjl_rdy = sem("tj_ps"), sem("xjh_rdy"), sem("xjl_rdy")
        scat = [sem(f"scat{a}") for a in range(2)]

        block = es.enter_context(nc.Block())

        def alone(eng):
            eng.sem_inc(passed, 1)

        def view(t, *shape):
            pat = {2: "p (a b) -> p a b", 3: "p (a b c) -> p a b c"}[len(shape)]
            n = 1
            for k in shape:
                n *= k
            return t[:, 0:n].rearrange(pat, **dict(zip("abc", shape)))

        def gu(t, kd, f0, sz):
            return t[:, kd, :].rearrange("p (t f) -> p t f", t=2)[:, :, f0:f0 + sz]

        @block.sync
        def _(sp):
            def load_seg(s, h):
                sp.dma_start(x_all[:, s, :], x_seg[s]).then_inc(ld_x[h], 16)
                sp.dma_start(ctx_s[h][:, :], ctx_seg[s]).then_inc(ld_c[h], 16)

            load_seg(0, 0)
            load_seg(1, 1)
            with sp.Fori(1, NSEG // 2) as i:
                for h in range(2):
                    sp.wait_ge(ld_x[h], 16 * i)
                    alone(sp)
                    sp.wait_ge(ct_ps, 2 * i + (h + 1))
                    load_seg(2 * i + h, h)
            def load_mlp(h, w_gu, w_d):
                sp.dma_start(raw_gu[h][:, :, :], w_gu.rearrange("(k p) f -> p k f", p=P)).then_inc(ld_raw[h], 16)
                sp.dma_start(raw_d[h][:, 0:FB - 1, :], w_d[0:(FB - 1) * P, :].rearrange("(k p) n -> p k n", p=P)).then_inc(ld_raw[h], 16)
                sp.dma_start(raw_d[h][0:FSZ[-1], FB - 1, :], w_d[(FB - 1) * P:F, :]).then_inc(ld_raw[h], 16)

            load_mlp(0, base_wgu, base_wd)
            with sp.Fori(0, NSEG // 2) as i:
                for h in range(2):
                    sp.wait_ge(xn2_rdy, 2 * i + (h + 1))
                    alone(sp)
                    sp.wait_ge(xn2_st[h], 16 * i)
                    sp.dma_start(xn_seg[2 * i + h], xn[h][:, :, :].rearrange("p a d -> p (a d)")).then_inc(xn2_st[h], 16)
            sp.wait_ge(consts, 2)
            sp.dma_start(xn_tab[T:ROWS, :].rearrange("(a p) d -> p a d", a=2), zero[:, :, :]).then_inc(zero_st, 16)
            sp.dma_start(out[T:ROWS, :].rearrange("(a p) d -> p a d", a=2), zero[:, :, :]).then_inc(zero_st, 16)
            with sp.Fori(0, NSEG // 2) as i:
                for h in range(2):
                    sp.wait_ge(y_rdy, 2 * i + (h + 3))
                    alone(sp)
                    sp.wait_ge(out_st[h], 16 * i)
                    sp.dma_start(out_seg[2 * i + h], y_s[h][:, :, :].rearrange("p a d -> p (a d)")).then_inc(out_st[h], 16)
            def load_expert(j, h):
                e = sp.value_load(jobi[0:1, ds(j, 1)], min_val=0, max_val=E - 1)
                load_mlp(h, exp_wgu[ds(e, 1), :, :].rearrange("u k f -> (u k) f"),
                         exp_wd[ds(e, 1), :, :].rearrange("u k n -> (u k) n"))

            sp.wait_ge(jobs_rdy, 1)
            sp.wait_ge(wl_rdy, FB)
            sp.wait_ge(wdl_rdy, FB)
            load_expert(0, 0)
            sp.wait_ge(u_ps, FB * NSEG)
            load_expert(1, 1)

            def load_next(j, h):
                sp.wait_ge(wl_rdy, FB * j)
                sp.wait_ge(wdl_rdy, FB * j)
                alone(sp)
                load_expert(j, h)

            with sp.Fori(1, JOBS // 2) as i:
                for h in range(2):
                    load_next(2 * i + h, h)
            load_next(JOBS - 1, 0)
            sp.wait_ge(ld_raw[0], 48 * (JOBS // 2 + 2))
            sp.wait_ge(ld_raw[1], 48 * (JOBS // 2))
            for h in range(2):
                sp.wait_ge(xn2_st[h], 16 * (NSEG // 2))
                sp.wait_ge(out_st[h], 16 * (NSEG // 2))
            for a in range(2):
                sp.wait_ge(scat[a], 16 * JOBS)
            sp.wait_ge(zero_st, 32)

        @block.gpsimd
        def _(pool):
            n = [0]

            def step(ins):
                n[0] += 1
                ins.then_inc(gp, 1)
                pool.wait_ge(gp, n[0])

            step(pool.memset(ident[:, :], 0.0))
            step(pool.affine_select(out=ident[:, :], in_=ident[:, :], compare_op=ALU.not_equal, fill=1.0,
                                    base=0, pattern=[[-1, P]], channel_multiplier=1))
            step(pool.memset(headmask[:, :], 1.0))
            step(pool.affine_select(out=headmask[:, :], in_=headmask[:, :], compare_op=ALU.is_ge, fill=0.0,
                                    base=0, pattern=[[-HDIM, GH]], channel_multiplier=1))
            step(pool.affine_select(out=headmask[:, :], in_=headmask[:, :], compare_op=ALU.is_ge, fill=0.0,
                                    base=HDIM - 1, pattern=[[HDIM, GH]], channel_multiplier=-1))
            step(pool.memset(halves[:, :], -0.5))
            step(pool.memset(ones[:, :], 1.0))
            step(pool.memset(tri[:, :], 1.0))
            step(pool.affine_select(out=tri[:, :], in_=tri[:, :], compare_op=ALU.is_gt, fill=0.0,
                                    base=0, pattern=[[1, P]], channel_multiplier=-1))
            for h in range(2):
                step(pool.memset(vpad[h][:, :, :, :], 0.0))
            pool.sem_inc(consts, 1)

            with pool.Fori(0, NSEG // 2) as i:
                for h in range(2):
                    pool.wait_ge(var_rdy, 2 * i + (h + 1))
                    pool.tensor_tensor(rstd[h][:, :], veps[h][:, :], halves[:, :], ALU.pow).then_inc(rstd_rdy, 1)

            pool.wait_ge(q_ev, NSEG)
            pool.wait_ge(k_ev, NSEG)
            pool.wait_ge(v_ev, NSEG)
            with pool.Fori(0, UNITS // 2) as i:
                for h in range(2):
                    u = 2 * i + h
                    cols = ds(SEG * u, SEG)
                    pool.wait_ge(s_ps, 8 * u)
                    alone(pool)
                    pool.tensor_copy(qs[h][:, :], qT[:, cols]).then_inc(qs_rdy, 1)
                    for hp in range(PAIRS):
                        pool.wait_ge(s_ps, 8 * u + (2 * hp + 2))
                        alone(pool)
                        pool.tensor_tensor(km[hp][:, :, :],
                                           kT[:, cols].unsqueeze(1).to_broadcast([P, 2, SEG]),
                                           headmask[:, 2 * hp:2 * hp + 2].unsqueeze(2).to_broadcast([P, 2, SEG]),
                                           ALU.mult).then_inc(km_rdy, 1)
                    pool.wait_ge(rt_ps, u + 1)
                    alone(pool)
                    for kb in range(2):
                        diag = vpad[h][:, kb, :, :].rearrange("p g c -> p (g c)")
                        last = pool.tensor_copy(
                            bass.AP(diag.tensor, diag.offset, [list(diag.ap[0]), [P + HDIM, GH], [1, HDIM]]),
                            v_all[:, ds(2 * u + kb, 1), :].rearrange("p u (g c) -> p (u g) c", g=GH))
                    last.then_inc(vp_rdy, 1)

            pool.wait_ge(o_ev, UNITS)
            step(pool.memset(zero[:, :, :], 0.0))
            step(pool.iota(desc[:, :], [[-1, E]], base=E, channel_multiplier=0, allow_small_or_imprecise_dtypes=True))
            step(pool.iota(k256[:, :], [[SEG, T // SEG]], base=0, channel_multiplier=0, allow_small_or_imprecise_dtypes=True))
            step(pool.iota(jcol[:, :], [[1, JOBS + 1]], base=0, channel_multiplier=0, allow_small_or_imprecise_dtypes=True))
            step(pool.iota(rowid[:, :, :].rearrange("p c (s a) -> p c s a", a=2), [[0, TOPK], [SEG, NSEG], [1, 2]], base=1, channel_multiplier=2, allow_small_or_imprecise_dtypes=True))
            step(pool.iota(spare[:, :, :], [[0, JOBS + 1], [P, 2]], base=T + 1, channel_multiplier=1, allow_small_or_imprecise_dtypes=True))
            step(pool.iota(iota[:, :], [[1, P]], base=0, channel_multiplier=0, allow_small_or_imprecise_dtypes=True))
            pool.sem_inc(consts, 1)

            with pool.Fori(0, NSEG // 2) as i:
                for h in range(2):
                    pool.wait_ge(var2, 2 * i + (h + 1))
                    pool.tensor_tensor(rstd[h][:, :], veps[h][:, :], halves[:, :], ALU.pow).then_inc(rstd2, 1)
                for h in range(2):
                    pool.wait_ge(x2h_rdy, 2 * i + (h + 1))
                    alone(pool)
                    pool.tensor_tensor(x2l[:, ds(2 * i + h, 1), :, :].rearrange("p u k t -> p (u k) t"), x2T[h][:, :, :],
                                       x2h[:, ds(2 * i + h, 1), :, :].rearrange("p u k t -> p (u k) t").bitcast(F32),
                                       ALU.subtract).then_inc(x2l_rdy, 1)

            def low_parts(m, r):
                for fb in range(FB):
                    f0, sz = fb * P, FSZ[fb]
                    pool.wait_ge(wh_rdy, FB * m + (fb + 1))
                    for kd in range(KD):
                        last = pool.tensor_tensor(gu(wl_gu, kd, f0, sz), gu(raw_gu[r], kd, f0, sz),
                                                  gu(wh_gu, kd, f0, sz).bitcast(F32), ALU.subtract)
                    last.then_inc(wl_rdy, 1)
                for fb in range(FB):
                    sz = FSZ[fb]
                    pool.wait_ge(wd_rdy, FB * m + (fb + 1))
                    pool.tensor_tensor(wl_d[0:sz, fb, :], raw_d[r][0:sz, fb, :],
                                       wh_d[0:sz, fb, :].bitcast(F32), ALU.subtract).then_inc(wdl_rdy, 1)

            low_parts(0, 0)
            pool.wait_ge(slots_rdy, 1)
            pool.wait_ge(zero_st, 32)
            for h in range(2):
                pool.wait_ge(xn2_st[h], 16 * (NSEG // 2))
                pool.wait_ge(out_st[h], 16 * (NSEG // 2))

            def gather(j, h):
                pool.wait_ge(tj_ps, j)
                alone(pool)
                pool.tensor_copy(slot_g[:, :], toki[:, ds(2 * j, 2)]).then_inc(sg_cp, 1)
                pool.wait_ge(sg_cp, j + 1)
                alone(pool)
                for a in range(2):
                    pool.indirect_dma_start(xg[h][:, a, :], None, xn_tab[:, :],
                                            bass.IndirectOffsetOnAxis(slot_g[:, a:a + 1], 0)).then_inc(gath[h][a], 16)

            def expert_job(j, i, h):
                for a in range(2):
                    pool.wait_ge(gath[h][a], 16 * i + 16)
                if not (isinstance(j, int) and j == JOBS - 1):
                    gather(j + 1, 1 - h)
                    low_parts(j + 2, 1 - h)
                for a in range(2):
                    pool.wait_ge(scat[a], 16 * j)
                alone(pool)
                pool.tensor_copy(slot_s[:, :], toki[:, ds(2 * j, 2)]).then_inc(ss_cp, 1)
                pool.wait_ge(ss_cp, j + 1)
                pool.wait_ge(y_rdy, j + (NSEG + 3))
                alone(pool)
                for a in range(2):
                    pool.indirect_dma_start(out[:, :], bass.IndirectOffsetOnAxis(slot_s[:, a:a + 1], 0),
                                            y_s[h][:, a, :], None, compute_op=ALU.add).then_inc(scat[a], 16)

            gather(0, 0)
            low_parts(1, 0)
            with pool.Fori(0, JOBS // 2) as i:
                for h in range(2):
                    expert_job(2 * i + h, i, h)
            expert_job(JOBS - 1, JOBS // 2, 0)

        @block.scalar
        def _(sc):
            sc.sem_inc(p_rdy, 4)
            sc.sem_inc(sg_rdy, 2)
            sc.sem_inc(ah_rdy, 2)
            loads = [(w_s[:, :, :], w.rearrange("(k p) o -> p k o", p=P)) for w_s, w in
                     ((wq_s, Wq), (wk_s, Wk), (wg_s, Wg), (wv_s, Wv), (wo_s, Wo), (gw_s, gate_w))]
            for n, b in enumerate((bq, bk, bg)):
                for ob in range(2):
                    loads.append((bias_s[:, n, ob:ob + 1], b[ob * P:(ob + 1) * P].rearrange("(p u) -> p u", u=1)))
            loads += [(bv_b[:, :], bv.partition_broadcast(P)), (bo_b[:, :], bo.partition_broadcast(P))]
            for dst, src in loads:
                sc.dma_start(dst, src).then_inc(ld_w, 16)
            sc.wait_ge(ld_w, 16 * len(loads))
            sc.activation(bias_m[:, 0, :], bias_s[:, 0, :], ACT.Copy, scale=0.25)
            sc.activation(bias_m[:, 1, :], bias_s[:, 2, :], ACT.Copy, scale=-1.0).then_inc(bm_rdy, 1)
            sc.wait_ge(bm_rdy, 1)

            with sc.Fori(0, NSEG // 2) as i:
                for h in range(2):
                    s = 2 * i + h
                    g0, g1 = ds(SEG * s, SEG), ds(T + P * s, P)
                    sc.wait_ge(xt_ps, s + 3)
                    sc.wait_ge(v_ps, s + 1)
                    sc.activation(xT[h][:, :, :], view(bank[0], KD, SEG), ACT.Copy).then_inc(xt_ev, 1)
                    sc.wait_ge(q_ps, s + 1)
                    sc.activation(qT[:, g0], bank[2][:, 0:SEG], ACT.Identity, bias=bias_m[:, 0, 0:1], scale=0.25)
                    sc.activation(qT[:, g1], bank[2][:, SEG:SEG + P], ACT.Identity, bias=bias_m[:, 0, 1:2],
                                  scale=0.25).then_inc(q_ev, 1)
                    sc.wait_ge(g_ps1, s + 1)
                    sc.activation(gT[:, g0], bank[4][:, 0:SEG], ACT.Exp, bias=bias_m[:, 1, 0:1], scale=-1.0)
                    sc.activation(gT[:, g1], bank[4][:, SEG:SEG + P], ACT.Exp, bias=bias_m[:, 1, 1:2],
                                  scale=-1.0).then_inc(ge_ev, 1)

            def exps(g, h, hp):
                r = g % 2 if isinstance(g, int) else hp % 2
                sc.wait_ge(t_ps, 2 * g + 2)
                for qb in range(2):
                    sc.wait_ge(m_rdy, 2 * g + (qb + 1))
                    for k in range(2):
                        last = sc.activation(prob[r][:, qb, k, :], view(bank[2 * r + qb], 2, SEG)[:, k, :],
                                             ACT.Exp, bias=nmax[r][:, qb, k:k + 1],
                                             accum_out=rsum[h][:, qb, 2 * hp + k:2 * hp + k + 1])
                    last.then_inc(p_rdy, 1)

            def evacuate(g, hp):
                r = hp % 2
                sc.wait_ge(t_ps, 2 * g + 6)
                sc.wait_ge(pv_ps, g + 1)
                sc.activation(pT[r][1][:, :, :], view(bank[5], 2, SEG), ACT.Copy).then_inc(pt_ev[1], 1)

            def attend(i, last_units=False):
                for c in range(2 * PAIRS):
                    g = 8 * i + c
                    if not (last_units and c + 2 >= 2 * PAIRS):
                        exps(g + 2, ((c + 2) // PAIRS) % 2, (c + 2) % PAIRS)
                    if not (last_units and c + 1 >= 2 * PAIRS):
                        evacuate(g + 1, (c + 1) % PAIRS)
                    if c % PAIRS == PAIRS - 1:
                        h = c // PAIRS
                        sc.wait_ge(rt_ps, 2 * i + (h + 3))
                        sc.wait_ge(o_ev, 2 * i + h)
                        sc.activation(rts[h][:, :], bank[7][:, 0:SEG], ACT.Copy).then_inc(rts_rdy, 1)

            exps(0, 0, 0)
            exps(1, 0, 1)
            evacuate(0, 0)
            with sc.Fori(0, UNITS // 2 - 1) as i:
                attend(i)
            attend(UNITS // 2 - 1, True)

            def high_down(m, r, fb):
                sz = FSZ[fb]
                sc.activation(wh_d[0:sz, fb, :], raw_d[r][0:sz, fb, :], ACT.Copy).then_inc(wd_rdy, 1)

            sc.wait_ge(o_ev, UNITS)
            sc.wait_ge(ld_raw[0], 48)
            for fb in range(FB):
                high_down(0, 0, fb)
            with sc.Fori(0, NSEG // 2) as i:
                for h in range(2):
                    sc.wait_ge(t2_ev, 2 * i + (h + 1))
                    sc.activation(x2h[:, ds(2 * i + h, 1), :, :].rearrange("p u k t -> p (u k) t"),
                                  x2T[h][:, :, :], ACT.Copy).then_inc(x2h_rdy, 1)

            sc.wait_ge(dif_rdy, 1)
            sc.activation(wexp[:, 1, :], wexp[:, 0, :], ACT.Exp).then_inc(ex_rdy, 1)

            def silu(m, fb):
                sz = FSZ[fb]
                sc.wait_ge(g_ps, FB * m + (fb + 1))
                sc.wait_ge(a_rdy, FB * m + (fb + 1))
                sc.activation(sg[fb % 2][0:sz, :], bank[fb % 2][0:sz, 0:SEG], ACT.Silu).then_inc(sg_rdy, 1)

            def act_high(m, fb):
                sz = FSZ[fb]
                sc.wait_ge(a_rdy, FB * m + (fb + 3))
                sc.wait_ge(dn_ps, FB * m + (fb + 1))
                sc.activation(act_h[0:sz, fb, :], act[fb % 2][0:sz, :], ACT.Copy).then_inc(ah_rdy, 1)

            with sc.Fori(0, NSEG) as s:
                for fb in range(FB):
                    silu(s, fb)
                    if fb:
                        act_high(s, fb - 1)
                act_high(s, FB - 1)

            def token_high(j, h):
                sc.wait_ge(tj_ps, j + 1)
                sc.activation(xjh[h][:, :, :], view(bank[6], KD, SEG), ACT.Copy).then_inc(xjh_rdy, 1)

            def next_down(j, i, h, fb):
                sc.wait_ge(dn_ps, FB * (j + NSEG) + (fb + 7))
                high_down(j + 2, 1 - h, fb)

            def expert_job(j, i, h, last=False):
                m = j + NSEG
                for fb in range(FB):
                    silu(m, fb)
                    if fb:
                        act_high(m, fb - 1)
                    if fb == 4 and not last:
                        token_high(j + 1, 1 - h)
                    if fb >= 3 and not last:
                        if fb == 3:
                            sc.wait_ge(ld_raw[1 - h], 48 * i + (48 * 3 if h else 48))
                        next_down(j, i, h, fb - 3)
                act_high(m, FB - 1)
                sc.wait_ge(dn_ps, FB * m + 2 * FB)
                sc.wait_ge(ss_cp, j)
                for a in range(2):
                    ins = sc.activation(y_s[h][:, a, :], view(bank[4 + h], 2, D)[:, a, :], ACT.Copy,
                                        scale=tokf[:, 1, ds(2 * j + a, 1)])
                ins.then_inc(y_rdy, 1)
                if not last:
                    for fb in range(3, FB):
                        next_down(j, i, h, fb)

            for h in range(2):
                sc.wait_ge(out_st[h], 16 * (NSEG // 2))
            sc.wait_ge(slots_rdy, 1)
            sc.wait_ge(ld_raw[0], 96)
            sc.wait_ge(dn_ps, FB * NSEG + 6)
            for fb in range(FB):
                high_down(1, 0, fb)
            token_high(0, 0)
            with sc.Fori(0, JOBS // 2) as i:
                for h in range(2):
                    expert_job(2 * i + h, i, h)
            expert_job(JOBS - 1, JOBS // 2, 0, True)

        @block.tensor
        def _(pe):
            for s_, c_ in ((xt_ps, 2), (ct_ps, 2), (v_ps, 2), (s_ps, 8), (t_ps, 4), (pv_ps, 2), (rt_ps, 2),
                           (xo_ps, 2), (t2_ps, 2), (lg_ps, 2), (dn_ps, 6), (hot_ps, 2)):
                pe.sem_inc(s_, c_)
            pe.wait_ge(consts, 1)
            pe.wait_ge(ld_w, 16 * 14)

            def transposes(dst, src):
                for kd in range(KD):
                    for a in range(2):
                        last = pe.transpose(dst[:, kd * SEG + a * P:kd * SEG + (a + 1) * P],
                                            src[:, a, kd * P:(kd + 1) * P], ident[:, :])
                return last

            with pe.Fori(0, NSEG // 2) as i:
                for h in range(2):
                    s = 2 * i + h
                    pe.wait_ge(xn_rdy, s + 1)
                    pe.wait_ge(xt_ev, s)
                    transposes(bank[0], xn[h]).then_inc(xt_ps, 1)
                    pe.wait_ge(ld_c[h], 16 * i + 16)
                    pe.wait_ge(ct_ev, s)
                    transposes(bank[1], ctx_s[h][:, :].rearrange("p (a d) -> p a d", a=2)).then_inc(ct_ps, 1)

                    def project(bk, w, src, done, free):
                        pe.wait_ge(free, s)
                        for n, (c0, t0) in enumerate(((0, 0), (SEG, P))):
                            for kd in range(KD):
                                last = pe.matmul(bank[bk][:, c0:c0 + SEG - t0], w[:, kd, n * P:(n + 1) * P],
                                                 src[:, kd, t0:SEG], start=(kd == 0), stop=(kd == KD - 1))
                        last.then_inc(done, 1)

                    pe.wait_ge(xt_ev, s + 1)
                    project(2, wq_s, xT[h], q_ps, q_ev)
                    project(4, wg_s, xT[h], g_ps1, ge_ev)
                    pe.wait_ge(ct_ev, s + 1)
                    project(3, wk_s, cT[h], k_ps, k_ev)
                    pe.wait_ge(v_ev, s)
                    for a in range(2):
                        n = P if a == 0 else D
                        for kd in range(KD):
                            last = pe.matmul(bank[5][:, a * D:a * D + n], cT[h][:, kd, a * P:(a + 1) * P],
                                             wv_s[:, kd, 0:n], start=(kd == 0), stop=(kd == KD - 1))
                    last.then_inc(v_ps, 1)

            def scores(g, u, h, hp):
                if hp == 0:
                    pe.wait_ge(qs_rdy, u + 1)
                pe.wait_ge(km_rdy, g + 1)
                for qb in range(2):
                    pe.wait_ge(p_rdy, 2 * g + (qb + 1))
                    pe.matmul(bank[2 * (hp % 2) + qb][:, :], qs[h][:, qb * P:(qb + 1) * P],
                              km[hp][:, :, :].rearrange("p k t -> p (k t)"), start=True, stop=True).then_inc(s_ps, 1)

            def transpose_probs(g, hp):
                pe.wait_ge(p_rdy, 2 * g + 6)
                for k in range(2):
                    pe.wait_ge(pt_ev[k], g)
                    for kb in range(2):
                        for qb in range(2):
                            last = pe.transpose(bank[4 + k][:, kb * SEG + qb * P:kb * SEG + (qb + 1) * P],
                                                prob[hp % 2][:, qb, k, kb * P:(kb + 1) * P], ident[:, :])
                    last.then_inc(t_ps, 1)

            def values(g, u, h, hp):
                if hp == 0:
                    pe.wait_ge(vp_rdy, u + 1)
                    pe.wait_ge(o_ev, u)
                for k in range(2):
                    pe.wait_ge(pt_ev[k], g + 1)
                    for kb in range(2):
                        last = pe.matmul(bank[6][:, 0:SEG], vpad[h][:, kb, 2 * hp + k, :], pT[hp % 2][k][:, kb, :],
                                         start=(hp == 0 and k == 0 and kb == 0),
                                         stop=(hp == PAIRS - 1 and k == 1 and kb == 1))
                last.then_inc(pv_ps, 1)
                if hp == PAIRS - 1:
                    pe.wait_ge(rexp_rdy, u + 1)
                    pe.wait_ge(rts_rdy, u)
                    for qb in range(2):
                        last = pe.transpose(bank[7][:, qb * P:(qb + 1) * P],
                                            rexp[h][:, qb, :, :].rearrange("p g c -> p (g c)"), ident[:, :])
                    last.then_inc(rt_ps, 1)

            def attend(i, last_units=False):
                for c in range(2 * PAIRS):
                    g = 8 * i + c
                    if not (last_units and c + 2 >= 2 * PAIRS):
                        n = c + 2
                        scores(g + 2, 2 * i + n // PAIRS, (n // PAIRS) % 2, n % PAIRS)
                    if not (last_units and c + 1 >= 2 * PAIRS):
                        transpose_probs(g + 1, (c + 1) % PAIRS)
                    values(g, 2 * i + c // PAIRS, c // PAIRS, c % PAIRS)

            scores(0, 0, 0, 0)
            scores(1, 0, 0, 1)
            transpose_probs(0, 0)
            with pe.Fori(0, UNITS // 2 - 1) as i:
                attend(i)
            attend(UNITS // 2 - 1, True)

            with pe.Fori(0, NSEG // 2) as i:
                for h in range(2):
                    s = 2 * i + h
                    pe.wait_ge(ag_rdy, s + 1)
                    pe.wait_ge(x1_rdy, 2 * i)
                    xo = view(bank[h], 2, D)
                    pe.matmul(xo[:, 0, :], ag[h][:, 0:P], wo_s[:, 0, :], start=True, stop=True)
                    pe.matmul(xo[:, 1, :], ag[h][:, P:2 * P], wo_s[:, 0, :], start=True, stop=False)
                    pe.matmul(xo[:, 1, :], ag[h][:, 2 * P:3 * P], wo_s[:, 1, :], start=False, stop=True).then_inc(xo_ps, 1)
                for h in range(2):
                    s = 2 * i + h
                    pe.wait_ge(xn2_rdy, s + 1)
                    pe.wait_ge(t2_ev, 2 * i)
                    transposes(bank[2 + h], xn[h]).then_inc(t2_ps, 1)
                for h in range(2):
                    s = 2 * i + h
                    pe.wait_ge(t2_ev, s + 1)
                    pe.wait_ge(lg_ev, 2 * i)
                    for a in range(2):
                        for kd in range(KD):
                            last = pe.matmul(bank[4 + h][:, a * E:(a + 1) * E], x2T[h][:, kd, a * P:(a + 1) * P],
                                             gw_s[:, kd, :], start=(kd == 0), stop=(kd == KD - 1))
                    last.then_inc(lg_ps, 1)

            pe.wait_ge(m_in, 1)
            mem = member[:, :, :].rearrange("p t e -> p (t e)")
            pe.matmul(bank[7][:, 0:P], tri[:, :], mem, start=True, stop=True)
            pe.matmul(bank[7][:, P:2 * P], ones[:, :], mem, start=True, stop=True).then_inc(pre_ps, 1)

            def up(m, fb, high, low):
                sz = FSZ[fb]
                for n, (t, free, done) in enumerate(((0, sg_rdy, g_ps), (1, a_rdy, u_ps))):
                    pe.wait_ge(free, FB * m + (fb + 1))
                    alone(pe)
                    o = bank[2 * n + fb % 2][0:sz, 0:SEG]
                    f0 = t * F + fb * P
                    for kd in range(KD):
                        pe.matmul(o, wh_gu[:, kd, f0:f0 + sz], high(kd), start=(kd == 0), stop=False)
                        pe.matmul(o, wh_gu[:, kd, f0:f0 + sz], low(kd), start=False, stop=False)
                        last = pe.matmul(o, wl_gu[:, kd, f0:f0 + sz], high(kd), start=False, stop=(kd == KD - 1))
                    last.then_inc(done, 1)

            def down(m, fb, h):
                sz = FSZ[fb]
                if fb == 0:
                    pe.wait_ge(y_rdy, m + 1)
                pe.wait_ge(ah_rdy, FB * m + (fb + 3))
                pe.wait_ge(al_rdy, FB * m + (fb + 3))
                y = view(bank[4 + h], 2, D)
                for a in range(2):
                    t = slice(a * P, (a + 1) * P)
                    pe.matmul(y[:, a, :], act_h[0:sz, fb, t], wh_d[0:sz, fb, :], start=(fb == 0 and a == 0),
                              stop=False, skip_group_check=True)
                    pe.matmul(y[:, a, :], act_h[0:sz, fb, t], wl_d[0:sz, fb, :], start=False, stop=False,
                              skip_group_check=True)
                    last = pe.matmul(y[:, a, :], act_l[0:sz, fb, t], wh_d[0:sz, fb, :], start=False,
                                     stop=(fb == FB - 1 and a == 1), skip_group_check=True)
                last.then_inc(dn_ps, 1)

            def base_tokens(t, s):
                return lambda kd: t[:, ds(s, 1), kd, :].rearrange("p u t -> p (u t)")

            pe.wait_ge(wl_rdy, FB)
            pe.wait_ge(wdl_rdy, FB)
            pe.wait_ge(pre_ev, 1)
            slots = bank[7][:, 0:2 * COLS]
            pe.matmul(slots, ones[:, :], val[0][:, :, :].rearrange("p v c -> p (v c)"), start=True, stop=False,
                      skip_group_check=True).then_inc(hot_ps, 1)

            with pe.Fori(0, NSEG // 2) as i:
                for h in range(2):
                    s = 2 * i + h
                    pe.wait_ge(x2l_rdy, s + 1)
                    for fb in range(FB):
                        up(s, fb, base_tokens(x2h, s), base_tokens(x2l, s))
                        if fb >= 2:
                            down(s, fb - 2, h)
                        if fb < 4:
                            pe.wait_ge(hot_rdy, 4 * s + (fb + 1))
                            pe.matmul(slots, hot[fb % 2][:, :], val[fb % 2][:, :, :].rearrange("p v c -> p (v c)"),
                                      start=False, stop=False, skip_group_check=True).then_inc(hot_ps, 1)
                    down(s, FB - 2, h)
                    down(s, FB - 1, h)

            def job_tokens(j, i, h):
                for a in range(2):
                    pe.wait_ge(gath[h][a], 16 * i + 16)
                pe.wait_ge(xjl_rdy, j)
                transposes(bank[6], xg[h]).then_inc(tj_ps, 1)

            def expert_job(j, i, h, last=False):
                m = j + NSEG
                pe.wait_ge(xjl_rdy, j + 1)
                for fb in range(FB):
                    pe.wait_ge(wl_rdy, FB * j + (FB + fb + 1))
                    up(m, fb, lambda kd: xjh[h][:, kd, :], lambda kd: xjl[h][:, kd, :])
                    if fb >= 2:
                        pe.wait_ge(wdl_rdy, FB * j + (FB + fb - 1))
                        down(m, fb - 2, h)
                    if fb == 3 and not last:
                        job_tokens(j + 1, i + h, 1 - h)
                for fb in (FB - 2, FB - 1):
                    pe.wait_ge(wdl_rdy, FB * j + (FB + fb + 1))
                    down(m, fb, h)

            job_tokens(0, 0, 0)
            with pe.Fori(0, JOBS // 2) as i:
                for h in range(2):
                    expert_job(2 * i + h, i, h)
            expert_job(JOBS - 1, JOBS // 2, 0, True)

        @block.vector
        def _(ve):
            chain = dict(n=0, i=0, per=0)

            def mark(ins):
                chain["n"] += 1
                ins.then_inc(dv, 1)

            def chained():
                ve.wait_ge(dv, chain["i"] * chain["per"] + chain["n"])

            def step(ins):
                mark(ins)
                chained()

            def loop_of(i, per):
                chain.update(i=i, per=per, at=chain["n"])

            def loop_end(count):
                assert chain["n"] - chain["at"] == chain["per"], (chain, "per")
                chain["n"] += chain["per"] * (count - 1)
                chain.update(i=0, per=0)

            ve.sem_inc(a_rdy, 2)
            ve.sem_inc(y_rdy, 2)
            ve.sem_inc(al_rdy, 2)

            def variance(src, h, done):
                alone(ve)
                for a in range(2):
                    mark(ve.bn_stats(stats[h][:, a, :], src[:, a, :]))
                chained()
                alone(ve)
                for a in range(2):
                    mark(ve.bn_aggr(mv[h][:, a, :], stats[h][:, a, :]))
                chained()
                ve.tensor_scalar(veps[h][:, :], mv[h][:, :, 1], LN_EPS, None, ALU.add).then_inc(done, 1)

            def normalise(src, h, done):
                for a in range(2):
                    last = ve.tensor_scalar(xn[h][:, a, :], src[:, a, :], mv[h][:, a, 0:1], rstd[h][:, a:a + 1],
                                            ALU.subtract, ALU.mult)
                last.then_inc(done, 1)

            def seg_rows(s):
                return x_all[:, ds(s, 1), :].rearrange("p u (a d) -> p (u a) d", a=2)

            with ve.Fori(0, NSEG // 2) as i:
                loop_of(i, 8)
                for h in range(2):
                    ve.wait_ge(ld_x[h], 16 * i + 16)
                    variance(seg_rows(2 * i + h), h, var_rdy)
                for h in range(2):
                    ve.wait_ge(rstd_rdy, 2 * i + (h + 1))
                    ve.wait_ge(xt_ps, 2 * i + (h + 1))
                    normalise(seg_rows(2 * i + h), h, xn_rdy)
                for h in range(2):
                    s = 2 * i + h
                    ve.wait_ge(ct_ps, s + 3)
                    ve.wait_ge(v_ps, s + 1)
                    ve.tensor_copy(cT[h][:, :, :], view(bank[1], KD, SEG)).then_inc(ct_ev, 1)
                    g0, g1 = ds(SEG * s, SEG), ds(T + P * s, P)
                    ve.wait_ge(k_ps, s + 1)
                    ve.tensor_scalar(kT[:, g0], bank[3][:, 0:SEG], bias_s[:, 1, 0:1], None, ALU.add)
                    ve.tensor_scalar(kT[:, g1], bank[3][:, SEG:SEG + P], bias_s[:, 1, 1:2], None,
                                     ALU.add).then_inc(k_ev, 1)
                    ve.wait_ge(v_ps, s + 3)
                    pv = view(bank[5], 2, D)
                    ve.tensor_tensor(v_all[:, ds(2 * s, 2), :], pv[:, :, 0:P],
                                     bv_b[:, 0:P].unsqueeze(1).to_broadcast([P, 2, P]), ALU.add)
                    ve.tensor_tensor(v_all[:, ds(2 * NSEG + s, 1), :].rearrange("p u f -> p (u f)"), pv[:, 1, P:D],
                                     bv_b[:, P:D], ALU.add).then_inc(v_ev, 1)
                    ve.wait_ge(ge_ev, s + 1)
                    ve.tensor_scalar(gT[:, g0], gT[:, g0], 1.0, None, ALU.add)
                    ve.tensor_scalar(gT[:, g1], gT[:, g1], 1.0, None, ALU.add).then_inc(gate_rdy, 1)
                    ve.wait_ge(gate_rdy, s + 1)
                    alone(ve)
                    ve.reciprocal(gT[:, g0], gT[:, g0])
                    ve.reciprocal(gT[:, g1], gT[:, g1])
            loop_end(NSEG // 2)

            def maxima(g, hp):
                for qb in range(2):
                    ve.wait_ge(s_ps, 2 * g + (qb + 9))
                    ve.tensor_reduce(nmax[hp % 2][:, qb, :], view(bank[2 * (hp % 2) + qb], 2, SEG), X, ALU.max,
                                     negate=True).then_inc(m_rdy, 1)

            def evacuate(g, hp):
                ve.wait_ge(t_ps, 2 * g + 5)
                ve.wait_ge(pv_ps, g + 1)
                ve.tensor_copy(pT[hp % 2][0][:, :, :], view(bank[4], 2, SEG)).then_inc(pt_ev[0], 1)

            def attend(i, last_units=False):
                for c in range(2 * PAIRS):
                    g = 8 * i + c
                    h = c // PAIRS
                    u = 2 * i + h
                    if not (last_units and c + 2 >= 2 * PAIRS):
                        maxima(g + 2, (c + 2) % PAIRS)
                    if not (last_units and c + 1 >= 2 * PAIRS):
                        evacuate(g + 1, (c + 1) % PAIRS)
                    if c % PAIRS == PAIRS - 2:
                        ve.wait_ge(p_rdy, 2 * g + 8)
                        step(ve.reciprocal(rinv[h][:, :, :], rsum[h][:, :, :]))
                        ve.tensor_copy(rexp[h][:, :, :, :], rinv[h][:, :, :].unsqueeze(3).to_broadcast([P, 2, GH, HDIM]))\
                            .then_inc(rexp_rdy, 1)
                    if c % PAIRS == PAIRS - 1:
                        ve.wait_ge(rts_rdy, u + 1)
                        ve.tensor_tensor(attn[:, ds(SEG * u, SEG)], bank[6][:, 0:SEG], rts[h][:, :],
                                         ALU.mult).then_inc(o_ev, 1)

            maxima(0, 0)
            maxima(1, 1)
            evacuate(0, 0)
            with ve.Fori(0, UNITS // 2 - 1) as i:
                loop_of(i, 2)
                attend(i)
            loop_end(UNITS // 2 - 1)
            attend(UNITS // 2 - 1, True)

            def high_up(m, r, fb):
                f0, sz = fb * P, FSZ[fb]
                for kd in range(KD):
                    last = ve.tensor_copy(gu(wh_gu, kd, f0, sz), gu(raw_gu[r], kd, f0, sz))
                last.then_inc(wh_rdy, 1)

            ve.wait_ge(ld_raw[0], 48)
            for fb in range(FB):
                high_up(0, 0, fb)
            ve.wait_ge(o_ev, UNITS)

            with ve.Fori(0, NSEG // 2) as i:
                loop_of(i, 10)
                for h in range(2):
                    s = 2 * i + h
                    ve.wait_ge(xo_ps, s + 1)
                    ve.tensor_tensor(ag[h][:, 0:SEG], attn[:, ds(SEG * s, SEG)], gT[:, ds(SEG * s, SEG)], ALU.mult)
                    ve.tensor_tensor(ag[h][:, SEG:SEG + P], attn[:, ds(T + P * s, P)], gT[:, ds(T + P * s, P)],
                                     ALU.mult).then_inc(ag_rdy, 1)
                for h in range(2):
                    s = 2 * i + h
                    rows = seg_rows(s)
                    step(ve.tensor_tensor(rows, rows, bo_b[:, :].unsqueeze(1).to_broadcast([P, 2, D]), ALU.add))
                    ve.wait_ge(xo_ps, s + 3)
                    ve.tensor_tensor(rows, rows, view(bank[h], 2, D), ALU.add).then_inc(x1_rdy, 1)
                    ve.wait_ge(x1_rdy, s + 1)
                    variance(rows, h, var2)
                for h in range(2):
                    s = 2 * i + h
                    ve.wait_ge(rstd2, s + 1)
                    ve.wait_ge(t2_ps, s + 1)
                    ve.wait_ge(xn2_st[h], 16 * i)
                    normalise(seg_rows(s), h, xn2_rdy)
                for h in range(2):
                    s = 2 * i + h
                    ve.wait_ge(t2_ps, s + 3)
                    ve.wait_ge(lg_ps, s + 1)
                    ve.wait_ge(x2l_rdy, 2 * i)
                    ve.tensor_copy(x2T[h][:, :, :], view(bank[2 + h], KD, SEG)).then_inc(t2_ev, 1)
                for h in range(2):
                    s = 2 * i + h
                    ve.wait_ge(lg_ps, s + 3)
                    ve.tensor_copy(logits[:, ds(2 * s, 2), :], view(bank[4 + h], 2, E)).then_inc(lg_ev, 1)
            loop_end(NSEG // 2)

            ve.wait_ge(lg_ev, NSEG)
            ve.wait_ge(consts, 2)
            by_e = desc[:, :].unsqueeze(1).to_broadcast([P, NT, E])

            def over_e(t):
                return t.unsqueeze(2).to_broadcast([P, NT, E])

            def top(c, src):
                step(ve.tensor_reduce(m1[:, c, :], src, X, ALU.max))
                step(ve.tensor_tensor(eq[:, :, :], src, over_e(m1[:, c, :]), ALU.is_equal))
                step(ve.tensor_tensor(eq[:, :, :], eq[:, :, :], by_e, ALU.mult))
                step(ve.tensor_reduce(fi[:, :], eq[:, :, :], X, ALU.max))
                step(ve.tensor_tensor(sel[:, c, :, :], by_e, over_e(fi[:, :]), ALU.is_equal))

            top(0, logits[:, :, :])
            step(ve.scalar_tensor_tensor(out=l2[:, :, :], in0=sel[:, 0, :, :], scalar=-BIG, in1=logits[:, :, :],
                                         op0=ALU.mult, op1=ALU.add))
            top(1, l2[:, :, :])
            ve.tensor_tensor(wexp[:, 0, :], m1[:, 1, :], m1[:, 0, :], ALU.subtract).then_inc(dif_rdy, 1)
            ve.tensor_tensor(member[:, :, :], sel[:, 0, :, :], sel[:, 1, :, :], ALU.add).then_inc(m_in, 1)
            ve.wait_ge(ex_rdy, 1)
            step(ve.tensor_scalar(wexp[:, 2, :], wexp[:, 1, :], 1.0, None, ALU.add))
            step(ve.reciprocal(wts[:, 0, :], wexp[:, 2, :]))
            step(ve.tensor_tensor(wts[:, 1, :], wts[:, 0, :], wexp[:, 1, :], ALU.mult))
            ve.wait_ge(pre_ps, 1)
            step(ve.tensor_copy(scan[0][:, :, :], view(bank[7], 2, NT, E)[:, 1, :, :]))
            step(ve.tensor_copy(pos[:, :, :], view(bank[7], 2, NT, E)[:, 0, :, :]))
            step(ve.tensor_tensor(pos[:, :, :], pos[:, :, :], scan[0][:, :, :], ALU.subtract))
            r, d = 0, 1
            while d < NT:
                step(ve.tensor_copy(scan[1 - r][:, 0:d, :], scan[r][:, 0:d, :]))
                step(ve.tensor_tensor(scan[1 - r][:, d:NT, :], scan[r][:, d:NT, :], scan[r][:, 0:NT - d, :], ALU.add))
                r, d = 1 - r, 2 * d
            step(ve.tensor_tensor(pos[:, :, :], pos[:, :, :], scan[r][:, :, :], ALU.add))
            step(ve.tensor_tensor(ntile[:, :, :], scan[r][:, NT - 1, :].unsqueeze(2).to_broadcast([P, E, T // SEG]),
                                  k256[:, :].unsqueeze(1).to_broadcast([P, E, T // SEG]), ALU.is_gt))
            step(ve.tensor_reduce(tiles[:, :], ntile[:, :, :], X, ALU.add))
            step(ve.tensor_copy(tend[0][:, :], tiles[:, :]))
            r, d = 0, 1
            while d < E:
                step(ve.tensor_copy(tend[1 - r][:, 0:d], tend[r][:, 0:d]))
                step(ve.tensor_tensor(tend[1 - r][:, d:E], tend[r][:, d:E], tend[r][:, 0:E - d], ALU.add))
                r, d = 1 - r, 2 * d
            step(ve.tensor_tensor(jobe[:, :, :], tend[r][0:1, :].unsqueeze(1).to_broadcast([1, JOBS + 1, E]),
                                  jcol[:, :].unsqueeze(2).to_broadcast([1, JOBS + 1, E]), ALU.is_le))
            step(ve.tensor_reduce(jobf[:, :], jobe[:, :, :], X, ALU.add))
            step(ve.tensor_scalar(jobf[:, :], jobf[:, :], float(E - 1), None, ALU.min))
            ve.tensor_copy(jobi[:, :], jobf[:, :]).then_inc(jobs_rdy, 1)
            step(ve.tensor_tensor(tend[1 - r][:, :], tend[r][:, :], tiles[:, :], ALU.subtract))
            step(ve.tensor_scalar(tend[1 - r][:, :], tend[1 - r][:, :], float(SEG), None, ALU.mult))
            step(ve.tensor_tensor(pos[:, :, :], pos[:, :, :], tend[1 - r][:, :].unsqueeze(1).to_broadcast([P, NT, E]),
                                  ALU.add))
            for c in range(TOPK):
                step(ve.tensor_tensor(eq[:, :, :], sel[:, c, :, :], pos[:, :, :], ALU.mult))
                step(ve.tensor_reduce(poss[:, c, :], eq[:, :, :], X, ALU.add))
            step(ve.tensor_copy(posi[:, 0, :, :], poss[:, :, :]))
            step(ve.tensor_scalar(posi[:, 1, :, :], posi[:, 0, :, :], P - 1, None, ALU.bitwise_and))
            step(ve.tensor_scalar(posi[:, 2, :, :], posi[:, 0, :, :], P.bit_length() - 1, None, ALU.logical_shift_right))
            step(ve.tensor_copy(posf[:, :, :, :], posi[:, 1:3, :, :]))
            step(ve.memset(val[0][:, :, :], 0.0))
            ve.sem_inc(pre_ev, 1)

            row_of, col_of = [posf[:, n, :, :].rearrange("p c t -> p (c t)") for n in range(2)]
            tok_of = rowid[:, :, :].rearrange("p c t -> p (c t)")
            wt_of = wts[:, :, :].rearrange("p c t -> p (c t)")

            def one_hot(s, c):
                k = ds(4 * s + c, 1)
                ve.wait_ge(hot_ps, 4 * s + (c + 2))
                ve.tensor_scalar(hot[c % 2][:, :], iota[:, :], row_of[:, k], None, ALU.is_equal)
                ve.tensor_scalar(val[c % 2][:, 0, :], iota[:, 0:COLS], col_of[:, k], tok_of[:, k],
                                 ALU.is_equal, ALU.mult)
                ve.tensor_scalar(val[c % 2][:, 1, :], iota[:, 0:COLS], col_of[:, k], wt_of[:, k],
                                 ALU.is_equal, ALU.mult).then_inc(hot_rdy, 1)

            def gate(m, fb):
                sz = FSZ[fb]
                ve.wait_ge(sg_rdy, FB * m + (fb + 3))
                ve.wait_ge(u_ps, FB * m + (fb + 1))
                ve.wait_ge(ah_rdy, FB * m + (fb + 1))
                ve.wait_ge(al_rdy, FB * m + (fb + 1))
                ve.tensor_tensor(act[fb % 2][0:sz, :], sg[fb % 2][0:sz, :], bank[2 + fb % 2][0:sz, 0:SEG],
                                 ALU.mult).then_inc(a_rdy, 1)

            def act_low(m, fb):
                sz = FSZ[fb]
                ve.wait_ge(ah_rdy, FB * m + (fb + 3))
                ve.tensor_tensor(act_l[0:sz, fb, :], act[fb % 2][0:sz, :], act_h[0:sz, fb, :].bitcast(F32),
                                 ALU.subtract).then_inc(al_rdy, 1)

            ve.wait_ge(hot_ps, 3)
            with ve.Fori(0, NSEG // 2) as i:
                for h in range(2):
                    s = 2 * i + h
                    for fb in range(FB):
                        if fb < 4:
                            one_hot(s, fb)
                        gate(s, fb)
                        if fb:
                            act_low(s, fb - 1)
                    act_low(s, FB - 1)
                    ve.wait_ge(dn_ps, FB * s + 2 * FB)
                    ve.wait_ge(out_st[h], 16 * i)
                    ve.tensor_tensor(y_s[h][:, :, :], seg_rows(s), view(bank[4 + h], 2, D), ALU.add).then_inc(y_rdy, 1)

            ve.wait_ge(hot_ps, 3 + 4 * NSEG)
            step(ve.tensor_copy(tokf[:, 0:2, :], view(bank[7], 2, COLS)))
            step(ve.scalar_tensor_tensor(out=tokf[:, 2, :], in0=tokf[:, 0, :], scalar=0.0,
                                         in1=spare[:, :, :].rearrange("p j a -> p (j a)"),
                                         op0=ALU.is_equal, op1=ALU.mult))
            step(ve.tensor_tensor(tokf[:, 2, :], tokf[:, 2, :], tokf[:, 0, :], ALU.add))
            step(ve.tensor_scalar(tokf[:, 2, :], tokf[:, 2, :], -1.0, None, ALU.add))
            ve.tensor_copy(toki[:, :], tokf[:, 2, :]).then_inc(slots_rdy, 1)

            def token_low(j, h):
                ve.wait_ge(xjh_rdy, j + 1)
                ve.tensor_tensor(xjl[h][:, :, :], view(bank[6], KD, SEG), xjh[h][:, :, :].bitcast(F32),
                                 ALU.subtract).then_inc(xjl_rdy, 1)

            def expert_job(j, i, h, last=False):
                m = j + NSEG
                for fb in range(FB):
                    gate(m, fb)
                    if fb:
                        act_low(m, fb - 1)
                    if not last:
                        if fb == 0:
                            ve.wait_ge(ld_raw[1 - h], 48 * i + (48 * 3 if h else 48))
                        high_up(j + 2, 1 - h, fb)
                        if fb == 4:
                            token_low(j + 1, 1 - h)
                act_low(m, FB - 1)

            ve.wait_ge(ld_raw[0], 96)
            ve.wait_ge(u_ps, FB * NSEG)
            for fb in range(FB):
                high_up(1, 0, fb)
            token_low(0, 0)
            with ve.Fori(0, JOBS // 2) as i:
                for h in range(2):
                    expert_job(2 * i + h, i, h)
            expert_job(JOBS - 1, JOBS // 2, 0, True)


_INS = ["x", "ctx_1024"] + [f"L0_xattn_{w}{g}" for g in "qkvgo" for w in ("W", "b")] + \
       ["L0_ffn_gate_w", "L0_ffn_base_wgu", "L0_ffn_base_wd", "L0_ffn_exp_wgu", "L0_ffn_exp_wd"]


def kernel(**inputs):
    import numpy as np
    import concourse.bacc as bacc
    from concourse.bass_utils import run_bass_kernel_spmd

    nc = bacc.Bacc("TRN2", target_bir_lowering=False, num_devices=1)
    arrays, args = {}, []
    for name in _INS:
        a = np.ascontiguousarray(inputs[name])
        arrays[name] = a
        args.append(nc.dram_tensor(name, a.shape, mybir.dt.from_np(a.dtype), kind="ExternalInput").ap())
    args.append(nc.dram_tensor("out", (ROWS, D), F32, kind="ExternalOutput").ap())
    build(nc, *args)
    r = run_bass_kernel_spmd(nc, [arrays], core_ids=[0])
    return r.results[0]["out"][0:T].reshape(BATCH, NTOK, D)
```

```python
from contextlib import ExitStack

import concourse.bass as bass
from concourse import mybir

F32 = mybir.dt.float32
F32R = mybir.dt.float32r
I32 = mybir.dt.int32
ALU = mybir.AluOpType
ACT = mybir.ActivationFunctionType
X = mybir.AxisListType.X
ds = bass.ds

P = 128
BATCH, NTOK, D = 4, 512, 256
T = BATCH * NTOK
KD = D // P
HEADS, HDIM = 16, 16
GH = HEADS // 2
SEG = 256
NSEG = T // SEG
UNITS = NSEG + BATCH
PAIRS = GH // 2
LN_EPS = 1e-5
F = 704
FB = 6
FSZ = [P] * (F // P) + [F % P]
E = 8
TOPK = 2
JOBS = T * TOPK // SEG + E - 1
COLS = 2 * (JOBS + 1)
ROWS = T + SEG
BIG = 3.0e38


def build(nc, x, ctx_in, Wq, bq, Wk, bk, Wv, bv, Wg, bg, Wo, bo, gate_w, base_wgu, base_wd,
          exp_wgu, exp_wd, out):
    xn_tab = nc.dram_tensor("xn_tab", (ROWS, D), F32, kind="Internal").ap()
    x_seg = x.rearrange("b (s p a) d -> (b s) p (a d)", p=P, a=2)
    ctx_seg = ctx_in.rearrange("b (s p a) d -> (b s) p (a d)", p=P, a=2)
    out_seg = out[0:T, :].rearrange("(s p a) d -> s p (a d)", p=P, a=2)
    xn_seg = xn_tab[0:T, :].rearrange("(s p a) d -> s p (a d)", p=P, a=2)

    es = ExitStack()
    with es:
        def sb(name, shape, dt=F32, where=None):
            return (where or es).enter_context(nc.sbuf_tensor(name, shape, dt))

        def ps(name, shape=(P, 512), where=None):
            return (where or es).enter_context(nc.psum_tensor(name, list(shape), F32))

        starts = []

        def sem(name, start=0):
            made = es.enter_context(nc.semaphore(name))
            starts.append((made, start))
            return made

        def at(waited, count):
            return count + next(n for made, n in starts if made is waited)

        x_all = sb("x_all", [P, NSEG, 2 * D])
        ident = sb("ident", [P, P])
        headmask = sb("headmask", [P, GH])
        ones = sb("ones", [P, P])
        tri = sb("tri", [P, P])
        halves = sb("halves", [P, 2])
        wq_s = sb("wq_s", [P, KD, D])
        wk_s = sb("wk_s", [P, KD, D])
        wv_s = sb("wv_s", [P, KD, D])
        wg_s = sb("wg_s", [P, KD, D])
        wo_s = sb("wo_s", [P, KD, D])
        gw_s = sb("gw_s", [P, KD, E])
        bias_s = sb("bias_s", [P, 3, 2])
        bias_m = sb("bias_m", [P, 2])
        bv_b = sb("bv_b", [P, D])
        bo_b = sb("bo_b", [P, D])
        gT = sb("gT", [P, UNITS * SEG])
        attn = sb("attn", [P, UNITS * SEG])
        xn = [sb(f"xn{h}", [P, 2, D]) for h in range(2)]
        stats = [sb(f"stats{h}", [P, 2, 6]) for h in range(2)]
        mv = [sb(f"mv{h}", [P, 2, 2]) for h in range(2)]
        veps = [sb(f"veps{h}", [P, 2]) for h in range(2)]
        rstd = [sb(f"rstd{h}", [P, 2]) for h in range(2)]
        raw_gu0 = sb("raw_gu0", [P, KD, 2 * F])
        raw_d0 = sb("raw_d0", [P, FB, D])
        logits = sb("logits", [P, 2 * NSEG, E])

        early = ExitStack()
        ctx_s = [sb(f"ctx_s{h}", [P, 2 * D], where=early) for h in range(2)]
        xT = [sb(f"xT{h}", [P, KD, SEG], where=early) for h in range(2)]
        cT = [sb(f"cT{h}", [P, KD, SEG], where=early) for h in range(2)]
        qT = sb("qT", [P, UNITS * SEG], where=early)
        kT = sb("kT", [P, UNITS * SEG], where=early)
        v_all = sb("v_all", [P, UNITS * 2, P], where=early)
        km = [sb(f"km{r}", [P, 2, SEG], where=early) for r in range(PAIRS)]
        qs = [sb(f"qs{h}", [P, SEG], where=early) for h in range(2)]
        vpad = [sb(f"vpad{h}", [P, 2, GH, P], where=early) for h in range(2)]
        prob = [sb(f"prob{r}", [P, 2, 2, SEG], where=early) for r in range(2)]
        pT = [[sb(f"pT{r}{h}", [P, 2, SEG], where=early) for h in range(2)] for r in range(2)]
        nmax = [sb(f"nmax{r}", [P, 2, 2], where=early) for r in range(2)]
        rsum = [sb(f"rsum{h}", [P, 2, GH], where=early) for h in range(2)]
        rinv = [sb(f"rinv{h}", [P, 2, GH], where=early) for h in range(2)]
        rexp = [sb(f"rexp{h}", [P, 2, GH, HDIM], where=early) for h in range(2)]
        rts = [sb(f"rts{h}", [P, SEG], where=early) for h in range(2)]
        early.close()

        ag = [sb(f"ag{h}", [P, 3 * P]) for h in range(2)]
        x2T = [sb(f"x2T{h}", [P, KD, SEG]) for h in range(2)]
        shared = ExitStack()
        x2h = sb("x2h", [P, NSEG, KD, SEG], F32R, where=shared)
        x2l = sb("x2l", [P, NSEG, KD, SEG], F32R, where=shared)
        shared.close()
        raw_gu1 = sb("raw_gu1", [P, KD, 2 * F])
        raw_d1 = sb("raw_d1", [P, FB, D])
        raw_gu, raw_d = [raw_gu0, raw_gu1], [raw_d0, raw_d1]
        xg = [sb(f"xg{h}", [P, 2, D]) for h in range(2)]
        xjh = [sb(f"xjh{h}", [P, KD, SEG], F32R) for h in range(2)]
        xjl = [sb(f"xjl{h}", [P, KD, SEG], F32R) for h in range(2)]
        rest = 2 * NSEG * KD * SEG - (KD * 2 * F + FB * D) - 3 * 2 * KD * SEG
        sb("rest", [P, rest])
        wh_gu = sb("wh_gu", [P, KD, 2 * F], F32R)
        wl_gu = sb("wl_gu", [P, KD, 2 * F], F32R)
        wh_d = sb("wh_d", [P, FB, D], F32R)
        wl_d = sb("wl_d", [P, FB, D], F32R)
        sg = [sb(f"sg{r}", [P, SEG]) for r in range(2)]
        act = [sb(f"act{r}", [P, SEG]) for r in range(2)]
        act_h = sb("act_h", [P, FB, SEG], F32R)
        act_l = sb("act_l", [P, FB, SEG], F32R)
        y_s = [sb(f"y_s{h}", [P, 2, D]) for h in range(2)]
        NT = 2 * NSEG
        desc = sb("desc", [P, E])
        k256 = sb("k256", [P, T // SEG])
        jcol = sb("jcol", [1, JOBS + 1])
        rowid = sb("rowid", [P, TOPK, NT])
        spare = sb("spare", [P, JOBS + 1, 2])
        iota = sb("iota", [P, P])
        m1 = sb("m1", [P, TOPK, NT])
        eq = sb("eq", [P, NT, E])
        fi = sb("fi", [P, NT])
        sel = sb("sel", [P, TOPK, NT, E])
        l2 = sb("l2", [P, NT, E])
        wexp = sb("wexp", [P, 3, NT])
        wts = sb("wts", [P, TOPK, NT])
        member = sb("member", [P, NT, E])
        scan = [sb(f"scan{r}", [P, NT, E]) for r in range(2)]
        ntile = sb("ntile", [P, E, T // SEG])
        tiles = sb("tiles", [P, E])
        tend = [sb(f"tend{r}", [P, E]) for r in range(2)]
        pos = sb("pos", [P, NT, E])
        poss = sb("poss", [P, TOPK, NT])
        posi = sb("posi", [P, 3, TOPK, NT], I32)
        posf = sb("posf", [P, 2, TOPK, NT])
        jobe = sb("jobe", [1, JOBS + 1, E])
        jobf = sb("jobf", [1, JOBS + 1])
        jobi = sb("jobi", [1, JOBS + 1], I32)
        hot = [sb(f"hot{r}", [P, P]) for r in range(4)]
        val = [sb(f"val{r}", [P, 2, COLS]) for r in range(4)]
        tokf = sb("tokf", [P, 3, COLS])
        toki = sb("toki", [P, COLS], I32)
        slot_g = sb("slot_g", [P, 2], I32)
        slot_s = sb("slot_s", [P, 2], I32)
        zero = sb("zero", [P, 2, D])

        bank = [ps(f"bank{n}") for n in range(8)]

        ld_w = sem("ld_w")
        ld_x = [sem(f"ld_x{h}") for h in range(2)]
        ld_x2 = sem("ld_x2")
        ld_c = [sem(f"ld_c{h}") for h in range(2)]
        passed = sem("passed")
        consts = sem("consts")
        dv = sem("dv")
        gp = sem("gp")
        var_rdy = sem("var_rdy")
        rstd_rdy = sem("rstd_rdy")
        xn_rdy = sem("xn_rdy")
        xt_ps = sem("xt_ps", 2)
        ct_ps = sem("ct_ps", 2)
        xt_ev = sem("xt_ev", 1)
        ct_ev = sem("ct_ev", 1)
        q_ps, k_ps, g_ps1, v_ps = sem("q_ps"), sem("k_ps"), sem("g_ps1"), sem("v_ps", 2)
        q_ev, k_ev, ge_ev, v_ev = sem("q_ev", 1), sem("k_ev", 1), sem("ge_ev", 1), sem("v_ev", 1)
        bm_rdy = sem("bm_rdy")
        qs_rdy, vp_rdy, km_rdy = sem("qs_rdy"), sem("vp_rdy"), sem("km_rdy")
        s_ps = sem("s_ps", 9)
        m_rdy = sem("m_rdy")
        p_rdy = sem("p_rdy", 4)
        t_ps = sem("t_ps", 3)
        pt_ev = [sem(f"pt_ev{h}", 1) for h in range(2)]
        pv_ps = sem("pv_ps", 2)
        o_ev = sem("o_ev", 1)
        rt_ps = sem("rt_ps", 2)
        rexp_rdy, rts_rdy = sem("rexp_rdy"), sem("rts_rdy", 1)
        gated = sem("gated")
        xbo_rdy = sem("xbo_rdy")
        xo_ps = sem("xo_ps", 2)
        ag_rdy = sem("ag_rdy")
        x1_rdy = sem("x1_rdy", 2)
        var2, rstd2, xn2_rdy = sem("var2"), sem("rstd2"), sem("xn2_rdy")
        xn2_st = [sem(f"xn2_st{h}", 1) for h in range(2)]
        t2_ps = sem("t2_ps", 2)
        t2_ev = sem("t2_ev")
        lg_ps = sem("lg_ps", 2)
        x2h_rdy, x2l_rdy = sem("x2h_rdy", 2), sem("x2l_rdy", 2)
        ld_gu = [sem(f"ld_gu{h}") for h in range(2)]
        ld_d = [sem(f"ld_d{h}") for h in range(2)]
        wh_rdy, wl_rdy = sem("wh_rdy"), sem("wl_rdy")
        wd_rdy, wdl_rdy = sem("wd_rdy"), sem("wdl_rdy")
        g_ps, u_ps = sem("g_ps"), sem("u_ps")
        sg_rdy = sem("sg_rdy", 2)
        a_rdy = sem("a_rdy", 2)
        ah_rdy = sem("ah_rdy", 2)
        al_rdy = sem("al_rdy", 2)
        dn_ps = sem("dn_ps", 6)
        y_rdy = sem("y_rdy", 2)
        out_st = [sem(f"out_st{h}", 1) for h in range(2)]
        zero_st = sem("zero_st")
        m_in, dif_rdy, ex_rdy = sem("m_in"), sem("dif_rdy"), sem("ex_rdy")
        pre_ps, pre_ev = sem("pre_ps"), sem("pre_ev")
        hot_rdy, hot_ps = sem("hot_rdy"), sem("hot_ps", 3)
        jobs_rdy, slots_rdy = sem("jobs_rdy"), sem("slots_rdy")
        sg_cp, ss_cp = sem("sg_cp"), sem("ss_cp", 1)
        gath = [[sem(f"gath{h}{a}") for a in range(2)] for h in range(2)]
        tj_ps, xjh_rdy, xjl_rdy = sem("tj_ps", 1), sem("xjh_rdy"), sem("xjl_rdy", 1)
        scat = [sem(f"scat{a}") for a in range(2)]

        block = es.enter_context(nc.Block())

        def alone(eng):
            eng.sem_inc(passed, 1)

        def view(t, *shape):
            pat = {2: "p (a b) -> p a b", 3: "p (a b c) -> p a b c"}[len(shape)]
            n = 1
            for k in shape:
                n *= k
            return t[:, 0:n].rearrange(pat, **dict(zip("abc", shape)))

        def gu(t, fb):
            return t[:, :, :].rearrange("p k (t f) -> p k t f", t=2)[:, :, :, fb * P:fb * P + FSZ[fb]]

        WEIGHT_LOADS = 14
        HOT = 8
        HOT0 = NSEG - 1 - TOPK * 2 * NSEG // HOT

        def raw_loads(h, n, size=16):
            return size * n + (size if h == 0 else 0)

        @block.sync
        def _(sp):
            def load_ctx(s, h):
                sp.dma_start(ctx_s[h][:, :], ctx_seg[s]).then_inc(ld_c[h], 16)

            for h in range(2):
                sp.dma_start(x_all[:, h, :], x_seg[h]).then_inc(ld_x[h], 16)
                load_ctx(h, h)
            sp.wait_ge(ld_w, 16 * WEIGHT_LOADS)
            sp.dma_start(x_all[:, 2:NSEG, :], x_seg[2:NSEG].rearrange("s p d -> p s d")).then_inc(ld_x2, 16)
            for made, start in starts:
                if start:
                    sp.sem_inc(made, start)
            with sp.Fori(1, NSEG // 2) as i:
                for h in range(2):
                    sp.wait_ge(ld_c[h], 16 * i)
                    alone(sp)
                    sp.wait_ge(ct_ps, at(ct_ps, 2 * i + (h - 1)))
                    load_ctx(2 * i + h, h)

            def load_gu(h, w):
                sp.dma_start(raw_gu[h][:, :, :], w.rearrange("(k p) f -> p k f", p=P)).then_inc(ld_gu[h], 16)

            def load_d(h, w):
                sp.dma_start(raw_d[h][:, 0:FB - 1, :],
                             w[0:(FB - 1) * P, :].rearrange("(k p) n -> p k n", p=P)).then_inc(ld_d[h], 16)
                sp.dma_start(raw_d[h][0:FSZ[-1], FB - 1, :], w[(FB - 1) * P:F, :]).then_inc(ld_d[h], 16)

            load_gu(0, base_wgu)
            load_d(0, base_wd)
            with sp.Fori(0, NSEG // 2) as i:
                for h in range(2):
                    sp.wait_ge(xn2_rdy, 2 * i + (h + 1))
                    alone(sp)
                    sp.wait_ge(xn2_st[h], at(xn2_st[h], 16 * i))
                    sp.dma_start(xn_seg[2 * i + h], xn[h][:, :, :].rearrange("p a d -> p (a d)")).then_inc(xn2_st[h], 16)
            sp.wait_ge(consts, 2)
            sp.dma_start(xn_tab[T:ROWS, :].rearrange("(a p) d -> p a d", a=2), zero[:, :, :]).then_inc(zero_st, 16)
            sp.dma_start(out[T:ROWS, :].rearrange("(a p) d -> p a d", a=2), zero[:, :, :]).then_inc(zero_st, 16)
            def expert_of(j):
                return ds(sp.value_load(jobi[0:1, ds(j, 1)], min_val=0, max_val=E - 1), 1)

            def expert_gu(j, h):
                sp.wait_ge(wl_rdy, FB * j)
                alone(sp)
                load_gu(h, exp_wgu[expert_of(j), :, :].rearrange("u k f -> (u k) f"))

            def expert_d(j, h):
                sp.wait_ge(wdl_rdy, FB * j)
                alone(sp)
                load_d(h, exp_wd[expert_of(j), :, :].rearrange("u k n -> (u k) n"))

            def store(s, h, n):
                sp.wait_ge(y_rdy, at(y_rdy, s + 1))
                alone(sp)
                sp.wait_ge(out_st[h], at(out_st[h], 16 * n))
                sp.dma_start(out_seg[s], y_s[h][:, :, :].rearrange("p a d -> p (a d)")).then_inc(out_st[h], 16)

            store(0, 0, 0)
            store(1, 1, 0)
            sp.wait_ge(jobs_rdy, 1)
            sp.wait_ge(wl_rdy, FB)
            sp.wait_ge(wdl_rdy, FB)
            load_gu(0, exp_wgu[expert_of(0), :, :].rearrange("u k f -> (u k) f"))
            load_d(0, exp_wd[expert_of(0), :, :].rearrange("u k n -> (u k) n"))
            with sp.Fori(1, NSEG // 2 - 1) as i:
                for h in range(2):
                    store(2 * i + h, h, i)
            store(NSEG - 2, 0, NSEG // 2 - 1)
            sp.wait_ge(u_ps, FB * NSEG)
            expert_gu(1, 1)
            expert_d(1, 1)
            store(NSEG - 1, 1, NSEG // 2 - 1)
            expert_gu(2, 0)
            with sp.Fori(1, JOBS // 2) as i:
                expert_d(2 * i, 0)
                expert_gu(2 * i + 1, 1)
                expert_d(2 * i + 1, 1)
                expert_gu(2 * i + 2, 0)
            expert_d(JOBS - 1, 0)
            for h, n in enumerate((JOBS // 2 + 1, JOBS // 2)):
                sp.wait_ge(ld_gu[h], raw_loads(h, n))
                sp.wait_ge(ld_d[h], raw_loads(h, n, 32))
            for h in range(2):
                sp.wait_ge(xn2_st[h], at(xn2_st[h], 16 * (NSEG // 2)))
                sp.wait_ge(out_st[h], at(out_st[h], 16 * (NSEG // 2)))
            for a in range(2):
                sp.wait_ge(scat[a], at(scat[a], 16 * JOBS))
            sp.wait_ge(zero_st, 32)

        @block.gpsimd
        def _(pool):
            n = [0]

            def step(ins):
                n[0] += 1
                ins.then_inc(gp, 1)
                pool.wait_ge(gp, n[0])

            step(pool.memset(ident[:, :], 0.0))
            step(pool.affine_select(out=ident[:, :], in_=ident[:, :], compare_op=ALU.not_equal, fill=1.0,
                                    base=0, pattern=[[-1, P]], channel_multiplier=1))
            step(pool.memset(headmask[:, :], 1.0))
            step(pool.affine_select(out=headmask[:, :], in_=headmask[:, :], compare_op=ALU.is_ge, fill=0.0,
                                    base=0, pattern=[[-HDIM, GH]], channel_multiplier=1))
            step(pool.affine_select(out=headmask[:, :], in_=headmask[:, :], compare_op=ALU.is_ge, fill=0.0,
                                    base=HDIM - 1, pattern=[[HDIM, GH]], channel_multiplier=-1))
            step(pool.memset(halves[:, :], -0.5))
            step(pool.memset(ones[:, :], 1.0))
            step(pool.memset(tri[:, :], 1.0))
            step(pool.affine_select(out=tri[:, :], in_=tri[:, :], compare_op=ALU.is_gt, fill=0.0,
                                    base=0, pattern=[[1, P]], channel_multiplier=-1))
            for h in range(2):
                step(pool.memset(vpad[h][:, :, :, :], 0.0))
            pool.sem_inc(consts, 1)

            def rsqrt1(s, h):
                pool.wait_ge(var_rdy, s + 1)
                pool.tensor_tensor(rstd[h][:, :], veps[h][:, :], halves[:, :], ALU.pow).then_inc(rstd_rdy, 1)

            def operands(u, h):
                cols = ds(SEG * u, SEG)
                pool.wait_ge(s_ps, at(s_ps, 8 * u - 8))
                alone(pool)
                pool.tensor_copy(qs[h][:, :], qT[:, cols]).then_inc(qs_rdy, 1)
                for hp in range(PAIRS):
                    pool.wait_ge(s_ps, at(s_ps, 8 * u + (2 * hp - 6)))
                    alone(pool)
                    pool.tensor_tensor(km[hp][:, :, :],
                                       kT[:, cols].unsqueeze(1).to_broadcast([P, 2, SEG]),
                                       headmask[:, 2 * hp:2 * hp + 2].unsqueeze(2).to_broadcast([P, 2, SEG]),
                                       ALU.mult).then_inc(km_rdy, 1)
                pool.wait_ge(rt_ps, at(rt_ps, u - 1))
                alone(pool)
                for kb in range(2):
                    diag = vpad[h][:, kb, :, :].rearrange("p g c -> p (g c)")
                    last = pool.tensor_copy(
                        bass.AP(diag.tensor, diag.offset, [list(diag.ap[0]), [P + HDIM, GH], [1, HDIM]]),
                        v_all[:, ds(2 * u + kb, 1), :].rearrange("p u (g c) -> p (u g) c", g=GH))
                last.then_inc(vp_rdy, 1)

            for h in range(2):
                rsqrt1(h, h)
            with pool.Fori(0, NSEG // 2 - 1) as i:
                for h in range(2):
                    rsqrt1(2 * i + (h + 2), h)
            pool.wait_ge(q_ev, at(q_ev, 1))
            pool.wait_ge(k_ev, at(k_ev, 1))
            pool.wait_ge(v_ev, at(v_ev, 1))
            operands(0, 0)
            pool.wait_ge(q_ev, at(q_ev, NSEG))
            pool.wait_ge(k_ev, at(k_ev, NSEG))
            pool.wait_ge(v_ev, at(v_ev, NSEG))
            operands(1, 1)
            with pool.Fori(1, UNITS // 2) as i:
                for h in range(2):
                    operands(2 * i + h, h)

            pool.tensor_tensor(x_all[:, :, :].rearrange("p s (a d) -> p (s a) d", a=2),
                               x_all[:, :, :].rearrange("p s (a d) -> p (s a) d", a=2),
                               bo_b[:, :].unsqueeze(1).to_broadcast([P, 2 * NSEG, D]), ALU.add).then_inc(xbo_rdy, 1)

            pool.wait_ge(o_ev, at(o_ev, UNITS))
            def rsqrt2(s, h):
                pool.wait_ge(var2, s + 1)
                pool.tensor_tensor(rstd[h][:, :], veps[h][:, :], halves[:, :], ALU.pow).then_inc(rstd2, 1)

            def token_low2(s, h):
                pool.wait_ge(x2h_rdy, at(x2h_rdy, s + 1))
                alone(pool)
                pool.tensor_tensor(x2l[:, ds(s, 1), :, :].rearrange("p u k t -> p (u k) t"), x2T[h][:, :, :],
                                   x2h[:, ds(s, 1), :, :].rearrange("p u k t -> p (u k) t").bitcast(F32),
                                   ALU.subtract).then_inc(x2l_rdy, 1)

            def low_down(m, r, blocks=range(FB)):
                for fb in blocks:
                    sz = FSZ[fb]
                    pool.wait_ge(wd_rdy, FB * m + (fb + 1))
                    pool.tensor_tensor(wl_d[0:sz, fb, :], raw_d[r][0:sz, fb, :],
                                       wh_d[0:sz, fb, :].bitcast(F32), ALU.subtract).then_inc(wdl_rdy, 1)

            for h in range(2):
                rsqrt2(h, h)
            low_down(0, 0)
            with pool.Fori(0, NSEG // 2 - 1) as i:
                for h in range(2):
                    token_low2(2 * i + h, h)
                    rsqrt2(2 * i + (h + 2), h)
            for h in range(2):
                token_low2(NSEG - 2 + h, h)

            step(pool.memset(zero[:, :, :], 0.0))
            step(pool.iota(desc[:, :], [[-1, E]], base=E, channel_multiplier=0, allow_small_or_imprecise_dtypes=True))
            step(pool.iota(k256[:, :], [[SEG, T // SEG]], base=0, channel_multiplier=0, allow_small_or_imprecise_dtypes=True))
            step(pool.iota(jcol[:, :], [[1, JOBS + 1]], base=0, channel_multiplier=0, allow_small_or_imprecise_dtypes=True))
            step(pool.iota(rowid[:, :, :].rearrange("p c (s a) -> p c s a", a=2), [[0, TOPK], [SEG, NSEG], [1, 2]], base=1, channel_multiplier=2, allow_small_or_imprecise_dtypes=True))
            step(pool.iota(spare[:, :, :], [[0, JOBS + 1], [P, 2]], base=T + 1, channel_multiplier=1, allow_small_or_imprecise_dtypes=True))
            step(pool.iota(iota[:, :], [[1, P]], base=0, channel_multiplier=0, allow_small_or_imprecise_dtypes=True))
            pool.sem_inc(consts, 1)

            pool.wait_ge(slots_rdy, 1)
            pool.wait_ge(zero_st, 32)
            for h in range(2):
                pool.wait_ge(xn2_st[h], at(xn2_st[h], 16 * (NSEG // 2)))

            def gather(j, h):
                pool.wait_ge(tj_ps, at(tj_ps, j))
                alone(pool)
                pool.tensor_copy(slot_g[:, :], toki[:, ds(2 * j, 2)]).then_inc(sg_cp, 1)
                pool.wait_ge(sg_cp, j + 1)
                alone(pool)
                for a in range(2):
                    pool.indirect_dma_start(xg[h][:, a, :], None, xn_tab[:, :],
                                            bass.IndirectOffsetOnAxis(slot_g[:, a:a + 1], 0)).then_inc(gath[h][a], 16)

            def scatter(j, h, first=False):
                if not first:
                    for a in range(2):
                        pool.wait_ge(scat[a], 16 * j)
                    alone(pool)
                pool.tensor_copy(slot_s[:, :], toki[:, ds(2 * j, 2)]).then_inc(ss_cp, 1)
                pool.wait_ge(ss_cp, at(ss_cp, j + 1))
                pool.wait_ge(y_rdy, at(y_rdy, j + (NSEG + 1)))
                alone(pool)
                for a in range(2):
                    pool.indirect_dma_start(out[:, :], bass.IndirectOffsetOnAxis(slot_s[:, a:a + 1], 0),
                                            y_s[h][:, a, :], None, compute_op=ALU.add).then_inc(scat[a], 16)

            def expert_job(j, h, n, last=False, previous="job"):
                if not last:
                    for a in range(2):
                        pool.wait_ge(gath[h][a], 16 * n)
                    gather(j + 1, 1 - h)
                low_down(j + 1, h, range(3, FB))
                if previous:
                    scatter(j - 1, 1 - h, first=previous == "first")
                if not last:
                    low_down(j + 2, 1 - h, range(3))

            gather(0, 0)
            low_down(1, 0, range(3))
            expert_job(0, 0, 1, previous=None)
            for h in range(2):
                pool.wait_ge(out_st[h], at(out_st[h], 16 * (NSEG // 2)))
            expert_job(1, 1, 1, previous="first")
            expert_job(2, 0, 2)
            with pool.Fori(1, JOBS // 2 - 1) as i:
                expert_job(2 * i + 1, 1, i + 1)
                expert_job(2 * i + 2, 0, i + 2)
            expert_job(JOBS - 2, 1, JOBS // 2)
            expert_job(JOBS - 1, 0, JOBS // 2 + 1, last=True)
            scatter(JOBS - 1, 0)

        @block.scalar
        def _(sc):
            loads = [(w_s[:, :, :], w.rearrange("(k p) o -> p k o", p=P)) for w_s, w in
                     ((wq_s, Wq), (wk_s, Wk), (wg_s, Wg), (wv_s, Wv), (wo_s, Wo), (gw_s, gate_w))]
            for n, b in enumerate((bq, bk, bg)):
                for ob in range(2):
                    loads.append((bias_s[:, n, ob:ob + 1], b[ob * P:(ob + 1) * P].rearrange("(p u) -> p u", u=1)))
            loads += [(bv_b[:, :], bv.partition_broadcast(P)), (bo_b[:, :], bo.partition_broadcast(P))]
            for dst, src in loads:
                sc.dma_start(dst, src).then_inc(ld_w, 16)
            assert len(loads) == WEIGHT_LOADS
            sc.wait_ge(ld_w, 16 * WEIGHT_LOADS)
            sc.activation(bias_m[:, :], bias_s[:, 0, :], ACT.Copy, scale=0.25).then_inc(bm_rdy, 1)
            sc.wait_ge(bm_rdy, 1)

            def input_tile(s, h):
                sc.wait_ge(xt_ps, at(xt_ps, s + 1))
                sc.wait_ge(v_ps, at(v_ps, s - 1))
                sc.activation(xT[h][:, :, :], view(bank[0], KD, SEG), ACT.Copy).then_inc(xt_ev, 1)

            def projected(s):
                g0, g1 = ds(SEG * s, SEG), ds(T + P * s, P)
                sc.wait_ge(q_ps, s + 1)
                sc.activation(qT[:, g0], bank[2][:, 0:SEG], ACT.Identity, bias=bias_m[:, 0:1], scale=0.25)
                sc.activation(qT[:, g1], bank[2][:, SEG:SEG + P], ACT.Identity, bias=bias_m[:, 1:2],
                              scale=0.25).then_inc(q_ev, 1)
                sc.wait_ge(g_ps1, s + 1)
                sc.activation(gT[:, g0], bank[4][:, 0:SEG], ACT.Sigmoid, bias=bias_s[:, 2, 0:1])
                sc.activation(gT[:, g1], bank[4][:, SEG:SEG + P], ACT.Sigmoid,
                              bias=bias_s[:, 2, 1:2]).then_inc(ge_ev, 1)

            input_tile(0, 0)
            with sc.Fori(0, NSEG // 2 - 1) as i:
                for h in range(2):
                    input_tile(2 * i + (h + 1), 1 - h)
                    projected(2 * i + h)
            input_tile(NSEG - 1, 1)
            projected(NSEG - 2)
            projected(NSEG - 1)

            def exps(g, h, hp):
                r = g % 2 if isinstance(g, int) else hp % 2
                sc.wait_ge(t_ps, at(t_ps, 2 * g - 2))
                for qb in range(2):
                    sc.wait_ge(m_rdy, 2 * g + (qb + 1))
                    for k in range(2):
                        last = sc.activation(prob[r][:, qb, k, :], view(bank[2 * r + qb], 2, SEG)[:, k, :],
                                             ACT.Exp, bias=nmax[r][:, qb, k:k + 1],
                                             accum_out=rsum[h][:, qb, 2 * hp + k:2 * hp + k + 1])
                    last.then_inc(p_rdy, 1)

            def evacuate(g, hp):
                r = hp % 2
                sc.wait_ge(t_ps, at(t_ps, 2 * g + 2))
                sc.wait_ge(pv_ps, at(pv_ps, g - 1))
                sc.activation(pT[r][1][:, :, :], view(bank[5], 2, SEG), ACT.Copy).then_inc(pt_ev[1], 1)

            def attend(i, last_units=False):
                for c in range(2 * PAIRS):
                    g = 8 * i + c
                    if not (last_units and c + 2 >= 2 * PAIRS):
                        exps(g + 2, ((c + 2) // PAIRS) % 2, (c + 2) % PAIRS)
                    if not (last_units and c + 1 >= 2 * PAIRS):
                        evacuate(g + 1, (c + 1) % PAIRS)
                    if c % PAIRS == PAIRS - 1:
                        h = c // PAIRS
                        sc.wait_ge(rt_ps, at(rt_ps, 2 * i + (h + 1)))
                        sc.wait_ge(o_ev, at(o_ev, 2 * i + h))
                        sc.activation(rts[h][:, :], bank[7][:, 0:SEG], ACT.Copy).then_inc(rts_rdy, 1)

            exps(0, 0, 0)
            exps(1, 0, 1)
            evacuate(0, 0)
            with sc.Fori(0, UNITS // 2 - 1) as i:
                attend(i)
            attend(UNITS // 2 - 1, True)

            def high_down(m, r, fb):
                sz = FSZ[fb]
                sc.activation(wh_d[0:sz, fb, :], raw_d[r][0:sz, fb, :], ACT.Copy).then_inc(wd_rdy, 1)

            def attention_tile(s, h):
                sc.wait_ge(xo_ps, at(xo_ps, s - 1))
                sc.activation(ag[h][:, 0:SEG], attn[:, ds(SEG * s, SEG)], ACT.Copy)
                sc.activation(ag[h][:, SEG:SEG + P], attn[:, ds(P * s + T, P)], ACT.Copy).then_inc(ag_rdy, 1)

            def tokens2(s, h):
                sc.wait_ge(t2_ps, at(t2_ps, s + 1))
                sc.wait_ge(lg_ps, at(lg_ps, s - 1))
                sc.wait_ge(x2l_rdy, at(x2l_rdy, s - 1))
                sc.activation(x2T[h][:, :, :], view(bank[2 + h], KD, SEG), ACT.Copy).then_inc(t2_ev, 1)
                sc.activation(x2h[:, ds(s, 1), :, :].rearrange("p u k t -> p (u k) t"),
                              view(bank[2 + h], KD, SEG), ACT.Copy).then_inc(x2h_rdy, 1)

            sc.wait_ge(gated, UNITS)
            for h in range(2):
                attention_tile(h, h)
            sc.wait_ge(ld_d[0], 32)
            for fb in range(FB):
                high_down(0, 0, fb)
            with sc.Fori(0, NSEG // 2 - 1) as i:
                for h in range(2):
                    attention_tile(2 * i + (h + 2), h)
                    tokens2(2 * i + h, h)
            for h in range(2):
                tokens2(NSEG - 2 + h, h)

            def silu(m, fb):
                sz = FSZ[fb]
                sc.wait_ge(g_ps, FB * m + (fb + 1))
                sc.wait_ge(a_rdy, at(a_rdy, FB * m + (fb - 1)))
                sc.activation(sg[fb % 2][0:sz, :], bank[fb % 2][0:sz, 0:SEG], ACT.Silu).then_inc(sg_rdy, 1)

            def act_high(m, fb):
                sz = FSZ[fb]
                sc.wait_ge(a_rdy, at(a_rdy, FB * m + (fb + 1)))
                sc.wait_ge(dn_ps, at(dn_ps, FB * m + (fb - 5)))
                sc.activation(act_h[0:sz, fb, :], act[fb % 2][0:sz, :], ACT.Copy).then_inc(ah_rdy, 1)

            def token_high(j, h):
                sc.wait_ge(tj_ps, at(tj_ps, j + 1))
                sc.activation(xjh[h][:, :, :], view(bank[6], KD, SEG), ACT.Copy).then_inc(xjh_rdy, 1)

            def split_down(j, h, fb):
                sc.wait_ge(dn_ps, at(dn_ps, FB * j + (FB * (NSEG - 1) + fb + 1)))
                high_down(j + 1, h, fb)

            def weigh(j, h):
                sc.wait_ge(dn_ps, at(dn_ps, FB * j + FB * (NSEG + 1)))
                sc.wait_ge(ss_cp, at(ss_cp, j))
                for a in range(2):
                    ins = sc.activation(y_s[h][:, a, :], view(bank[4 + h], 2, D)[:, a, :], ACT.Copy,
                                        scale=tokf[:, 1, ds(2 * j + a, 1)])
                ins.then_inc(y_rdy, 1)

            def mlp(m, j=None, h=None, n=None, n_next=1, own=True, following=True, previous=True):
                for fb in range(FB):
                    silu(m, fb)
                    if fb:
                        act_high(m, fb - 1)
                    if j is None:
                        continue
                    if fb < 3 and own:
                        split_down(j, h, fb + 3)
                    if fb == 2 and previous:
                        weigh(j - 1, 1 - h)
                    if fb >= 3 and following:
                        if fb == 3:
                            sc.wait_ge(ld_d[1 - h], raw_loads(1 - h, n_next, 32))
                        split_down(j + 1, 1 - h, fb - 3)
                        if fb == 4:
                            token_high(j + 1, 1 - h)
                act_high(m, FB - 1)

            for s in range(2):
                mlp(s)
                if s == 0:
                    sc.wait_ge(dif_rdy, 1)
                    sc.activation(wexp[:, 1, :], wexp[:, 0, :], ACT.Exp).then_inc(ex_rdy, 1)
            with sc.Fori(2, NSEG - 1) as s:
                mlp(s)
            mlp(NSEG - 1, -1, 1, own=False, previous=False)
            mlp(NSEG, 0, 0, n_next=1, previous=False)
            for h in range(2):
                sc.wait_ge(out_st[h], at(out_st[h], 16 * (NSEG // 2)))
            with sc.Fori(0, JOBS // 2 - 1) as i:
                mlp(2 * i + (NSEG + 1), 2 * i + 1, 1, n_next=i + 2)
                mlp(2 * i + (NSEG + 2), 2 * i + 2, 0, n_next=i + 2)
            mlp(NSEG + JOBS - 2, JOBS - 2, 1, n_next=JOBS // 2 + 1)
            mlp(NSEG + JOBS - 1, JOBS - 1, 0, following=False)
            weigh(JOBS - 1, 0)

        @block.tensor
        def _(pe):
            pe.wait_ge(consts, 1)
            pe.wait_ge(ld_w, 16 * WEIGHT_LOADS)

            def transposes(dst, src):
                for kd in range(KD):
                    for a in range(2):
                        last = pe.transpose(dst[:, kd * SEG + a * P:kd * SEG + (a + 1) * P],
                                            src[:, a, kd * P:(kd + 1) * P], ident[:, :])
                return last

            def input_tiles(s, h, n):
                pe.wait_ge(xn_rdy, s + 1)
                pe.wait_ge(xt_ev, at(xt_ev, s))
                transposes(bank[0], xn[h]).then_inc(xt_ps, 1)
                pe.wait_ge(ld_c[h], 16 * n)
                pe.wait_ge(ct_ev, at(ct_ev, s))
                transposes(bank[1], ctx_s[h][:, :].rearrange("p (a d) -> p a d", a=2)).then_inc(ct_ps, 1)

            def project(s, bk, w, src, done, free):
                pe.wait_ge(free, at(free, s))
                for n, (c0, t0) in enumerate(((0, 0), (SEG, P))):
                    for kd in range(KD):
                        last = pe.matmul(bank[bk][:, c0:c0 + SEG - t0], w[:, kd, n * P:(n + 1) * P],
                                         src[:, kd, t0:SEG], start=(kd == 0), stop=(kd == KD - 1))
                last.then_inc(done, 1)

            def projections(s, h):
                pe.wait_ge(xt_ev, at(xt_ev, s + 1))
                project(s, 2, wq_s, xT[h], q_ps, q_ev)
                project(s, 4, wg_s, xT[h], g_ps1, ge_ev)
                pe.wait_ge(ct_ev, at(ct_ev, s + 1))
                project(s, 3, wk_s, cT[h], k_ps, k_ev)
                pe.wait_ge(v_ev, at(v_ev, s))
                for a in range(2):
                    n = P if a == 0 else D
                    for kd in range(KD):
                        last = pe.matmul(bank[5][:, a * D:a * D + n], cT[h][:, kd, a * P:(a + 1) * P],
                                         wv_s[:, kd, 0:n], start=(kd == 0), stop=(kd == KD - 1))
                last.then_inc(v_ps, 1)

            input_tiles(0, 0, 1)
            with pe.Fori(0, NSEG // 2 - 1) as i:
                for h in range(2):
                    input_tiles(2 * i + (h + 1), 1 - h, i + (h + 1))
                    projections(2 * i + h, h)
            input_tiles(NSEG - 1, 1, NSEG // 2)
            projections(NSEG - 2, 0)
            projections(NSEG - 1, 1)

            def scores(g, u, h, hp):
                if hp == 0:
                    pe.wait_ge(qs_rdy, u + 1)
                pe.wait_ge(km_rdy, g + 1)
                for qb in range(2):
                    pe.wait_ge(p_rdy, at(p_rdy, 2 * g + (qb - 3)))
                    pe.matmul(bank[2 * (hp % 2) + qb][:, :], qs[h][:, qb * P:(qb + 1) * P],
                              km[hp][:, :, :].rearrange("p k t -> p (k t)"), start=True, stop=True).then_inc(s_ps, 1)

            def transpose_probs(g, hp):
                pe.wait_ge(p_rdy, at(p_rdy, 2 * g + 2))
                for k in range(2):
                    pe.wait_ge(pt_ev[k], at(pt_ev[k], g))
                    for kb in range(2):
                        for qb in range(2):
                            last = pe.transpose(bank[4 + k][:, kb * SEG + qb * P:kb * SEG + (qb + 1) * P],
                                                prob[hp % 2][:, qb, k, kb * P:(kb + 1) * P], ident[:, :])
                    last.then_inc(t_ps, 1)

            def values(g, u, h, hp):
                if hp == 0:
                    pe.wait_ge(vp_rdy, u + 1)
                    pe.wait_ge(o_ev, at(o_ev, u))
                for k in range(2):
                    pe.wait_ge(pt_ev[k], at(pt_ev[k], g + 1))
                    for kb in range(2):
                        last = pe.matmul(bank[6][:, 0:SEG], vpad[h][:, kb, 2 * hp + k, :], pT[hp % 2][k][:, kb, :],
                                         start=(hp == 0 and k == 0 and kb == 0),
                                         stop=(hp == PAIRS - 1 and k == 1 and kb == 1))
                last.then_inc(pv_ps, 1)
                if hp == PAIRS - 1:
                    pe.wait_ge(rexp_rdy, u + 1)
                    pe.wait_ge(rts_rdy, at(rts_rdy, u))
                    for qb in range(2):
                        last = pe.transpose(bank[7][:, qb * P:(qb + 1) * P],
                                            rexp[h][:, qb, :, :].rearrange("p g c -> p (g c)"), ident[:, :])
                    last.then_inc(rt_ps, 1)

            def attend(i, last_units=False):
                for c in range(2 * PAIRS):
                    g = 8 * i + c
                    if not (last_units and c + 2 >= 2 * PAIRS):
                        n = c + 2
                        scores(g + 2, 2 * i + n // PAIRS, (n // PAIRS) % 2, n % PAIRS)
                    if not (last_units and c + 1 >= 2 * PAIRS):
                        transpose_probs(g + 1, (c + 1) % PAIRS)
                    values(g, 2 * i + c // PAIRS, c // PAIRS, c % PAIRS)

            for evacuated in (q_ev, k_ev, v_ev, ge_ev):
                pe.wait_ge(evacuated, at(evacuated, NSEG))
            scores(0, 0, 0, 0)
            scores(1, 0, 0, 1)
            transpose_probs(0, 0)
            with pe.Fori(0, UNITS // 2 - 1) as i:
                attend(i)
            attend(UNITS // 2 - 1, True)

            def out_project(s, h):
                pe.wait_ge(ag_rdy, s + 1)
                pe.wait_ge(x1_rdy, at(x1_rdy, s - 1))
                xo = view(bank[h], 2, D)
                even, odd, group1 = (ag[h][:, c * P:(c + 1) * P] for c in range(3))
                pe.matmul(xo[:, 0, :], even, wo_s[:, 0, :], start=True, stop=True)
                pe.matmul(xo[:, 1, :], odd, wo_s[:, 0, :], start=True, stop=False)
                pe.matmul(xo[:, 1, :], group1, wo_s[:, 1, :], start=False, stop=True).then_inc(xo_ps, 1)

            def router_logits(s, h, next_one=True):
                pe.wait_ge(xn2_rdy, s + 1)
                pe.wait_ge(x2h_rdy, at(x2h_rdy, s - 1))
                transposes(bank[2 + h], xn[h]).then_inc(t2_ps, 1)
                if next_one:
                    out_project(s + 2, h)
                pe.wait_ge(t2_ev, s + 1)
                alone(pe)
                for a in range(2):
                    for kd in range(KD):
                        last = pe.matmul(bank[7][:, ds(2 * E * s + a * E, E)], x2T[h][:, kd, a * P:(a + 1) * P],
                                         gw_s[:, kd, :], start=(kd == 0), stop=(kd == KD - 1))
                last.then_inc(lg_ps, 1)

            for h in range(2):
                out_project(h, h)
            with pe.Fori(0, NSEG // 2 - 1) as i:
                for h in range(2):
                    router_logits(2 * i + h, h)
            for h in range(2):
                router_logits(NSEG - 2 + h, h, next_one=False)

            def up(m, fb, high, low):
                sz = FSZ[fb]
                for n, (t, free, done) in enumerate(((0, sg_rdy, g_ps), (1, a_rdy, u_ps))):
                    pe.wait_ge(free, at(free, FB * m + (fb - 1)))
                    alone(pe)
                    o = bank[2 * n + fb % 2][0:sz, 0:SEG]
                    f0 = t * F + fb * P
                    for kd in range(KD):
                        pe.matmul(o, wh_gu[:, kd, f0:f0 + sz], high(kd), start=(kd == 0), stop=False)
                        pe.matmul(o, wh_gu[:, kd, f0:f0 + sz], low(kd), start=False, stop=False)
                        last = pe.matmul(o, wl_gu[:, kd, f0:f0 + sz], high(kd), start=False, stop=(kd == KD - 1))
                    last.then_inc(done, 1)

            def down(m, fb, h):
                sz = FSZ[fb]
                if fb == 0:
                    pe.wait_ge(y_rdy, at(y_rdy, m - 1))
                pe.wait_ge(ah_rdy, at(ah_rdy, FB * m + (fb + 1)))
                pe.wait_ge(al_rdy, at(al_rdy, FB * m + (fb + 1)))
                y = view(bank[4 + h], 2, D)
                for a in range(2):
                    t = slice(a * P, (a + 1) * P)
                    pe.matmul(y[:, a, :], act_h[0:sz, fb, t], wh_d[0:sz, fb, :], start=(fb == 0 and a == 0),
                              stop=False, skip_group_check=True)
                    pe.matmul(y[:, a, :], act_h[0:sz, fb, t], wl_d[0:sz, fb, :], start=False, stop=False,
                              skip_group_check=True)
                    last = pe.matmul(y[:, a, :], act_l[0:sz, fb, t], wh_d[0:sz, fb, :], start=False,
                                     stop=(fb == FB - 1 and a == 1), skip_group_check=True)
                last.then_inc(dn_ps, 1)

            def mlp(m, h, high, low, previous=True, each=None, job=None):
                for fb in range(FB):
                    if job is not None:
                        pe.wait_ge(wl_rdy, FB * job + (FB + fb + 1))
                    up(m, fb, high, low)
                    if fb >= 2:
                        if job is not None:
                            pe.wait_ge(wdl_rdy, FB * job + (FB + fb - 1))
                        down(m, fb - 2, h)
                    elif previous:
                        if job is not None and previous != "shared":
                            pe.wait_ge(wdl_rdy, FB * job + (fb + 5))
                        down(m - 1, fb + FB - 2, 1 - h)
                    if each:
                        each(fb)

            def shared(s, h, previous=True, each=None, job=None):
                def tokens(t):
                    return lambda kd: t[:, ds(s, 1), kd, :].rearrange("p u t -> p (u t)")

                pe.wait_ge(x2l_rdy, at(x2l_rdy, s + 1))
                mlp(s, h, tokens(x2h), tokens(x2l), previous, each, job)

            def count_tokens(fb):
                if fb == 0:
                    pe.wait_ge(m_in, 1)
                    mem = member[:, :, :].rearrange("p t e -> p (t e)")
                    pe.matmul(bank[7][:, 0:P], tri[:, :], mem, start=True, stop=True)
                    pe.matmul(bank[7][:, P:2 * P], ones[:, :], mem, start=True, stop=True).then_inc(pre_ps, 1)

            slots = bank[7][:, 0:2 * COLS]

            def place_tokens(s):
                def each(fb):
                    for c in range(2 * fb - 2, 2 * fb) if 0 < fb <= HOT // 2 else ():
                        pe.wait_ge(hot_rdy, HOT * s + (c + 1 - HOT0 * HOT))
                        pe.matmul(slots, hot[c % 4][:, :], val[c % 4][:, :, :].rearrange("p v c -> p (v c)"),
                                  start=False, stop=False, skip_group_check=True).then_inc(hot_ps, 1)
                return each

            def job_tokens(j, h, n):
                for a in range(2):
                    pe.wait_ge(gath[h][a], 16 * n)
                pe.wait_ge(xjl_rdy, at(xjl_rdy, j))
                transposes(bank[6], xg[h]).then_inc(tj_ps, 1)

            def expert_job(j, h, n_next=None, previous=True):
                def each(fb):
                    if fb == 3 and n_next is not None:
                        job_tokens(j + 1, 1 - h, n_next)

                pe.wait_ge(xjl_rdy, at(xjl_rdy, j + 1))
                mlp(j + NSEG, h, lambda kd: xjh[h][:, kd, :], lambda kd: xjl[h][:, kd, :], previous, each, j)

            pe.wait_ge(x1_rdy, at(x1_rdy, NSEG))
            pe.wait_ge(x2h_rdy, at(x2h_rdy, NSEG))
            shared(0, 0, previous=False, job=-1)
            pe.wait_ge(wdl_rdy, FB)
            shared(1, 1, each=count_tokens)
            shared(2, 0)
            pe.wait_ge(pre_ev, 1)
            pe.matmul(slots, ones[:, :], val[0][:, :, :].rearrange("p v c -> p (v c)"), start=True, stop=False,
                      skip_group_check=True).then_inc(hot_ps, 1)
            with pe.Fori(0, (NSEG - 1 - HOT0) // 2) as i:
                for h in range(2):
                    shared(2 * i + (HOT0 + h), (HOT0 + h) % 2, each=place_tokens(2 * i + (HOT0 + h)))
            shared(NSEG - 1, 1, each=lambda fb: job_tokens(0, 0, 1) if fb == 3 else None)
            expert_job(0, 0, 1, previous="shared")
            with pe.Fori(0, JOBS // 2 - 1) as i:
                expert_job(2 * i + 1, 1, i + 2)
                expert_job(2 * i + 2, 0, i + 2)
            expert_job(JOBS - 2, 1, JOBS // 2 + 1)
            expert_job(JOBS - 1, 0)
            for fb in (FB - 2, FB - 1):
                pe.wait_ge(wdl_rdy, FB * JOBS + (fb + 1))
                down(NSEG + JOBS - 1, fb, 0)

        @block.vector
        def _(ve):
            chain = dict(n=0, i=0, per=0)

            def mark(ins):
                chain["n"] += 1
                ins.then_inc(dv, 1)

            def chained():
                ve.wait_ge(dv, chain["i"] * chain["per"] + chain["n"])

            def step(ins):
                mark(ins)
                chained()

            def loop_of(i, per):
                chain.update(i=i, per=per, at=chain["n"])

            def loop_end(count):
                assert chain["n"] - chain["at"] == chain["per"], (chain, "per")
                chain["n"] += chain["per"] * (count - 1)
                chain.update(i=0, per=0)


            def variance(src, h, done):
                alone(ve)
                for a in range(2):
                    mark(ve.bn_stats(stats[h][:, a, :], src[:, a, :]))
                chained()
                alone(ve)
                for a in range(2):
                    mark(ve.bn_aggr(mv[h][:, a, :], stats[h][:, a, :]))
                chained()
                ve.tensor_scalar(veps[h][:, :], mv[h][:, :, 1], LN_EPS, None, ALU.add).then_inc(done, 1)

            def normalise(src, h, done):
                for a in range(2):
                    last = ve.tensor_scalar(xn[h][:, a, :], src[:, a, :], mv[h][:, a, 0:1], rstd[h][:, a:a + 1],
                                            ALU.subtract, ALU.mult)
                last.then_inc(done, 1)

            def seg_rows(s):
                return x_all[:, ds(s, 1), :].rearrange("p u (a d) -> p (u a) d", a=2)

            def context_tile(s, h):
                ve.wait_ge(ct_ps, at(ct_ps, s + 1))
                ve.wait_ge(v_ps, at(v_ps, s - 1))
                ve.tensor_copy(cT[h][:, :, :], view(bank[1], KD, SEG)).then_inc(ct_ev, 1)

            def norm(s, h):
                ve.wait_ge(rstd_rdy, s + 1)
                ve.wait_ge(xt_ps, at(xt_ps, s - 1))
                normalise(seg_rows(s), h, xn_rdy)

            def keys(s):
                ve.wait_ge(k_ps, s + 1)
                ve.tensor_scalar(kT[:, ds(SEG * s, SEG)], bank[3][:, 0:SEG], bias_s[:, 1, 0:1], None, ALU.add)
                ve.tensor_scalar(kT[:, ds(T + P * s, P)], bank[3][:, SEG:SEG + P], bias_s[:, 1, 1:2], None,
                                 ALU.add).then_inc(k_ev, 1)

            def values_of(s):
                ve.wait_ge(v_ps, at(v_ps, s + 1))
                pv = view(bank[5], 2, D)
                ve.tensor_tensor(v_all[:, ds(2 * s, 2), :], pv[:, :, 0:P],
                                 bv_b[:, 0:P].unsqueeze(1).to_broadcast([P, 2, P]), ALU.add)
                ve.tensor_tensor(v_all[:, ds(2 * NSEG + s, 1), :].rearrange("p u f -> p (u f)"), pv[:, 1, P:D],
                                 bv_b[:, P:D], ALU.add).then_inc(v_ev, 1)

            def project_steps(s, h, ahead=2):
                if ahead >= 1:
                    context_tile(s + 1, 1 - h)
                if ahead >= 2:
                    variance(seg_rows(s + 2), h, var_rdy)
                keys(s)
                if ahead >= 2:
                    norm(s + 2, h)
                values_of(s)

            for h in range(2):
                ve.wait_ge(ld_x[h], 16)
                variance(seg_rows(h), h, var_rdy)
            for h in range(2):
                norm(h, h)
            context_tile(0, 0)
            ve.wait_ge(ld_x2, 16)
            with ve.Fori(0, NSEG // 2 - 1) as i:
                loop_of(i, 8)
                for h in range(2):
                    project_steps(2 * i + h, h)
            loop_end(NSEG // 2 - 1)
            project_steps(NSEG - 2, 0, ahead=1)
            project_steps(NSEG - 1, 1, ahead=0)

            def maxima(g, hp):
                for qb in range(2):
                    ve.wait_ge(s_ps, at(s_ps, 2 * g + (qb + 1)))
                    ve.tensor_reduce(nmax[hp % 2][:, qb, :], view(bank[2 * (hp % 2) + qb], 2, SEG), X, ALU.max,
                                     negate=True).then_inc(m_rdy, 1)

            def evacuate(g, hp):
                ve.wait_ge(t_ps, at(t_ps, 2 * g + 1))
                ve.wait_ge(pv_ps, at(pv_ps, g - 1))
                ve.tensor_copy(pT[hp % 2][0][:, :, :], view(bank[4], 2, SEG)).then_inc(pt_ev[0], 1)

            def attend(i, last_units=False):
                for c in range(2 * PAIRS):
                    g = 8 * i + c
                    h = c // PAIRS
                    u = 2 * i + h
                    if not (last_units and c + 2 >= 2 * PAIRS):
                        maxima(g + 2, (c + 2) % PAIRS)
                    if not (last_units and c + 1 >= 2 * PAIRS):
                        evacuate(g + 1, (c + 1) % PAIRS)
                    if c % PAIRS == PAIRS - 2:
                        ve.wait_ge(p_rdy, at(p_rdy, 2 * g + 4))
                        step(ve.reciprocal(rinv[h][:, :, :], rsum[h][:, :, :]))
                        ve.tensor_copy(rexp[h][:, :, :, :], rinv[h][:, :, :].unsqueeze(3).to_broadcast([P, 2, GH, HDIM]))\
                            .then_inc(rexp_rdy, 1)
                    if c % PAIRS == PAIRS - 1:
                        ve.wait_ge(rts_rdy, at(rts_rdy, u + 1))
                        ve.tensor_tensor(attn[:, ds(SEG * u, SEG)], bank[6][:, 0:SEG], rts[h][:, :],
                                         ALU.mult).then_inc(o_ev, 1)
                        ve.wait_ge(o_ev, at(o_ev, u + 1))
                        ve.tensor_tensor(attn[:, ds(SEG * u, SEG)], attn[:, ds(SEG * u, SEG)], gT[:, ds(SEG * u, SEG)],
                                         ALU.mult).then_inc(gated, 1)

            ve.wait_ge(ge_ev, at(ge_ev, NSEG))
            maxima(0, 0)
            maxima(1, 1)
            evacuate(0, 0)
            with ve.Fori(0, UNITS // 2 - 1) as i:
                loop_of(i, 2)
                attend(i)
            loop_end(UNITS // 2 - 1)
            attend(UNITS // 2 - 1, True)

            def high_up(m, r, fb):
                ve.tensor_copy(gu(wh_gu, fb), gu(raw_gu[r], fb)).then_inc(wh_rdy, 1)

            def low_up(m, r, fb):
                ve.wait_ge(wh_rdy, FB * m + (fb + 1))
                ve.tensor_tensor(gu(wl_gu, fb), gu(raw_gu[r], fb), gu(wh_gu, fb).bitcast(F32),
                                 ALU.subtract).then_inc(wl_rdy, 1)

            ve.wait_ge(o_ev, at(o_ev, UNITS))

            def residual1(s, h):
                ve.wait_ge(xo_ps, at(xo_ps, s + 1))
                ve.tensor_tensor(seg_rows(s), seg_rows(s), view(bank[h], 2, D), ALU.add).then_inc(x1_rdy, 1)
                ve.wait_ge(x1_rdy, at(x1_rdy, s + 1))
                variance(seg_rows(s), h, var2)

            def norm2(s, h, n):
                ve.wait_ge(rstd2, s + 1)
                ve.wait_ge(t2_ps, at(t2_ps, s - 1))
                ve.wait_ge(xn2_st[h], at(xn2_st[h], 16 * n))
                normalise(seg_rows(s), h, xn2_rdy)

            ve.wait_ge(xbo_rdy, 1)
            residual1(0, 0)
            with ve.Fori(0, NSEG // 2 - 1) as i:
                loop_of(i, 8)
                for h in range(2):
                    norm2(2 * i + h, h, i)
                    residual1(2 * i + (h + 1), 1 - h)
            loop_end(NSEG // 2 - 1)
            norm2(NSEG - 2, 0, NSEG // 2 - 1)
            residual1(NSEG - 1, 1)
            norm2(NSEG - 1, 1, NSEG // 2 - 1)

            ve.wait_ge(ld_gu[0], 16)
            for fb in range(FB):
                high_up(0, 0, fb)
                if fb:
                    low_up(0, 0, fb - 1)
            low_up(0, 0, FB - 1)

            by_e = desc[:, :].unsqueeze(1).to_broadcast([P, NT, E])

            def over_e(t):
                return t.unsqueeze(2).to_broadcast([P, NT, E])

            def top(c, src):
                step(ve.tensor_reduce(m1[:, c, :], src, X, ALU.max))
                step(ve.tensor_tensor(eq[:, :, :], src, over_e(m1[:, c, :]), ALU.is_equal))
                step(ve.tensor_tensor(eq[:, :, :], eq[:, :, :], by_e, ALU.mult))
                step(ve.tensor_reduce(fi[:, :], eq[:, :, :], X, ALU.max))
                step(ve.tensor_tensor(sel[:, c, :, :], by_e, over_e(fi[:, :]), ALU.is_equal))

            def route_top():
                ve.wait_ge(lg_ps, at(lg_ps, NSEG))
                step(ve.tensor_copy(logits[:, :, :], view(bank[7], 2 * NSEG, E)))
                ve.wait_ge(consts, 2)
                top(0, logits[:, :, :])

            def route_second():
                step(ve.scalar_tensor_tensor(out=l2[:, :, :], in0=sel[:, 0, :, :], scalar=-BIG, in1=logits[:, :, :],
                                             op0=ALU.mult, op1=ALU.add))
                top(1, l2[:, :, :])
                ve.tensor_tensor(wexp[:, 0, :], m1[:, 1, :], m1[:, 0, :], ALU.subtract).then_inc(dif_rdy, 1)
                ve.tensor_tensor(member[:, :, :], sel[:, 0, :, :], sel[:, 1, :, :], ALU.add).then_inc(m_in, 1)

            def route_weights():
                ve.wait_ge(ex_rdy, 1)
                step(ve.tensor_scalar(wexp[:, 2, :], wexp[:, 1, :], 1.0, None, ALU.add))
                step(ve.reciprocal(wts[:, 0, :], wexp[:, 2, :]))
                step(ve.tensor_tensor(wts[:, 1, :], wts[:, 0, :], wexp[:, 1, :], ALU.mult))

            def route_counts():
                ve.wait_ge(pre_ps, 1)
                step(ve.tensor_copy(scan[0][:, :, :], view(bank[7], 2, NT, E)[:, 1, :, :]))
                step(ve.tensor_copy(pos[:, :, :], view(bank[7], 2, NT, E)[:, 0, :, :]))
                step(ve.tensor_tensor(pos[:, :, :], pos[:, :, :], scan[0][:, :, :], ALU.subtract))
                r, d = 0, 1
                while d < NT:
                    step(ve.tensor_copy(scan[1 - r][:, 0:d, :], scan[r][:, 0:d, :]))
                    step(ve.tensor_tensor(scan[1 - r][:, d:NT, :], scan[r][:, d:NT, :], scan[r][:, 0:NT - d, :], ALU.add))
                    r, d = 1 - r, 2 * d
                step(ve.tensor_tensor(pos[:, :, :], pos[:, :, :], scan[r][:, :, :], ALU.add))

            def route_jobs():
                step(ve.tensor_tensor(ntile[:, :, :], scan[(NT.bit_length() - 1) % 2][:, NT - 1, :].unsqueeze(2).to_broadcast([P, E, T // SEG]),
                                      k256[:, :].unsqueeze(1).to_broadcast([P, E, T // SEG]), ALU.is_gt))
                step(ve.tensor_reduce(tiles[:, :], ntile[:, :, :], X, ALU.add))
                step(ve.tensor_copy(tend[0][:, :], tiles[:, :]))
                r, d = 0, 1
                while d < E:
                    step(ve.tensor_copy(tend[1 - r][:, 0:d], tend[r][:, 0:d]))
                    step(ve.tensor_tensor(tend[1 - r][:, d:E], tend[r][:, d:E], tend[r][:, 0:E - d], ALU.add))
                    r, d = 1 - r, 2 * d
                step(ve.tensor_tensor(jobe[:, :, :], tend[r][0:1, :].unsqueeze(1).to_broadcast([1, JOBS + 1, E]),
                                      jcol[:, :].unsqueeze(2).to_broadcast([1, JOBS + 1, E]), ALU.is_le))
                step(ve.tensor_reduce(jobf[:, :], jobe[:, :, :], X, ALU.add))
                step(ve.tensor_scalar(jobf[:, :], jobf[:, :], float(E - 1), None, ALU.min))
                ve.tensor_copy(jobi[:, :], jobf[:, :]).then_inc(jobs_rdy, 1)

            def route_places():
                r = (E.bit_length() - 1) % 2
                step(ve.tensor_tensor(tend[1 - r][:, :], tend[r][:, :], tiles[:, :], ALU.subtract))
                step(ve.tensor_scalar(tend[1 - r][:, :], tend[1 - r][:, :], float(SEG), None, ALU.mult))
                step(ve.tensor_tensor(pos[:, :, :], pos[:, :, :], tend[1 - r][:, :].unsqueeze(1).to_broadcast([P, NT, E]),
                                      ALU.add))
                for c in range(TOPK):
                    step(ve.tensor_tensor(eq[:, :, :], sel[:, c, :, :], pos[:, :, :], ALU.mult))
                    step(ve.tensor_reduce(poss[:, c, :], eq[:, :, :], X, ALU.add))
                step(ve.tensor_copy(posi[:, 0, :, :], poss[:, :, :]))
                step(ve.tensor_scalar(posi[:, 1, :, :], posi[:, 0, :, :], P - 1, None, ALU.bitwise_and))
                step(ve.tensor_scalar(posi[:, 2, :, :], posi[:, 0, :, :], P.bit_length() - 1, None, ALU.logical_shift_right))
                step(ve.tensor_copy(posf[:, :, :, :], posi[:, 1:3, :, :]))
                step(ve.memset(val[0][:, :, :], 0.0))
                ve.sem_inc(pre_ev, 1)

            row_of, col_of = [posf[:, n, :, :].rearrange("p c t -> p (c t)") for n in range(2)]
            tok_of = rowid[:, :, :].rearrange("p c t -> p (c t)")
            wt_of = wts[:, :, :].rearrange("p c t -> p (c t)")

            def one_hot(s, c):
                k = ds(HOT * s + (c - HOT0 * HOT), 1)
                ve.wait_ge(hot_ps, at(hot_ps, HOT * s + (c - HOT0 * HOT - 2)))
                ve.tensor_scalar(hot[c % 4][:, :], iota[:, :], row_of[:, k], None, ALU.is_equal)
                ve.tensor_scalar(val[c % 4][:, 0, :], iota[:, 0:COLS], col_of[:, k], tok_of[:, k],
                                 ALU.is_equal, ALU.mult)
                ve.tensor_scalar(val[c % 4][:, 1, :], iota[:, 0:COLS], col_of[:, k], wt_of[:, k],
                                 ALU.is_equal, ALU.mult).then_inc(hot_rdy, 1)

            def gate(m, fb):
                sz = FSZ[fb]
                ve.wait_ge(sg_rdy, at(sg_rdy, FB * m + (fb + 1)))
                ve.wait_ge(u_ps, FB * m + (fb + 1))
                ve.wait_ge(ah_rdy, at(ah_rdy, FB * m + (fb - 1)))
                ve.wait_ge(al_rdy, at(al_rdy, FB * m + (fb - 1)))
                ve.tensor_tensor(act[fb % 2][0:sz, :], sg[fb % 2][0:sz, :], bank[2 + fb % 2][0:sz, 0:SEG],
                                 ALU.mult).then_inc(a_rdy, 1)

            def act_low(m, fb):
                sz = FSZ[fb]
                ve.wait_ge(ah_rdy, at(ah_rdy, FB * m + (fb + 1)))
                ve.tensor_tensor(act_l[0:sz, fb, :], act[fb % 2][0:sz, :], act_h[0:sz, fb, :].bitcast(F32),
                                 ALU.subtract).then_inc(al_rdy, 1)

            def slot_table():
                ve.wait_ge(hot_ps, at(hot_ps, TOPK * NT + 1))
                step(ve.tensor_copy(tokf[:, 0:2, :], view(bank[7], 2, COLS)))
                step(ve.scalar_tensor_tensor(out=tokf[:, 2, :], in0=tokf[:, 0, :], scalar=0.0,
                                             in1=spare[:, :, :].rearrange("p j a -> p (j a)"),
                                             op0=ALU.is_equal, op1=ALU.mult))
                step(ve.tensor_tensor(tokf[:, 2, :], tokf[:, 2, :], tokf[:, 0, :], ALU.add))
                step(ve.tensor_scalar(tokf[:, 2, :], tokf[:, 2, :], -1.0, None, ALU.add))
                ve.tensor_copy(toki[:, :], tokf[:, 2, :]).then_inc(slots_rdy, 1)

            def residual(s, h, n):
                ve.wait_ge(dn_ps, at(dn_ps, FB * s + FB))
                ve.wait_ge(out_st[h], at(out_st[h], 16 * n - 16))
                ve.tensor_tensor(y_s[h][:, :, :], seg_rows(s), view(bank[4 + h], 2, D), ALU.add).then_inc(y_rdy, 1)

            def token_low(j, h):
                ve.wait_ge(xjh_rdy, j + 1)
                ve.tensor_tensor(xjl[h][:, :, :], view(bank[6], KD, SEG), xjh[h][:, :, :].bitcast(F32),
                                 ALU.subtract).then_inc(xjl_rdy, 1)

            def mlp(m, each=lambda fb: None, job=None, h=None, n_next=None):
                for fb in range(FB):
                    gate(m, fb)
                    if fb:
                        act_low(m, fb - 1)
                    if n_next is not None:
                        if fb == 0:
                            ve.wait_ge(ld_gu[1 - h], raw_loads(1 - h, n_next))
                        high_up(job + 2, 1 - h, fb)
                        if fb:
                            low_up(job + 2, 1 - h, fb - 1)
                        if fb == 4:
                            token_low(job + 1, 1 - h)
                    each(fb)
                act_low(m, FB - 1)
                if n_next is not None:
                    low_up(job + 2, 1 - h, FB - 1)

            def hot_and_residual(s, h, n):
                def each(fb):
                    if fb == 2:
                        residual(s - 1, 1 - h, n)
                    for c in range(2 if fb < HOT // 2 else 0):
                        one_hot(s, 2 * fb + c)
                return each

            mlp(0, each=lambda fb: {1: route_top, 3: route_second}.get(fb, lambda: None)())
            mlp(1, each=lambda fb: {0: route_weights, 2: lambda: residual(0, 0, 1),
                                    3: route_counts}.get(fb, lambda: None)())
            mlp(2, each=lambda fb: {0: route_jobs, 2: lambda: residual(1, 1, 1),
                                    3: route_places}.get(fb, lambda: None)())
            ve.wait_ge(hot_ps, at(hot_ps, 1))
            with ve.Fori(0, 2) as i:
                mlp(2 * i + 3, each=hot_and_residual(2 * i + 3, 1, i + 2))
                mlp(2 * i + 4, each=hot_and_residual(2 * i + 4, 0, i + 2))
            mlp(NSEG - 1, each=lambda fb: {0: slot_table, 2: lambda: residual(NSEG - 2, 0, NSEG // 2)}
                .get(fb, lambda: None)(), job=-1, h=1, n_next=1)
            mlp(NSEG, each=lambda fb: residual(NSEG - 1, 1, NSEG // 2) if fb == 2 else None, job=0, h=0, n_next=1)
            with ve.Fori(0, JOBS // 2 - 1) as i:
                mlp(2 * i + (NSEG + 1), job=2 * i + 1, h=1, n_next=i + 2)
                mlp(2 * i + (NSEG + 2), job=2 * i + 2, h=0, n_next=i + 2)
            mlp(NSEG + JOBS - 2, job=JOBS - 2, h=1, n_next=JOBS // 2 + 1)
            mlp(NSEG + JOBS - 1)


_INS = ["x", "ctx_1024"] + [f"L0_xattn_{w}{g}" for g in "qkvgo" for w in ("W", "b")] + \
       ["L0_ffn_gate_w", "L0_ffn_base_wgu", "L0_ffn_base_wd", "L0_ffn_exp_wgu", "L0_ffn_exp_wd"]


def kernel(**inputs):
    import numpy as np
    import concourse.bacc as bacc
    from concourse.bass_utils import run_bass_kernel_spmd

    nc = bacc.Bacc("TRN2", target_bir_lowering=False, num_devices=1)
    arrays, args = {}, []
    for name in _INS:
        a = np.ascontiguousarray(inputs[name])
        arrays[name] = a
        args.append(nc.dram_tensor(name, a.shape, mybir.dt.from_np(a.dtype), kind="ExternalInput").ap())
    args.append(nc.dram_tensor("out", (ROWS, D), F32, kind="ExternalOutput").ap())
    build(nc, *args)
    r = run_bass_kernel_spmd(nc, [arrays], core_ids=[0])
    return r.results[0]["out"][0:T].reshape(BATCH, NTOK, D)
```

```python
from contextlib import ExitStack

import concourse.bass as bass
from concourse import mybir

F32 = mybir.dt.float32
F32R = mybir.dt.float32r
I32 = mybir.dt.int32
ALU = mybir.AluOpType
ACT = mybir.ActivationFunctionType
X = mybir.AxisListType.X
ds = bass.ds

P = 128
BATCH, NTOK, D = 4, 512, 256
T = BATCH * NTOK
KD = D // P
HEADS, HDIM = 16, 16
GH = HEADS // 2
SEG = 256
NSEG = T // SEG
UNITS = NSEG + BATCH
PAIRS = GH // 2
LN_EPS = 1e-5
F = 704
FB = 6
FSZ = [P] * (F // P) + [F % P]
E = 8
TOPK = 2
JOBS = T * TOPK // SEG + E - 1
COLS = 2 * (JOBS + 1)
ROWS = T + SEG
BIG = 3.0e38


def build(nc, x, ctx_in, Wq, bq, Wk, bk, Wv, bv, Wg, bg, Wo, bo, gate_w, base_wgu, base_wd,
          exp_wgu, exp_wd, out):
    xn_tab = nc.dram_tensor("xn_tab", (ROWS, D), F32, kind="Internal").ap()
    qk_tab = nc.dram_tensor("qk_tab", (UNITS, 4, P, SEG), F32, kind="Internal").ap()
    x_seg = x.rearrange("b (s p a) d -> (b s) p (a d)", p=P, a=2)
    ctx_seg = ctx_in.rearrange("b (s p a) d -> (b s) p (a d)", p=P, a=2)
    out_seg = out[0:T, :].rearrange("(s p a) d -> s p (a d)", p=P, a=2)
    xn_seg = xn_tab[0:T, :].rearrange("(s p a) d -> s p (a d)", p=P, a=2)

    es = ExitStack()
    with es:
        def sb(name, shape, dt=F32, where=None):
            return (where or es).enter_context(nc.sbuf_tensor(name, shape, dt))

        def ps(name, shape=(P, 512), where=None):
            return (where or es).enter_context(nc.psum_tensor(name, list(shape), F32))

        starts = []

        def sem(name, start=0):
            made = es.enter_context(nc.semaphore(name))
            starts.append((made, start))
            return made

        def at(waited, count):
            return count + next(n for made, n in starts if made is waited)

        x_all = sb("x_all", [P, NSEG, 2 * D])
        ident = sb("ident", [P, P])
        ones = sb("ones", [P, P])
        tri = sb("tri", [P, P])
        halves = sb("halves", [P, 2])
        wq_s = sb("wq_s", [P, KD, D])
        wk_s = sb("wk_s", [P, KD, D])
        wv_s = sb("wv_s", [P, KD, D])
        wg_s = sb("wg_s", [P, KD, D])
        wo_s = sb("wo_s", [P, KD, D])
        gw_s = sb("gw_s", [P, KD, E])
        gw_h = sb("gw_h", [P, KD, E], F32R)
        gw_l = sb("gw_l", [P, KD, E], F32R)
        bias_s = sb("bias_s", [P, 3, 2])
        bias_m = sb("bias_m", [P, 2])
        bv_b = sb("bv_b", [P, D])
        bo_b = sb("bo_b", [P, D])
        gT = sb("gT", [P, UNITS * SEG])
        attn = sb("attn", [P, UNITS * SEG])
        xn = [sb(f"xn{h}", [P, 2, D]) for h in range(2)]
        stats = [sb(f"stats{h}", [P, 2, 6]) for h in range(2)]
        mv = [sb(f"mv{h}", [P, 2, 2]) for h in range(2)]
        veps = [sb(f"veps{h}", [P, 2]) for h in range(2)]
        rstd = [sb(f"rstd{h}", [P, 2]) for h in range(2)]
        raw_gu0 = sb("raw_gu0", [P, KD, 2 * F])
        raw_d0 = sb("raw_d0", [P, FB, D])
        logits = sb("logits", [P, 2 * NSEG, E])
        logits_t = sb("logits_t", [E, T])

        early = ExitStack()
        ctx_s = [sb(f"ctx_s{h}", [P, 2 * D], where=early) for h in range(2)]
        xT = [sb(f"xT{h}", [P, KD, SEG], where=early) for h in range(2)]
        cT = [sb(f"cT{h}", [P, KD, SEG], where=early) for h in range(2)]
        qk32 = [sb(f"qk32{h}", [P, 2, SEG + P], where=early) for h in range(2)]
        qk_hl = [sb(f"qk_hl{h}", [P, 4, SEG + P], F32R, where=early) for h in range(2)]
        v_all = sb("v_all", [P, UNITS * 2, P], where=early)
        q_st = [sb(f"q_st{h}", [P, PAIRS, SEG], F32R, where=early) for h in range(2)]
        k_st = [sb(f"k_st{h}", [P, PAIRS, 2 * SEG], F32R, where=early) for h in range(2)]
        vpad = [sb(f"vpad{h}", [P, 2, GH, P], where=early) for h in range(2)]
        prob = [sb(f"prob{r}", [P, 2, 2, SEG], where=early) for r in range(2)]
        pT = [[sb(f"pT{r}{h}", [P, 2, SEG], where=early) for h in range(2)] for r in range(2)]
        nmax = [sb(f"nmax{r}", [P, 2, 2], where=early) for r in range(2)]
        rsum = [sb(f"rsum{h}", [P, 2, GH], where=early) for h in range(2)]
        rinv = [sb(f"rinv{h}", [P, 2, GH], where=early) for h in range(2)]
        rexp = [sb(f"rexp{h}", [P, 2, GH, HDIM], where=early) for h in range(2)]
        rts = [sb(f"rts{h}", [P, SEG], where=early) for h in range(2)]
        early.close()

        x2T = [sb(f"x2T{h}", [P, KD, SEG]) for h in range(2)]
        shared = ExitStack()
        x2h = sb("x2h", [P, NSEG, KD, SEG], F32R, where=shared)
        x2l = sb("x2l", [P, NSEG, KD, SEG], F32R, where=shared)
        shared.close()
        raw_gu1 = sb("raw_gu1", [P, KD, 2 * F])
        raw_d1 = sb("raw_d1", [P, FB, D])
        raw_gu, raw_d = [raw_gu0, raw_gu1], [raw_d0, raw_d1]
        xg = [sb(f"xg{h}", [P, 2, D]) for h in range(2)]
        xjh = [sb(f"xjh{h}", [P, KD, SEG], F32R) for h in range(2)]
        xjl = [sb(f"xjl{h}", [P, KD, SEG], F32R) for h in range(2)]
        rest = 2 * NSEG * KD * SEG - (KD * 2 * F + FB * D) - 3 * 2 * KD * SEG
        sb("rest", [P, rest])
        wh_gu = sb("wh_gu", [P, KD, 2 * F], F32R)
        wl_gu = sb("wl_gu", [P, KD, 2 * F], F32R)
        wh_d = sb("wh_d", [P, FB, D], F32R)
        wl_d = sb("wl_d", [P, FB, D], F32R)
        sg = [sb(f"sg{r}", [P, SEG]) for r in range(2)]
        act = [sb(f"act{r}", [P, SEG]) for r in range(2)]
        act_h = sb("act_h", [P, FB, SEG], F32R)
        act_l = sb("act_l", [P, FB, SEG], F32R)
        y_s = [sb(f"y_s{h}", [P, 2, D]) for h in range(2)]
        NT = 2 * NSEG
        desc = sb("desc", [P, E])
        k256 = sb("k256", [P, T // SEG])
        jcol = sb("jcol", [1, JOBS + 1])
        rowid = sb("rowid", [P, TOPK, NT])
        spare = sb("spare", [P, JOBS + 1, 2])
        iota = sb("iota", [P, P])
        m1 = sb("m1", [P, TOPK, NT])
        eq = sb("eq", [P, NT, E])
        fi = sb("fi", [P, NT])
        sel = sb("sel", [P, TOPK, NT, E])
        l2 = sb("l2", [P, NT, E])
        wexp = sb("wexp", [P, 3, NT])
        wts = sb("wts", [P, TOPK, NT])
        member = sb("member", [P, NT, E])
        scan = [sb(f"scan{r}", [P, NT, E]) for r in range(2)]
        ntile = sb("ntile", [P, E, T // SEG])
        tiles = sb("tiles", [P, E])
        tend = [sb(f"tend{r}", [P, E]) for r in range(2)]
        pos = sb("pos", [P, NT, E])
        poss = sb("poss", [P, TOPK, NT])
        posi = sb("posi", [P, 3, TOPK, NT], I32)
        posf = sb("posf", [P, 2, TOPK, NT])
        jobe = sb("jobe", [1, JOBS + 1, E])
        jobf = sb("jobf", [1, JOBS + 1])
        jobi = sb("jobi", [1, JOBS + 1], I32)
        hot = [sb(f"hot{r}", [P, P]) for r in range(4)]
        val = [sb(f"val{r}", [P, 2, COLS]) for r in range(4)]
        tokf = sb("tokf", [P, 3, COLS])
        toki = sb("toki", [P, COLS], I32)
        slot_g = sb("slot_g", [P, 2], I32)
        slot_s = sb("slot_s", [P, 2], I32)
        zero = sb("zero", [P, 2, D])

        bank = [ps(f"bank{n}") for n in range(8)]

        ld_w = sem("ld_w")
        ld_x = [sem(f"ld_x{h}") for h in range(2)]
        ld_x2, ld_x3 = sem("ld_x2"), sem("ld_x3", 1)
        ld_c = [sem(f"ld_c{h}") for h in range(2)]
        passed = sem("passed")
        consts = sem("consts")
        pads_rdy = sem("pads_rdy")
        dv = sem("dv")
        gp = sem("gp")
        var_rdy = sem("var_rdy")
        rstd_rdy = sem("rstd_rdy")
        xn_rdy = sem("xn_rdy")
        xt_ps = sem("xt_ps", 2)
        ct_ps = sem("ct_ps", 2)
        xt_ev = sem("xt_ev", 1)
        ct_ev = sem("ct_ev", 1)
        q_ps, k_ps, g_ps1, v_ps = sem("q_ps"), sem("k_ps"), sem("g_ps1"), sem("v_ps", 2)
        q_ev, k_ev, ge_ev, v_ev = sem("q_ev", 1), sem("k_ev", 1), sem("ge_ev", 1), sem("v_ev", 1)
        bm_rdy = sem("bm_rdy")
        qkh_rdy, qkl_rdy = sem("qkh_rdy"), sem("qkl_rdy", 2)
        qk_stored = [sem(f"qk_stored{h}", 1) for h in range(2)]
        ld_unit = [sem(f"ld_unit{h}") for h in range(2)]
        vp_rdy = sem("vp_rdy")
        s_ps = sem("s_ps", 9)
        m_rdy = sem("m_rdy")
        p_rdy = sem("p_rdy", 4)
        t_ps = sem("t_ps", 3)
        pt_ev = [sem(f"pt_ev{h}", 1) for h in range(2)]
        pv_ps = sem("pv_ps", 2)
        o_ev = sem("o_ev", 2)
        rt_ps = sem("rt_ps", 2)
        rexp_rdy, rts_rdy = sem("rexp_rdy"), sem("rts_rdy", 1)
        gated = sem("gated")
        xbo_rdy = sem("xbo_rdy")
        xo_ps = sem("xo_ps", 2)
        x1_rdy = sem("x1_rdy", 2)
        var2, rstd2, xn2_rdy = sem("var2"), sem("rstd2"), sem("xn2_rdy")
        xn2_st = [sem(f"xn2_st{h}", 1) for h in range(2)]
        t2_ps = sem("t2_ps", 2)
        gwh_rdy, gwl_rdy = sem("gwh_rdy"), sem("gwl_rdy")
        lt_ps, lt_ev = sem("lt_ps"), sem("lt_ev")
        lg_ps = sem("lg_ps")
        x2h_rdy, x2l_rdy = sem("x2h_rdy", 2), sem("x2l_rdy", 2)
        ld_gu = [sem(f"ld_gu{h}") for h in range(2)]
        ld_d = [sem(f"ld_d{h}") for h in range(2)]
        wh_rdy, wl_rdy = sem("wh_rdy"), sem("wl_rdy")
        wd_rdy, wdl_rdy = sem("wd_rdy"), sem("wdl_rdy")
        g_ps, u_ps = sem("g_ps"), sem("u_ps")
        sg_rdy = sem("sg_rdy", 2)
        a_rdy = sem("a_rdy", 2)
        ah_rdy = sem("ah_rdy", 2)
        al_rdy = sem("al_rdy", 2)
        dn_ps = sem("dn_ps", 6)
        y_rdy = sem("y_rdy", 2)
        out_st = [sem(f"out_st{h}", 1) for h in range(2)]
        zero_st = sem("zero_st")
        m_in, dif_rdy, ex_rdy = sem("m_in"), sem("dif_rdy"), sem("ex_rdy")
        pre_ps, pre_ev = sem("pre_ps"), sem("pre_ev")
        hot_rdy, hot_ps = sem("hot_rdy"), sem("hot_ps", 3)
        jobs_rdy, slots_rdy = sem("jobs_rdy"), sem("slots_rdy")
        sg_cp, ss_cp = sem("sg_cp"), sem("ss_cp", 1)
        gath = [[sem(f"gath{h}{a}") for a in range(2)] for h in range(2)]
        tj_ps, xjh_rdy, xjl_rdy = sem("tj_ps", 2), sem("xjh_rdy"), sem("xjl_rdy", 1)
        scat = [sem(f"scat{a}") for a in range(2)]

        block = es.enter_context(nc.Block())

        def alone(eng):
            eng.sem_inc(passed, 1)

        def view(t, *shape):
            pat = {2: "p (a b) -> p a b", 3: "p (a b c) -> p a b c"}[len(shape)]
            n = 1
            for k in shape:
                n *= k
            return t[:, 0:n].rearrange(pat, **dict(zip("abc", shape)))

        def gu(t, fb):
            return t[:, :, :].rearrange("p k (t f) -> p k t f", t=2)[:, :, :, fb * P:fb * P + FSZ[fb]]

        WEIGHT_LOADS = 14
        GROUPS = NSEG // 2
        HOT_FB = (0, 0, 1, 1, 2, 3, 3, 4)
        HOT = len(HOT_FB)
        HOT0 = NSEG - 1 - TOPK * 2 * NSEG // HOT

        def raw_loads(h, n, size=16):
            return size * n + (size if h == 0 else 0)

        @block.sync
        def _(sp):
            def load_ctx(s, h):
                sp.dma_start(ctx_s[h][:, :], ctx_seg[s]).then_inc(ld_c[h], 16)

            def load_x(s, done):
                sp.dma_start(x_all[:, s:s + 2, :], x_seg[s:s + 2].rearrange("s p d -> p s d")).then_inc(done, 16)

            def store_qk(i, h):
                sp.wait_ge(qkl_rdy, at(qkl_rdy, 2 * i + (h + 1)))
                alone(sp)
                sp.wait_ge(qk_stored[h], at(qk_stored[h], 32 * i))
                sp.dma_start(qk_tab[ds(2 * i + h, 1), :, :, :].rearrange("u j p t -> p (u j) t"),
                             qk_hl[h][:, :, 0:SEG].bitcast(F32)).then_inc(qk_stored[h], 16)
                sp.dma_start(qk_tab[ds(NSEG + i, 1), :, :, h * P:(h + 1) * P].rearrange("u j p t -> p (u j) t"),
                             qk_hl[h][:, :, SEG:SEG + P].bitcast(F32)).then_inc(qk_stored[h], 16)

            def load_unit(u, h):
                tab = qk_tab[ds(u, 1), :, :, :].rearrange("u j (g r) t -> (u j) r g t", g=PAIRS)
                for c in range(4):
                    rows = slice(2 * HDIM * c, 2 * HDIM * (c + 1))
                    sp.dma_start(q_st[h][rows, :, :].bitcast(F32), tab[2 * (c // 2)]).then_inc(ld_unit[h], 16)
                    for k in range(2):
                        rows = slice(HDIM * (2 * c + k), HDIM * (2 * c + k + 1))
                        sp.dma_start(k_st[h][rows, :, k * SEG:(k + 1) * SEG].bitcast(F32),
                                     tab[1 + 2 * (c % 2)][k * HDIM:(k + 1) * HDIM]).then_inc(ld_unit[h], 16)

            for h in range(2):
                sp.dma_start(x_all[:, h, :], x_seg[h]).then_inc(ld_x[h], 16)
                load_ctx(h, h)
            load_x(2, ld_x2)
            for made, start in starts:
                if start:
                    sp.sem_inc(made, start)
            sp.wait_ge(ld_w, 16 * WEIGHT_LOADS)
            load_x(4, ld_x3)
            sp.wait_ge(ld_x3, at(ld_x3, 16))
            load_x(6, ld_x3)
            with sp.Fori(1, NSEG // 2) as i:
                for h in range(2):
                    sp.wait_ge(ld_c[h], 16 * i)
                    alone(sp)
                    sp.wait_ge(ct_ps, at(ct_ps, 2 * i + (h - 1)))
                    load_ctx(2 * i + h, h)
                    store_qk(i - 1, h)

            sp.wait_ge(pads_rdy, 1)
            for h in range(2):
                sp.wait_ge(qk_stored[h], at(qk_stored[h], 32))
                load_unit(h, h)
            for h in range(2):
                store_qk(NSEG // 2 - 1, h)
            def load_gu(h, w):
                sp.dma_start(raw_gu[h][:, :, :], w.rearrange("(k p) f -> p k f", p=P)).then_inc(ld_gu[h], 16)

            def load_d(h, w):
                sp.dma_start(raw_d[h][:, 0:FB - 1, :],
                             w[0:(FB - 1) * P, :].rearrange("(k p) n -> p k n", p=P)).then_inc(ld_d[h], 16)
                sp.dma_start(raw_d[h][0:FSZ[-1], FB - 1, :], w[(FB - 1) * P:F, :]).then_inc(ld_d[h], 16)

            load_gu(0, base_wgu)
            load_d(0, base_wd)
            for h in range(2):
                sp.wait_ge(qk_stored[h], at(qk_stored[h], 32 * (NSEG // 2)))
            with sp.Fori(1, UNITS // 2) as i:
                for h in range(2):
                    sp.wait_ge(s_ps, at(s_ps, 16 * i + (8 * h - 8)))
                    alone(sp)
                    load_unit(2 * i + h, h)
            with sp.Fori(0, NSEG // 2) as i:
                for h in range(2):
                    sp.wait_ge(xn2_rdy, 2 * i + (h + 1))
                    alone(sp)
                    sp.wait_ge(xn2_st[h], at(xn2_st[h], 16 * i))
                    sp.dma_start(xn_seg[2 * i + h], xn[h][:, :, :].rearrange("p a d -> p (a d)")).then_inc(xn2_st[h], 16)
            sp.wait_ge(consts, 2)
            sp.dma_start(xn_tab[T:ROWS, :].rearrange("(a p) d -> p a d", a=2), zero[:, :, :]).then_inc(zero_st, 16)
            sp.dma_start(out[T:ROWS, :].rearrange("(a p) d -> p a d", a=2), zero[:, :, :]).then_inc(zero_st, 16)
            def expert_of(j):
                return ds(sp.value_load(jobi[0:1, ds(j, 1)], min_val=0, max_val=E - 1), 1)

            def expert_gu(j, h):
                sp.wait_ge(wl_rdy, FB * j)
                alone(sp)
                load_gu(h, exp_wgu[expert_of(j), :, :].rearrange("u k f -> (u k) f"))

            def expert_d(j, h):
                sp.wait_ge(wdl_rdy, FB * j)
                alone(sp)
                load_d(h, exp_wd[expert_of(j), :, :].rearrange("u k n -> (u k) n"))

            def store(s, h, n):
                sp.wait_ge(y_rdy, at(y_rdy, s + 1))
                alone(sp)
                sp.wait_ge(out_st[h], at(out_st[h], 16 * n))
                sp.dma_start(out_seg[s], y_s[h][:, :, :].rearrange("p a d -> p (a d)")).then_inc(out_st[h], 16)

            store(0, 0, 0)
            store(1, 1, 0)
            sp.wait_ge(jobs_rdy, 1)
            sp.wait_ge(wl_rdy, FB)
            sp.wait_ge(wdl_rdy, FB)
            load_gu(0, exp_wgu[expert_of(0), :, :].rearrange("u k f -> (u k) f"))
            load_d(0, exp_wd[expert_of(0), :, :].rearrange("u k n -> (u k) n"))
            with sp.Fori(1, NSEG // 2 - 1) as i:
                for h in range(2):
                    store(2 * i + h, h, i)
            store(NSEG - 2, 0, NSEG // 2 - 1)
            sp.wait_ge(u_ps, FB * NSEG)
            expert_gu(1, 1)
            expert_d(1, 1)
            store(NSEG - 1, 1, NSEG // 2 - 1)
            expert_gu(2, 0)
            with sp.Fori(1, JOBS // 2) as i:
                expert_d(2 * i, 0)
                expert_gu(2 * i + 1, 1)
                expert_d(2 * i + 1, 1)
                expert_gu(2 * i + 2, 0)
            expert_d(JOBS - 1, 0)
            for h, n in enumerate((JOBS // 2 + 1, JOBS // 2)):
                sp.wait_ge(ld_gu[h], raw_loads(h, n))
                sp.wait_ge(ld_d[h], raw_loads(h, n, 32))
            for h in range(2):
                sp.wait_ge(xn2_st[h], at(xn2_st[h], 16 * (NSEG // 2)))
                sp.wait_ge(out_st[h], at(out_st[h], 16 * (NSEG // 2)))
            for a in range(2):
                sp.wait_ge(scat[a], at(scat[a], 16 * JOBS))
            sp.wait_ge(zero_st, 32)

        @block.gpsimd
        def _(pool):
            n = [0]

            def step(ins):
                n[0] += 1
                ins.then_inc(gp, 1)
                pool.wait_ge(gp, n[0])

            step(pool.memset(ident[:, :], 0.0))
            step(pool.affine_select(out=ident[:, :], in_=ident[:, :], compare_op=ALU.not_equal, fill=1.0,
                                    base=0, pattern=[[-1, P]], channel_multiplier=1))
            step(pool.memset(halves[:, :], -0.5))
            step(pool.memset(ones[:, :], 1.0))
            step(pool.memset(tri[:, :], 1.0))
            step(pool.affine_select(out=tri[:, :], in_=tri[:, :], compare_op=ALU.is_gt, fill=0.0,
                                    base=0, pattern=[[1, P]], channel_multiplier=-1))
            pool.sem_inc(consts, 1)
            def rsqrt1(s, h):
                pool.wait_ge(var_rdy, s + 1)
                pool.tensor_tensor(rstd[h][:, :], veps[h][:, :], halves[:, :], ALU.pow).then_inc(rstd_rdy, 1)

            def qk_low(s, h):
                pool.wait_ge(qkh_rdy, s + 1)
                pool.tensor_tensor(qk_hl[h][:, 2:4, :], qk32[h][:, :, :], qk_hl[h][:, 0:2, :].bitcast(F32),
                                   ALU.subtract).then_inc(qkl_rdy, 1)

            def pad_values(u, h):
                pool.wait_ge(rt_ps, at(rt_ps, u - 1))
                alone(pool)
                for kb in range(2):
                    diag = vpad[h][:, kb, :, :].rearrange("p g c -> p (g c)")
                    last = pool.tensor_copy(
                        bass.AP(diag.tensor, diag.offset, [list(diag.ap[0]), [P + HDIM, GH], [1, HDIM]]),
                        v_all[:, ds(2 * u + kb, 1), :].rearrange("p u (g c) -> p (u g) c", g=GH))
                last.then_inc(vp_rdy, 1)

            for h in range(2):
                rsqrt1(h, h)
            for h in range(2):
                step(pool.memset(k_st[h][:, :, :].bitcast(F32), 0.0))
                step(pool.memset(vpad[h][:, :, :, :], 0.0))
            pool.sem_inc(pads_rdy, 1)
            pool.wait_ge(gwh_rdy, 1)
            pool.tensor_tensor(gw_l[:, :, :], gw_s[:, :, :], gw_h[:, :, :].bitcast(F32), ALU.subtract).then_inc(gwl_rdy, 1)
            with pool.Fori(0, NSEG // 2 - 1) as i:
                for h in range(2):
                    rsqrt1(2 * i + (h + 2), h)
                    qk_low(2 * i + h, h)
            for h in range(2):
                qk_low(NSEG - 2 + h, h)
            pool.wait_ge(v_ev, at(v_ev, NSEG))
            with pool.Fori(0, UNITS // 2) as i:
                for h in range(2):
                    pad_values(2 * i + h, h)

            pool.tensor_tensor(x_all[:, :, :].rearrange("p s (a d) -> p (s a) d", a=2),
                               x_all[:, :, :].rearrange("p s (a d) -> p (s a) d", a=2),
                               bo_b[:, :].unsqueeze(1).to_broadcast([P, 2 * NSEG, D]), ALU.add).then_inc(xbo_rdy, 1)

            pool.wait_ge(o_ev, at(o_ev, UNITS))
            def rsqrt2(s, h):
                pool.wait_ge(var2, s + 1)
                pool.tensor_tensor(rstd[h][:, :], veps[h][:, :], halves[:, :], ALU.pow).then_inc(rstd2, 1)

            def token_low2(s, h):
                pool.wait_ge(x2h_rdy, at(x2h_rdy, s + 1))
                alone(pool)
                pool.tensor_tensor(x2l[:, ds(s, 1), :, :].rearrange("p u k t -> p (u k) t"), x2T[h][:, :, :],
                                   x2h[:, ds(s, 1), :, :].rearrange("p u k t -> p (u k) t").bitcast(F32),
                                   ALU.subtract).then_inc(x2l_rdy, 1)

            def low_down(m, r, blocks=range(FB)):
                for fb in blocks:
                    sz = FSZ[fb]
                    pool.wait_ge(wd_rdy, FB * m + (fb + 1))
                    pool.tensor_tensor(wl_d[0:sz, fb, :], raw_d[r][0:sz, fb, :],
                                       wh_d[0:sz, fb, :].bitcast(F32), ALU.subtract).then_inc(wdl_rdy, 1)

            def low_up(fb):
                pool.wait_ge(wh_rdy, fb + 1)
                pool.tensor_tensor(gu(wl_gu, fb), gu(raw_gu[0], fb), gu(wh_gu, fb).bitcast(F32),
                                   ALU.subtract).then_inc(wl_rdy, 1)

            low_up(0)
            rsqrt2(0, 0)
            low_up(1)
            rsqrt2(1, 1)
            low_up(2)
            low_up(3)
            with pool.Fori(0, NSEG // 2 - 1) as i:
                for h in range(2):
                    token_low2(2 * i + h, h)
                    rsqrt2(2 * i + (h + 2), h)
            for h in range(2):
                token_low2(NSEG - 2 + h, h)
                low_up(FB - 2 + h)
            low_down(0, 0)


            step(pool.memset(zero[:, :, :], 0.0))
            step(pool.iota(desc[:, :], [[-1, E]], base=E, channel_multiplier=0, allow_small_or_imprecise_dtypes=True))
            step(pool.iota(k256[:, :], [[SEG, T // SEG]], base=0, channel_multiplier=0, allow_small_or_imprecise_dtypes=True))
            step(pool.iota(jcol[:, :], [[1, JOBS + 1]], base=0, channel_multiplier=0, allow_small_or_imprecise_dtypes=True))
            step(pool.iota(rowid[:, :, :].rearrange("p c (s a) -> p c s a", a=2), [[0, TOPK], [SEG, NSEG], [1, 2]], base=1, channel_multiplier=2, allow_small_or_imprecise_dtypes=True))
            step(pool.iota(spare[:, :, :], [[0, JOBS + 1], [P, 2]], base=T + 1, channel_multiplier=1, allow_small_or_imprecise_dtypes=True))
            step(pool.iota(iota[:, :], [[1, P]], base=0, channel_multiplier=0, allow_small_or_imprecise_dtypes=True))
            pool.sem_inc(consts, 1)

            pool.wait_ge(slots_rdy, 1)
            pool.wait_ge(zero_st, 32)
            for h in range(2):
                pool.wait_ge(xn2_st[h], at(xn2_st[h], 16 * (NSEG // 2)))

            def gather(j, h):
                pool.wait_ge(tj_ps, at(tj_ps, j - 1))
                alone(pool)
                pool.tensor_copy(slot_g[:, :], toki[:, ds(2 * j, 2)]).then_inc(sg_cp, 1)
                pool.wait_ge(sg_cp, j + 1)
                alone(pool)
                for a in range(2):
                    pool.indirect_dma_start(xg[h][:, a, :], None, xn_tab[:, :],
                                            bass.IndirectOffsetOnAxis(slot_g[:, a:a + 1], 0)).then_inc(gath[h][a], 16)

            def scatter(j, h, first=False):
                if not first:
                    for a in range(2):
                        pool.wait_ge(scat[a], 16 * j)
                    alone(pool)
                pool.tensor_copy(slot_s[:, :], toki[:, ds(2 * j, 2)]).then_inc(ss_cp, 1)
                pool.wait_ge(ss_cp, at(ss_cp, j + 1))
                pool.wait_ge(y_rdy, at(y_rdy, j + (NSEG + 1)))
                alone(pool)
                for a in range(2):
                    pool.indirect_dma_start(out[:, :], bass.IndirectOffsetOnAxis(slot_s[:, a:a + 1], 0),
                                            y_s[h][:, a, :], None, compute_op=ALU.add).then_inc(scat[a], 16)

            def expert_job(j, h, n, gathers=True, last=False, previous="job"):
                low_down(j + 1, h, range(3, FB))
                if previous:
                    scatter(j - 1, 1 - h, first=previous == "first")
                if gathers:
                    for a in range(2):
                        pool.wait_ge(gath[1 - h][a], 16 * (n + h))
                    gather(j + 2, h)
                if not last:
                    low_down(j + 2, 1 - h, range(3))

            gather(0, 0)
            for a in range(2):
                pool.wait_ge(gath[0][a], 16)
            gather(1, 1)
            low_down(1, 0, range(3))
            expert_job(0, 0, 1, previous=None)
            for h in range(2):
                pool.wait_ge(out_st[h], at(out_st[h], 16 * (NSEG // 2)))
            expert_job(1, 1, 1, previous="first")
            expert_job(2, 0, 2)
            with pool.Fori(1, JOBS // 2 - 1) as i:
                expert_job(2 * i + 1, 1, i + 1)
                expert_job(2 * i + 2, 0, i + 2)
            expert_job(JOBS - 2, 1, JOBS // 2, gathers=False)
            expert_job(JOBS - 1, 0, JOBS // 2 + 1, gathers=False, last=True)
            scatter(JOBS - 1, 0)

        @block.scalar
        def _(sc):
            loads = [(w_s[:, :, :], w.rearrange("(k p) o -> p k o", p=P)) for w_s, w in
                     ((wq_s, Wq), (wk_s, Wk), (wg_s, Wg), (wv_s, Wv), (wo_s, Wo), (gw_s, gate_w))]
            for n, b in enumerate((bq, bk, bg)):
                for ob in range(2):
                    loads.append((bias_s[:, n, ob:ob + 1], b[ob * P:(ob + 1) * P].rearrange("(p u) -> p u", u=1)))
            loads += [(bv_b[:, :], bv.partition_broadcast(P)), (bo_b[:, :], bo.partition_broadcast(P))]
            for dst, src in loads:
                sc.dma_start(dst, src).then_inc(ld_w, 16)
            assert len(loads) == WEIGHT_LOADS
            sc.wait_ge(ld_w, 16 * WEIGHT_LOADS)
            sc.activation(bias_m[:, :], bias_s[:, 0, :], ACT.Copy, scale=0.25).then_inc(bm_rdy, 1)
            sc.activation(gw_h[:, :, :], gw_s[:, :, :], ACT.Copy).then_inc(gwh_rdy, 1)
            sc.wait_ge(bm_rdy, 1)

            def input_tile(s, h):
                sc.wait_ge(xt_ps, at(xt_ps, s + 1))
                sc.wait_ge(v_ps, at(v_ps, s - 1))
                sc.activation(xT[h][:, :, :], view(bank[0], KD, SEG), ACT.Copy).then_inc(xt_ev, 1)

            def projected(s, h, stored):
                g0, g1 = ds(SEG * s, SEG), ds(T + P * s, P)
                sc.wait_ge(q_ps, s + 1)
                sc.wait_ge(qkl_rdy, at(qkl_rdy, s - 1))
                sc.activation(qk32[h][:, 0, 0:SEG], bank[2][:, 0:SEG], ACT.Identity, bias=bias_m[:, 0:1], scale=0.25)
                sc.activation(qk32[h][:, 0, SEG:SEG + P], bank[2][:, SEG:SEG + P], ACT.Identity, bias=bias_m[:, 1:2],
                              scale=0.25).then_inc(q_ev, 1)
                sc.wait_ge(g_ps1, s + 1)
                sc.activation(gT[:, g0], bank[4][:, 0:SEG], ACT.Sigmoid, bias=bias_s[:, 2, 0:1])
                sc.activation(gT[:, g1], bank[4][:, SEG:SEG + P], ACT.Sigmoid,
                              bias=bias_s[:, 2, 1:2]).then_inc(ge_ev, 1)
                sc.wait_ge(q_ev, at(q_ev, s + 1))
                sc.wait_ge(k_ev, at(k_ev, s + 1))
                sc.wait_ge(qk_stored[h], at(qk_stored[h], stored))
                sc.activation(qk_hl[h][:, 0:2, :], qk32[h][:, :, :], ACT.Copy).then_inc(qkh_rdy, 1)

            input_tile(0, 0)
            with sc.Fori(0, NSEG // 2 - 1) as i:
                for h in range(2):
                    input_tile(2 * i + (h + 1), 1 - h)
                    projected(2 * i + h, h, 32 * i)
            input_tile(NSEG - 1, 1)
            projected(NSEG - 2, 0, 16 * (NSEG - 2))
            projected(NSEG - 1, 1, 16 * (NSEG - 2))

            def exps(g, h, hp):
                r = g % 2 if isinstance(g, int) else hp % 2
                sc.wait_ge(t_ps, at(t_ps, 2 * g - 2))
                for qb in range(2):
                    sc.wait_ge(m_rdy, 2 * g + (qb + 1))
                    for k in range(2):
                        last = sc.activation(prob[r][:, qb, k, :], view(bank[2 * r + qb], 2, SEG)[:, k, :],
                                             ACT.Exp, bias=nmax[r][:, qb, k:k + 1],
                                             accum_out=rsum[h][:, qb, 2 * hp + k:2 * hp + k + 1])
                    last.then_inc(p_rdy, 1)

            def evacuate(g, hp):
                r = hp % 2
                sc.wait_ge(t_ps, at(t_ps, 2 * g + 2))
                sc.wait_ge(pv_ps, at(pv_ps, g - 1))
                sc.activation(pT[r][1][:, :, :], view(bank[5], 2, SEG), ACT.Copy).then_inc(pt_ev[1], 1)

            def attend(i, last_units=False):
                for c in range(2 * PAIRS):
                    g = 8 * i + c
                    if not (last_units and c + 2 >= 2 * PAIRS):
                        exps(g + 2, ((c + 2) // PAIRS) % 2, (c + 2) % PAIRS)
                    if not (last_units and c + 1 >= 2 * PAIRS):
                        evacuate(g + 1, (c + 1) % PAIRS)
                    if c in (PAIRS, 2 * PAIRS - 1):
                        h = c // (PAIRS + 1)
                        sc.wait_ge(rt_ps, at(rt_ps, 2 * i + (h + 1)))
                        sc.wait_ge(o_ev, at(o_ev, 2 * i + (h - 1)))
                        sc.activation(rts[h][:, :], bank[6 + h][:, SEG:2 * SEG], ACT.Copy).then_inc(rts_rdy, 1)

            exps(0, 0, 0)
            exps(1, 0, 1)
            evacuate(0, 0)
            with sc.Fori(0, UNITS // 2 - 1) as i:
                attend(i)
            attend(UNITS // 2 - 1, True)

            def high_down(m, r, fb):
                sz = FSZ[fb]
                sc.activation(wh_d[0:sz, fb, :], raw_d[r][0:sz, fb, :], ACT.Copy).then_inc(wd_rdy, 1)

            def tokens2(s, h):
                sc.wait_ge(t2_ps, at(t2_ps, s + 1))
                sc.wait_ge(x2l_rdy, at(x2l_rdy, s - 1))
                sc.activation(x2T[h][:, :, :], view(bank[2 + h], KD, SEG), ACT.Copy)
                sc.activation(x2h[:, ds(s, 1), :, :].rearrange("p u k t -> p (u k) t"),
                              view(bank[2 + h], KD, SEG), ACT.Copy).then_inc(x2h_rdy, 1)

            sc.wait_ge(gated, UNITS)
            sc.wait_ge(ld_gu[0], 16)
            for fb in range(FB):
                sc.activation(gu(wh_gu, fb), gu(raw_gu[0], fb), ACT.Copy).then_inc(wh_rdy, 1)
            sc.wait_ge(ld_d[0], 32)
            for fb in range(FB):
                high_down(0, 0, fb)
            with sc.Fori(0, NSEG // 2 - 1) as i:
                for h in range(2):
                    tokens2(2 * i + h, h)
            for h in range(2):
                tokens2(NSEG - 2 + h, h)

            def logits_out(q):
                sc.wait_ge(lt_ps, q + 1)
                sc.activation(logits_t[:, 2 * SEG * q:2 * SEG * (q + 1)], bank[5 + q % 3][0:E, :], ACT.Copy)\
                    .then_inc(lt_ev, 1)

            for q in range(GROUPS - 1):
                logits_out(q)

            def silu(m, fb):
                sz = FSZ[fb]
                sc.wait_ge(g_ps, FB * m + (fb + 1))
                sc.wait_ge(a_rdy, at(a_rdy, FB * m + (fb - 1)))
                sc.activation(sg[fb % 2][0:sz, :], bank[fb % 2][0:sz, 0:SEG], ACT.Silu).then_inc(sg_rdy, 1)

            def act_high(m, fb):
                sz = FSZ[fb]
                sc.wait_ge(a_rdy, at(a_rdy, FB * m + (fb + 1)))
                sc.wait_ge(dn_ps, at(dn_ps, FB * m + (fb - 5)))
                sc.activation(act_h[0:sz, fb, :], act[fb % 2][0:sz, :], ACT.Copy).then_inc(ah_rdy, 1)

            def token_high(j, h):
                sc.wait_ge(tj_ps, at(tj_ps, j + 1))
                sc.activation(xjh[h][:, :, :], view(bank[6], KD, SEG), ACT.Copy).then_inc(xjh_rdy, 1)

            def split_down(j, h, fb):
                sc.wait_ge(dn_ps, at(dn_ps, FB * j + (FB * (NSEG - 1) + fb + 1)))
                high_down(j + 1, h, fb)

            def weigh(j, h):
                sc.wait_ge(dn_ps, at(dn_ps, FB * j + FB * (NSEG + 1)))
                sc.wait_ge(ss_cp, at(ss_cp, j))
                for a in range(2):
                    ins = sc.activation(y_s[h][:, a, :], view(bank[4 + h], 2, D)[:, a, :], ACT.Copy,
                                        scale=tokf[:, 1, ds(2 * j + a, 1)])
                ins.then_inc(y_rdy, 1)

            def mlp(m, j=None, h=None, n=None, n_next=1, own=True, following=True, previous=True,
                    last_logits=False, weights=False):
                for fb in range(FB):
                    silu(m, fb)
                    if last_logits and fb == 0:
                        logits_out(GROUPS - 1)
                    if weights and fb == 1:
                        sc.wait_ge(dif_rdy, 1)
                        sc.activation(wexp[:, 1, :], wexp[:, 0, :], ACT.Exp).then_inc(ex_rdy, 1)
                    if fb:
                        act_high(m, fb - 1)
                    if j is None:
                        continue
                    if fb < 3 and own:
                        split_down(j, h, fb + 3)
                    if fb == 2 and previous:
                        weigh(j - 1, 1 - h)
                    if fb >= 3 and following:
                        if fb == 3:
                            sc.wait_ge(ld_d[1 - h], raw_loads(1 - h, n_next, 32))
                        split_down(j + 1, 1 - h, fb - 3)
                        if fb == 3:
                            token_high(j + 1, 1 - h)
                act_high(m, FB - 1)

            mlp(0, last_logits=True)
            mlp(1, weights=True)
            with sc.Fori(2, NSEG - 1) as s:
                mlp(s)
            mlp(NSEG - 1, -1, 1, own=False, previous=False)
            mlp(NSEG, 0, 0, n_next=1, previous=False)
            for h in range(2):
                sc.wait_ge(out_st[h], at(out_st[h], 16 * (NSEG // 2)))
            with sc.Fori(0, JOBS // 2 - 1) as i:
                mlp(2 * i + (NSEG + 1), 2 * i + 1, 1, n_next=i + 2)
                mlp(2 * i + (NSEG + 2), 2 * i + 2, 0, n_next=i + 2)
            mlp(NSEG + JOBS - 2, JOBS - 2, 1, n_next=JOBS // 2 + 1)
            mlp(NSEG + JOBS - 1, JOBS - 1, 0, following=False)
            weigh(JOBS - 1, 0)

        @block.tensor
        def _(pe):
            pe.wait_ge(consts, 1)

            def transposes(dst, src):
                for kd in range(KD):
                    for a in range(2):
                        last = pe.transpose(dst[:, kd * SEG + a * P:kd * SEG + (a + 1) * P],
                                            src[:, a, kd * P:(kd + 1) * P], ident[:, :])
                return last

            def input_tiles(s, h, n):
                pe.wait_ge(xn_rdy, s + 1)
                pe.wait_ge(xt_ev, at(xt_ev, s))
                transposes(bank[0], xn[h]).then_inc(xt_ps, 1)
                pe.wait_ge(ld_c[h], 16 * n)
                pe.wait_ge(ct_ev, at(ct_ev, s))
                transposes(bank[1], ctx_s[h][:, :].rearrange("p (a d) -> p a d", a=2)).then_inc(ct_ps, 1)

            def project(s, bk, w, src, done, free):
                pe.wait_ge(free, at(free, s))
                for n, (c0, t0) in enumerate(((0, 0), (SEG, P))):
                    for kd in range(KD):
                        last = pe.matmul(bank[bk][:, c0:c0 + SEG - t0], w[:, kd, n * P:(n + 1) * P],
                                         src[:, kd, t0:SEG], start=(kd == 0), stop=(kd == KD - 1))
                last.then_inc(done, 1)

            def projections(s, h):
                pe.wait_ge(xt_ev, at(xt_ev, s + 1))
                project(s, 2, wq_s, xT[h], q_ps, q_ev)
                project(s, 4, wg_s, xT[h], g_ps1, ge_ev)
                pe.wait_ge(ct_ev, at(ct_ev, s + 1))
                project(s, 3, wk_s, cT[h], k_ps, k_ev)
                pe.wait_ge(v_ev, at(v_ev, s))
                for a in range(2):
                    n = P if a == 0 else D
                    for kd in range(KD):
                        last = pe.matmul(bank[5][:, a * D:a * D + n], cT[h][:, kd, a * P:(a + 1) * P],
                                         wv_s[:, kd, 0:n], start=(kd == 0), stop=(kd == KD - 1))
                last.then_inc(v_ps, 1)

            input_tiles(0, 0, 1)
            pe.wait_ge(ld_w, 16 * WEIGHT_LOADS)
            with pe.Fori(0, NSEG // 2 - 1) as i:
                for h in range(2):
                    input_tiles(2 * i + (h + 1), 1 - h, i + (h + 1))
                    projections(2 * i + h, h)
            input_tiles(NSEG - 1, 1, NSEG // 2)
            projections(NSEG - 2, 0)
            projections(NSEG - 1, 1)

            def scores(g, h, hp, n):
                if hp == 0:
                    pe.wait_ge(ld_unit[h], 16 * 12 * n)
                for qb in range(2):
                    pe.wait_ge(p_rdy, at(p_rdy, 2 * g + (qb - 3)))
                    pe.matmul(bank[2 * (hp % 2) + qb][:, :], q_st[h][:, hp, qb * P:(qb + 1) * P],
                              k_st[h][:, hp, :], start=True, stop=True).then_inc(s_ps, 1)

            def transpose_probs(g, hp):
                pe.wait_ge(p_rdy, at(p_rdy, 2 * g + 2))
                for k in range(2):
                    pe.wait_ge(pt_ev[k], at(pt_ev[k], g))
                    for kb in range(2):
                        for qb in range(2):
                            last = pe.transpose(bank[4 + k][:, kb * SEG + qb * P:kb * SEG + (qb + 1) * P],
                                                prob[hp % 2][:, qb, k, kb * P:(kb + 1) * P], ident[:, :])
                    last.then_inc(t_ps, 1)

            def values(g, u, h, hp):
                if hp == 0:
                    pe.wait_ge(vp_rdy, u + 1)
                    pe.wait_ge(o_ev, at(o_ev, u - 1))
                for k in range(2):
                    pe.wait_ge(pt_ev[k], at(pt_ev[k], g + 1))
                    for kb in range(2):
                        last = pe.matmul(bank[6 + h][:, 0:SEG], vpad[h][:, kb, 2 * hp + k, :], pT[hp % 2][k][:, kb, :],
                                         start=(hp == 0 and k == 0 and kb == 0),
                                         stop=(hp == PAIRS - 1 and k == 1 and kb == 1))
                last.then_inc(pv_ps, 1)
                if hp == PAIRS - 1:
                    pe.wait_ge(rexp_rdy, u + 1)
                    for qb in range(2):
                        last = pe.transpose(bank[6 + h][:, SEG + qb * P:SEG + (qb + 1) * P],
                                            rexp[h][:, qb, :, :].rearrange("p g c -> p (g c)"), ident[:, :])
                    last.then_inc(rt_ps, 1)

            def attend(i, last_units=False):
                for c in range(2 * PAIRS):
                    g = 8 * i + c
                    if not (last_units and c + 1 >= 2 * PAIRS):
                        transpose_probs(g + 1, (c + 1) % PAIRS)
                    n = c + 3
                    if not (last_units and n >= 2 * PAIRS):
                        scores(g + 3, (n // PAIRS) % 2, n % PAIRS, i + n // (2 * PAIRS) + 1)
                    values(g, 2 * i + c // PAIRS, c // PAIRS, c % PAIRS)

            for evacuated in (q_ev, k_ev, v_ev, ge_ev):
                pe.wait_ge(evacuated, at(evacuated, NSEG))
            scores(0, 0, 0, 1)
            scores(1, 0, 1, 1)
            transpose_probs(0, 0)
            scores(2, 0, 2, 1)
            with pe.Fori(0, UNITS // 2 - 1) as i:
                attend(i)
            attend(UNITS // 2 - 1, True)

            def out_project(s, h):
                pe.wait_ge(x1_rdy, at(x1_rdy, s - 1))
                xo = view(bank[h], 2, D)
                even, odd, group1 = (attn[:, c:c + P] for c in (SEG * s, SEG * s + P, P * s + T))
                pe.matmul(xo[:, 0, :], even, wo_s[:, 0, :], start=True, stop=True)
                pe.matmul(xo[:, 1, :], odd, wo_s[:, 0, :], start=True, stop=False)
                pe.matmul(xo[:, 1, :], group1, wo_s[:, 1, :], start=False, stop=True).then_inc(xo_ps, 1)

            def transpose_tokens(s, h, next_one=True):
                if next_one:
                    out_project(s + 2, h)
                pe.wait_ge(xn2_rdy, s + 1)
                pe.wait_ge(x2h_rdy, at(x2h_rdy, s - 1))
                transposes(bank[2 + h], xn[h]).then_inc(t2_ps, 1)

            def logits_of(q):
                pe.wait_ge(x2l_rdy, at(x2l_rdy, 2 * q + 2))
                o = bank[5 + q % 3][0:E, :]
                for kd in range(KD):
                    hi, lo = (t[:, 2 * q:2 * q + 2, kd, :] for t in (x2h, x2l))
                    pe.matmul(o, gw_h[:, kd, :], hi, start=(kd == 0), stop=False)
                    pe.matmul(o, gw_h[:, kd, :], lo, start=False, stop=False)
                    last = pe.matmul(o, gw_l[:, kd, :], hi, start=False, stop=(kd == KD - 1))
                last.then_inc(lt_ps, 1)

            def last_logits(fb):
                if fb == 0:
                    pe.wait_ge(lt_ev, 1)
                    logits_of(GROUPS - 1)
                if fb == 2:
                    pe.wait_ge(lt_ev, GROUPS)
                    for t in range(NT):
                        last = pe.transpose(bank[7][:, t * E:(t + 1) * E], logits_t[:, t * P:(t + 1) * P],
                                            ident[0:E, 0:E])
                    last.then_inc(lg_ps, 1)

            pe.wait_ge(gated, UNITS)
            pe.wait_ge(gwl_rdy, 1)
            for h in range(2):
                out_project(h, h)
            for s in range(NSEG):
                transpose_tokens(s, s % 2, next_one=s + 2 < NSEG)
                if s >= 3 and s % 2 == 1:
                    logits_of((s - 3) // 2)

            def up(m, fb, high, low):
                sz = FSZ[fb]
                for n, (t, free, done) in enumerate(((0, sg_rdy, g_ps), (1, a_rdy, u_ps))):
                    pe.wait_ge(free, at(free, FB * m + (fb - 1)))
                    alone(pe)
                    o = bank[2 * n + fb % 2][0:sz, 0:SEG]
                    f0 = t * F + fb * P
                    for kd in range(KD):
                        pe.matmul(o, wh_gu[:, kd, f0:f0 + sz], high(kd), start=(kd == 0), stop=False)
                        pe.matmul(o, wh_gu[:, kd, f0:f0 + sz], low(kd), start=False, stop=False)
                        last = pe.matmul(o, wl_gu[:, kd, f0:f0 + sz], high(kd), start=False, stop=(kd == KD - 1))
                    last.then_inc(done, 1)

            def down(m, fb, h):
                sz = FSZ[fb]
                if fb == 0:
                    pe.wait_ge(y_rdy, at(y_rdy, m - 1))
                pe.wait_ge(ah_rdy, at(ah_rdy, FB * m + (fb + 1)))
                pe.wait_ge(al_rdy, at(al_rdy, FB * m + (fb + 1)))
                y = view(bank[4 + h], 2, D)
                for a in range(2):
                    t = slice(a * P, (a + 1) * P)
                    pe.matmul(y[:, a, :], act_h[0:sz, fb, t], wh_d[0:sz, fb, :], start=(fb == 0 and a == 0),
                              stop=False, skip_group_check=True)
                    pe.matmul(y[:, a, :], act_h[0:sz, fb, t], wl_d[0:sz, fb, :], start=False, stop=False,
                              skip_group_check=True)
                    last = pe.matmul(y[:, a, :], act_l[0:sz, fb, t], wh_d[0:sz, fb, :], start=False,
                                     stop=(fb == FB - 1 and a == 1), skip_group_check=True)
                last.then_inc(dn_ps, 1)

            def mlp(m, h, high, low, previous=True, each=None, job=None):
                for fb in range(FB):
                    if job is not None:
                        pe.wait_ge(wl_rdy, FB * job + (FB + fb + 1))
                    up(m, fb, high, low)
                    if fb >= 2:
                        if job is not None:
                            pe.wait_ge(wdl_rdy, FB * job + (FB + fb - 1))
                        down(m, fb - 2, h)
                    elif previous:
                        if job is not None and previous != "shared":
                            pe.wait_ge(wdl_rdy, FB * job + (fb + 5))
                        down(m - 1, fb + FB - 2, 1 - h)
                    if each:
                        each(fb)

            def shared(s, h, previous=True, each=None, job=None):
                def tokens(t):
                    return lambda kd: t[:, ds(s, 1), kd, :].rearrange("p u t -> p (u t)")

                pe.wait_ge(x2l_rdy, at(x2l_rdy, s + 1))
                mlp(s, h, tokens(x2h), tokens(x2l), previous, each, job)

            def count_tokens(fb):
                if fb == 2:
                    pe.wait_ge(m_in, 1)
                    mem = member[:, :, :].rearrange("p t e -> p (t e)")
                    pe.matmul(bank[7][:, 0:P], tri[:, :], mem, start=True, stop=True)
                    pe.matmul(bank[7][:, P:2 * P], ones[:, :], mem, start=True, stop=True).then_inc(pre_ps, 1)

            slots = bank[7][:, 0:2 * COLS]

            def place_tokens(s):
                def each(fb):
                    for c in range(HOT):
                        if HOT_FB[c] != fb - 1:
                            continue
                        pe.wait_ge(hot_rdy, HOT * s + (c + 1 - HOT0 * HOT))
                        pe.matmul(slots, hot[c % 4][:, :], val[c % 4][:, :, :].rearrange("p v c -> p (v c)"),
                                  start=False, stop=False, skip_group_check=True).then_inc(hot_ps, 1)
                return each

            def job_tokens(j, h, n):
                for a in range(2):
                    pe.wait_ge(gath[h][a], 16 * n)
                pe.wait_ge(xjl_rdy, at(xjl_rdy, j))
                transposes(bank[6], xg[h]).then_inc(tj_ps, 1)

            def expert_job(j, h, n_next=None, previous=True):
                def each(fb):
                    if fb == 3 and n_next is not None:
                        job_tokens(j + 1, 1 - h, n_next)

                pe.wait_ge(xjl_rdy, at(xjl_rdy, j + 1))
                mlp(j + NSEG, h, lambda kd: xjh[h][:, kd, :], lambda kd: xjl[h][:, kd, :], previous, each, j)

            pe.wait_ge(x1_rdy, at(x1_rdy, NSEG))
            pe.wait_ge(x2h_rdy, at(x2h_rdy, NSEG))
            shared(0, 0, previous=False, job=-1, each=last_logits)
            pe.wait_ge(wdl_rdy, FB)
            shared(1, 1, each=count_tokens)

            def clear_slots(fb):
                if fb == 0:
                    pe.wait_ge(pre_ev, 1)
                    pe.wait_ge(consts, 2)
                    pe.matmul(slots, ones[:, :], zero[:, :, :].rearrange("p a d -> p (a d)")[:, 0:2 * COLS],
                              start=True, stop=False, skip_group_check=True).then_inc(hot_ps, 1)

            shared(2, 0, each=clear_slots)
            with pe.Fori(0, (NSEG - 1 - HOT0) // 2) as i:
                for h in range(2):
                    shared(2 * i + (HOT0 + h), (HOT0 + h) % 2, each=place_tokens(2 * i + (HOT0 + h)))
            shared(NSEG - 1, 1, each=lambda fb: job_tokens(0, 0, 1) if fb == 3 else None)
            expert_job(0, 0, 1, previous="shared")
            with pe.Fori(0, JOBS // 2 - 1) as i:
                expert_job(2 * i + 1, 1, i + 2)
                expert_job(2 * i + 2, 0, i + 2)
            expert_job(JOBS - 2, 1, JOBS // 2 + 1)
            expert_job(JOBS - 1, 0)
            for fb in (FB - 2, FB - 1):
                pe.wait_ge(wdl_rdy, FB * JOBS + (fb + 1))
                down(NSEG + JOBS - 1, fb, 0)

        @block.vector
        def _(ve):
            chain = dict(n=0, i=0, per=0)

            def mark(ins):
                chain["n"] += 1
                ins.then_inc(dv, 1)

            def chained():
                ve.wait_ge(dv, chain["i"] * chain["per"] + chain["n"])

            def step(ins):
                mark(ins)
                chained()

            def loop_of(i, per):
                chain.update(i=i, per=per, at=chain["n"])

            def loop_end(count):
                assert chain["n"] - chain["at"] == chain["per"], (chain, "per")
                chain["n"] += chain["per"] * (count - 1)
                chain.update(i=0, per=0)


            def variance(src, h, done):
                alone(ve)
                for a in range(2):
                    mark(ve.bn_stats(stats[h][:, a, :], src[:, a, :]))
                chained()
                alone(ve)
                for a in range(2):
                    mark(ve.bn_aggr(mv[h][:, a, :], stats[h][:, a, :]))
                chained()
                ve.tensor_scalar(veps[h][:, :], mv[h][:, :, 1], LN_EPS, None, ALU.add).then_inc(done, 1)

            def normalise(src, h, done):
                for a in range(2):
                    last = ve.tensor_scalar(xn[h][:, a, :], src[:, a, :], mv[h][:, a, 0:1], rstd[h][:, a:a + 1],
                                            ALU.subtract, ALU.mult)
                last.then_inc(done, 1)

            def seg_rows(s):
                return x_all[:, ds(s, 1), :].rearrange("p u (a d) -> p (u a) d", a=2)

            def context_tile(s, h):
                ve.wait_ge(ct_ps, at(ct_ps, s + 1))
                ve.wait_ge(v_ps, at(v_ps, s - 1))
                ve.tensor_copy(cT[h][:, :, :], view(bank[1], KD, SEG)).then_inc(ct_ev, 1)

            def norm(s, h):
                ve.wait_ge(rstd_rdy, s + 1)
                ve.wait_ge(xt_ps, at(xt_ps, s - 1))
                normalise(seg_rows(s), h, xn_rdy)

            def keys(s, h):
                ve.wait_ge(k_ps, s + 1)
                ve.wait_ge(qkl_rdy, at(qkl_rdy, s - 1))
                ve.tensor_scalar(qk32[h][:, 1, 0:SEG], bank[3][:, 0:SEG], bias_s[:, 1, 0:1], None, ALU.add)
                ve.tensor_scalar(qk32[h][:, 1, SEG:SEG + P], bank[3][:, SEG:SEG + P], bias_s[:, 1, 1:2], None,
                                 ALU.add).then_inc(k_ev, 1)

            def values_of(s):
                ve.wait_ge(v_ps, at(v_ps, s + 1))
                pv = view(bank[5], 2, D)
                ve.tensor_tensor(v_all[:, ds(2 * s, 2), :], pv[:, :, 0:P],
                                 bv_b[:, 0:P].unsqueeze(1).to_broadcast([P, 2, P]), ALU.add)
                ve.tensor_tensor(v_all[:, ds(2 * NSEG + s, 1), :].rearrange("p u f -> p (u f)"), pv[:, 1, P:D],
                                 bv_b[:, P:D], ALU.add).then_inc(v_ev, 1)

            def project_steps(s, h, ahead=2):
                if ahead >= 1:
                    context_tile(s + 1, 1 - h)
                if ahead >= 2:
                    variance(seg_rows(s + 2), h, var_rdy)
                keys(s, h)
                if ahead >= 2:
                    norm(s + 2, h)
                values_of(s)

            for h in range(2):
                ve.wait_ge(ld_x[h], 16)
                variance(seg_rows(h), h, var_rdy)
            for h in range(2):
                norm(h, h)
            context_tile(0, 0)
            ve.wait_ge(ld_x2, 16)
            with ve.Fori(0, NSEG // 2 - 1) as i:
                loop_of(i, 8)
                ve.wait_ge(ld_x3, at(ld_x3, 16 * i))
                for h in range(2):
                    project_steps(2 * i + h, h)
            loop_end(NSEG // 2 - 1)
            project_steps(NSEG - 2, 0, ahead=1)
            project_steps(NSEG - 1, 1, ahead=0)

            def maxima(g, hp):
                for qb in range(2):
                    ve.wait_ge(s_ps, at(s_ps, 2 * g + (qb + 1)))
                    ve.tensor_reduce(nmax[hp % 2][:, qb, :], view(bank[2 * (hp % 2) + qb], 2, SEG), X, ALU.max,
                                     negate=True).then_inc(m_rdy, 1)

            def evacuate(g, hp):
                ve.wait_ge(t_ps, at(t_ps, 2 * g + 1))
                ve.wait_ge(pv_ps, at(pv_ps, g - 1))
                ve.tensor_copy(pT[hp % 2][0][:, :, :], view(bank[4], 2, SEG)).then_inc(pt_ev[0], 1)

            def attend(i, last_units=False):
                for c in range(2 * PAIRS):
                    g = 8 * i + c
                    h = c // PAIRS
                    u = 2 * i + h
                    if not (last_units and c + 1 >= 2 * PAIRS):
                        evacuate(g + 1, (c + 1) % PAIRS)
                    if not (last_units and c + 3 >= 2 * PAIRS):
                        maxima(g + 3, (c + 3) % PAIRS)
                    if c % PAIRS == PAIRS - 2:
                        ve.wait_ge(p_rdy, at(p_rdy, 2 * g + 4))
                        step(ve.reciprocal(rinv[h][:, :, :], rsum[h][:, :, :]))
                        ve.tensor_copy(rexp[h][:, :, :, :], rinv[h][:, :, :].unsqueeze(3).to_broadcast([P, 2, GH, HDIM]))\
                            .then_inc(rexp_rdy, 1)
                    if c in (PAIRS, 2 * PAIRS - 1):
                        h = c // (PAIRS + 1)
                        u = 2 * i + h
                        ve.wait_ge(rts_rdy, at(rts_rdy, u + 1))
                        ve.tensor_tensor(attn[:, ds(SEG * u, SEG)], bank[6 + h][:, 0:SEG], rts[h][:, :],
                                         ALU.mult).then_inc(o_ev, 1)
                        ve.wait_ge(o_ev, at(o_ev, u + 1))
                        ve.tensor_tensor(attn[:, ds(SEG * u, SEG)], attn[:, ds(SEG * u, SEG)], gT[:, ds(SEG * u, SEG)],
                                         ALU.mult).then_inc(gated, 1)

            ve.wait_ge(ge_ev, at(ge_ev, NSEG))
            maxima(0, 0)
            maxima(1, 1)
            evacuate(0, 0)
            maxima(2, 2)
            with ve.Fori(0, UNITS // 2 - 1) as i:
                loop_of(i, 2)
                attend(i)
            loop_end(UNITS // 2 - 1)
            attend(UNITS // 2 - 1, True)

            def high_up(m, r, fb):
                ve.tensor_copy(gu(wh_gu, fb), gu(raw_gu[r], fb)).then_inc(wh_rdy, 1)

            def low_up(m, r, fb):
                ve.wait_ge(wh_rdy, FB * m + (fb + 1))
                ve.tensor_tensor(gu(wl_gu, fb), gu(raw_gu[r], fb), gu(wh_gu, fb).bitcast(F32),
                                 ALU.subtract).then_inc(wl_rdy, 1)

            ve.wait_ge(o_ev, at(o_ev, UNITS))

            def residual1(s, h):
                ve.wait_ge(xo_ps, at(xo_ps, s + 1))
                ve.tensor_tensor(seg_rows(s), seg_rows(s), view(bank[h], 2, D), ALU.add).then_inc(x1_rdy, 1)
                ve.wait_ge(x1_rdy, at(x1_rdy, s + 1))
                variance(seg_rows(s), h, var2)

            def norm2(s, h, n):
                ve.wait_ge(rstd2, s + 1)
                ve.wait_ge(t2_ps, at(t2_ps, s - 1))
                ve.wait_ge(xn2_st[h], at(xn2_st[h], 16 * n))
                normalise(seg_rows(s), h, xn2_rdy)

            ve.wait_ge(xbo_rdy, 1)
            residual1(0, 0)
            with ve.Fori(0, NSEG // 2 - 1) as i:
                loop_of(i, 8)
                for h in range(2):
                    residual1(2 * i + (h + 1), 1 - h)
                    norm2(2 * i + h, h, i)
            loop_end(NSEG // 2 - 1)
            residual1(NSEG - 1, 1)
            norm2(NSEG - 2, 0, NSEG // 2 - 1)
            norm2(NSEG - 1, 1, NSEG // 2 - 1)

            SCANS = (NT - 1).bit_length()
            by_e = desc[:, :].unsqueeze(1).to_broadcast([P, NT, E])

            def over_e(t):
                return t.unsqueeze(2).to_broadcast([P, NT, E])

            def top_max(c, src):
                step(ve.tensor_reduce(m1[:, c, :], src, X, ALU.max))
                step(ve.tensor_tensor(eq[:, :, :], src, over_e(m1[:, c, :]), ALU.is_equal))

            def top_expert(c):
                step(ve.tensor_tensor(eq[:, :, :], eq[:, :, :], by_e, ALU.mult))
                step(ve.tensor_reduce(fi[:, :], eq[:, :, :], X, ALU.max))
                step(ve.tensor_tensor(sel[:, c, :, :], by_e, over_e(fi[:, :]), ALU.is_equal))

            def route_top():
                ve.wait_ge(lg_ps, 1)
                step(ve.tensor_copy(logits[:, :, :], view(bank[7], 2 * NSEG, E)))
                ve.wait_ge(consts, 2)
                top_max(0, logits[:, :, :])

            def route_second_logits():
                top_expert(0)
                step(ve.scalar_tensor_tensor(out=l2[:, :, :], in0=sel[:, 0, :, :], scalar=-BIG, in1=logits[:, :, :],
                                             op0=ALU.mult, op1=ALU.add))

            def route_second():
                top_expert(1)
                ve.tensor_tensor(wexp[:, 0, :], m1[:, 1, :], m1[:, 0, :], ALU.subtract).then_inc(dif_rdy, 1)
                ve.tensor_tensor(member[:, :, :], sel[:, 0, :, :], sel[:, 1, :, :], ALU.add).then_inc(m_in, 1)

            def route_weights():
                ve.wait_ge(ex_rdy, 1)
                step(ve.tensor_scalar(wexp[:, 2, :], wexp[:, 1, :], 1.0, None, ALU.add))
                step(ve.reciprocal(wts[:, 0, :], wexp[:, 2, :]))
                step(ve.tensor_tensor(wts[:, 1, :], wts[:, 0, :], wexp[:, 1, :], ALU.mult))

            def route_counts():
                ve.wait_ge(pre_ps, 1)
                mark(ve.tensor_copy(scan[0][:, :, :], view(bank[7], 2, NT, E)[:, 1, :, :]))
                step(ve.tensor_copy(pos[:, :, :], view(bank[7], 2, NT, E)[:, 0, :, :]))
                ve.sem_inc(pre_ev, 1)
                step(ve.tensor_tensor(pos[:, :, :], pos[:, :, :], scan[0][:, :, :], ALU.subtract))

            def route_scan(first, last):
                for n in range(first, last + 1):
                    r, d = n % 2, 2 ** n
                    mark(ve.tensor_copy(scan[1 - r][:, 0:d, :], scan[r][:, 0:d, :]))
                    step(ve.tensor_tensor(scan[1 - r][:, d:NT, :], scan[r][:, d:NT, :], scan[r][:, 0:NT - d, :], ALU.add))
                if last < SCANS - 1:
                    return
                r = SCANS % 2
                step(ve.tensor_tensor(pos[:, :, :], pos[:, :, :], scan[r][:, :, :], ALU.add))

            def route_jobs():
                step(ve.tensor_tensor(ntile[:, :, :], scan[SCANS % 2][:, NT - 1, :].unsqueeze(2).to_broadcast([P, E, T // SEG]),
                                      k256[:, :].unsqueeze(1).to_broadcast([P, E, T // SEG]), ALU.is_gt))
                step(ve.tensor_reduce(tiles[:, :], ntile[:, :, :], X, ALU.add))
                step(ve.tensor_copy(tend[0][:, :], tiles[:, :]))
                r, d = 0, 1
                while d < E:
                    mark(ve.tensor_copy(tend[1 - r][:, 0:d], tend[r][:, 0:d]))
                    step(ve.tensor_tensor(tend[1 - r][:, d:E], tend[r][:, d:E], tend[r][:, 0:E - d], ALU.add))
                    r, d = 1 - r, 2 * d

            def route_job_experts():
                r = (E - 1).bit_length() % 2
                step(ve.tensor_tensor(jobe[:, :, :], tend[r][0:1, :].unsqueeze(1).to_broadcast([1, JOBS + 1, E]),
                                      jcol[:, :].unsqueeze(2).to_broadcast([1, JOBS + 1, E]), ALU.is_le))
                step(ve.tensor_reduce(jobf[:, :], jobe[:, :, :], X, ALU.add))
                step(ve.tensor_scalar(jobf[:, :], jobf[:, :], float(E - 1), None, ALU.min))
                ve.tensor_copy(jobi[:, :], jobf[:, :]).then_inc(jobs_rdy, 1)

            def route_places():
                r = (E - 1).bit_length() % 2
                step(ve.tensor_tensor(tend[1 - r][:, :], tend[r][:, :], tiles[:, :], ALU.subtract))
                step(ve.tensor_scalar(tend[1 - r][:, :], tend[1 - r][:, :], float(SEG), None, ALU.mult))
                step(ve.tensor_tensor(pos[:, :, :], pos[:, :, :], tend[1 - r][:, :].unsqueeze(1).to_broadcast([P, NT, E]),
                                      ALU.add))

            def route_slots():
                for c in range(TOPK):
                    step(ve.tensor_tensor(eq[:, :, :], sel[:, c, :, :], pos[:, :, :], ALU.mult))
                    step(ve.tensor_reduce(poss[:, c, :], eq[:, :, :], X, ALU.add))

            def route_rows():
                step(ve.tensor_copy(posi[:, 0, :, :], poss[:, :, :]))
                mark(ve.tensor_scalar(posi[:, 1, :, :], posi[:, 0, :, :], P - 1, None, ALU.bitwise_and))
                step(ve.tensor_scalar(posi[:, 2, :, :], posi[:, 0, :, :], P.bit_length() - 1, None, ALU.logical_shift_right))
                step(ve.tensor_copy(posf[:, :, :, :], posi[:, 1:3, :, :]))

            row_of, col_of = [posf[:, n, :, :].rearrange("p c t -> p (c t)") for n in range(2)]
            tok_of = rowid[:, :, :].rearrange("p c t -> p (c t)")
            wt_of = wts[:, :, :].rearrange("p c t -> p (c t)")

            def one_hot(s, c):
                k = ds(HOT * s + (c - HOT0 * HOT), 1)
                ve.wait_ge(hot_ps, at(hot_ps, HOT * s + (c - HOT0 * HOT - 2)))
                ve.tensor_scalar(hot[c % 4][:, :], iota[:, :], row_of[:, k], None, ALU.is_equal)
                ve.tensor_scalar(val[c % 4][:, 0, :], iota[:, 0:COLS], col_of[:, k], tok_of[:, k],
                                 ALU.is_equal, ALU.mult)
                ve.tensor_scalar(val[c % 4][:, 1, :], iota[:, 0:COLS], col_of[:, k], wt_of[:, k],
                                 ALU.is_equal, ALU.mult).then_inc(hot_rdy, 1)

            def gate(m, fb):
                sz = FSZ[fb]
                ve.wait_ge(sg_rdy, at(sg_rdy, FB * m + (fb + 1)))
                ve.wait_ge(u_ps, FB * m + (fb + 1))
                ve.wait_ge(ah_rdy, at(ah_rdy, FB * m + (fb - 1)))
                ve.wait_ge(al_rdy, at(al_rdy, FB * m + (fb - 1)))
                ve.tensor_tensor(act[fb % 2][0:sz, :], sg[fb % 2][0:sz, :], bank[2 + fb % 2][0:sz, 0:SEG],
                                 ALU.mult).then_inc(a_rdy, 1)

            def act_low(m, fb):
                sz = FSZ[fb]
                ve.wait_ge(ah_rdy, at(ah_rdy, FB * m + (fb + 1)))
                ve.tensor_tensor(act_l[0:sz, fb, :], act[fb % 2][0:sz, :], act_h[0:sz, fb, :].bitcast(F32),
                                 ALU.subtract).then_inc(al_rdy, 1)

            def slot_table():
                ve.wait_ge(hot_ps, at(hot_ps, TOPK * NT + 1))
                step(ve.tensor_copy(tokf[:, 0:2, :], view(bank[7], 2, COLS)))
                step(ve.scalar_tensor_tensor(out=tokf[:, 2, :], in0=tokf[:, 0, :], scalar=0.0,
                                             in1=spare[:, :, :].rearrange("p j a -> p (j a)"),
                                             op0=ALU.is_equal, op1=ALU.mult))
                step(ve.tensor_tensor(tokf[:, 2, :], tokf[:, 2, :], tokf[:, 0, :], ALU.add))
                step(ve.tensor_scalar(tokf[:, 2, :], tokf[:, 2, :], -1.0, None, ALU.add))
                ve.tensor_copy(toki[:, :], tokf[:, 2, :]).then_inc(slots_rdy, 1)

            def residual(s, h, n):
                ve.wait_ge(dn_ps, at(dn_ps, FB * s + FB))
                ve.wait_ge(out_st[h], at(out_st[h], 16 * n - 16))
                ve.tensor_tensor(y_s[h][:, :, :], seg_rows(s), view(bank[4 + h], 2, D), ALU.add).then_inc(y_rdy, 1)

            def token_low(j, h):
                ve.wait_ge(xjh_rdy, j + 1)
                ve.tensor_tensor(xjl[h][:, :, :], view(bank[6], KD, SEG), xjh[h][:, :, :].bitcast(F32),
                                 ALU.subtract).then_inc(xjl_rdy, 1)

            def mlp(m, each=lambda fb: None, job=None, h=None, n_next=None):
                for fb in range(FB):
                    gate(m, fb)
                    if fb:
                        act_low(m, fb - 1)
                    if n_next is not None:
                        if fb == 0:
                            ve.wait_ge(ld_gu[1 - h], raw_loads(1 - h, n_next))
                        high_up(job + 2, 1 - h, fb)
                        if fb:
                            low_up(job + 2, 1 - h, fb - 1)
                        if fb == 3:
                            token_low(job + 1, 1 - h)
                    each(fb)
                act_low(m, FB - 1)
                if n_next is not None:
                    low_up(job + 2, 1 - h, FB - 1)

            def hot_and_residual(s, h, n):
                def each(fb):
                    if fb == 2:
                        residual(s - 1, 1 - h, n)
                    for c in range(HOT):
                        if HOT_FB[c] == fb:
                            one_hot(s, c)
                return each

            mlp(0, each=lambda fb: {3: route_top, 4: route_second_logits, 5: lambda: top_max(1, l2[:, :, :])}.get(fb, lambda: None)())
            mlp(1, each=lambda fb: (route_second, route_weights, lambda: residual(0, 0, 1), route_counts,
                                    lambda: route_scan(0, 1), lambda: route_scan(2, SCANS - 1))[fb]())
            mlp(2, each=lambda fb: (route_jobs, route_job_experts, lambda: residual(1, 1, 1), route_places,
                                    route_slots, route_rows)[fb]())
            with ve.Fori(0, 2) as i:
                mlp(2 * i + 3, each=hot_and_residual(2 * i + 3, 1, i + 2))
                mlp(2 * i + 4, each=hot_and_residual(2 * i + 4, 0, i + 2))
            mlp(NSEG - 1, each=lambda fb: {0: slot_table, 2: lambda: residual(NSEG - 2, 0, NSEG // 2)}
                .get(fb, lambda: None)(), job=-1, h=1, n_next=1)
            mlp(NSEG, each=lambda fb: residual(NSEG - 1, 1, NSEG // 2) if fb == 2 else None, job=0, h=0, n_next=1)
            with ve.Fori(0, JOBS // 2 - 1) as i:
                mlp(2 * i + (NSEG + 1), job=2 * i + 1, h=1, n_next=i + 2)
                mlp(2 * i + (NSEG + 2), job=2 * i + 2, h=0, n_next=i + 2)
            mlp(NSEG + JOBS - 2, job=JOBS - 2, h=1, n_next=JOBS // 2 + 1)
            mlp(NSEG + JOBS - 1)


_INS = ["x", "ctx_1024"] + [f"L0_xattn_{w}{g}" for g in "qkvgo" for w in ("W", "b")] + \
       ["L0_ffn_gate_w", "L0_ffn_base_wgu", "L0_ffn_base_wd", "L0_ffn_exp_wgu", "L0_ffn_exp_wd"]


def kernel(**inputs):
    import numpy as np
    import concourse.bacc as bacc
    from concourse.bass_utils import run_bass_kernel_spmd

    nc = bacc.Bacc("TRN2", target_bir_lowering=False, num_devices=1)
    arrays, args = {}, []
    for name in _INS:
        a = np.ascontiguousarray(inputs[name])
        arrays[name] = a
        args.append(nc.dram_tensor(name, a.shape, mybir.dt.from_np(a.dtype), kind="ExternalInput").ap())
    args.append(nc.dram_tensor("out", (ROWS, D), F32, kind="ExternalOutput").ap())
    build(nc, *args)
    r = run_bass_kernel_spmd(nc, [arrays], core_ids=[0])
    return r.results[0]["out"][0:T].reshape(BATCH, NTOK, D)
```
